# Optimizing a Trainium2 kernel written in Bass

```python
import numpy as np
import jax
import jax.numpy as jnp

def _softmax(x, axis=-1):
    return jax.nn.softmax(x, axis=axis)

def _gelu(x):
    return jax.nn.gelu(x, approximate=True)

def _silu(x):
    return jax.nn.silu(x)

def _sigmoid(x):
    return jax.nn.sigmoid(x)

def _layernorm(x, axis=-1, eps=1e-05):
    m = jnp.mean(x, axis=axis, keepdims=True)
    v = jnp.var(x, axis=axis, keepdims=True)
    return (x - m) / jnp.sqrt(v + eps)

def _scatter_add(tgt, idx, src, axis=0):
    return tgt.at[idx].add(src)

def _segment_sum(src, seg, n):
    return jax.ops.segment_sum(src, seg, n)
kernel_name = 'mk_perceiver_d1_seqx_r4_cb2d18'

def setup_inputs(seed: int=0):
    np.random.seed(seed)
    _w = jnp.asarray

    def _rec_inputs():
        import jax
        import jax.numpy as jnp
        _rk = jax.random.key(seed)
        x = -1.394e-06 + 0.9999 * jax.random.normal(jax.random.fold_in(_rk, 1), (32, 64, 256), jnp.float32)
        _lenS = 64 - jax.random.randint(jax.random.fold_in(_rk, 7), (32,), 0, max(1, 64 // 4) + 1, jnp.int32)
        _lenS2 = 1601 - jax.random.randint(jax.random.fold_in(_rk, 8), (32,), 0, max(1, 1601 // 4) + 1, jnp.int32)
        _ctx_1024P = jax.random.normal(jax.random.fold_in(_rk, 11), (32, 16, 256), jnp.float32)
        _ctx_1024c = jax.random.dirichlet(jax.random.fold_in(_rk, 511), 0.3 * jnp.ones((16,), jnp.float32), (32, 1601))
        _ctx_1024t = jnp.einsum('bsk,bkd->bsd', _ctx_1024c, _ctx_1024P)
        _ctx_1024t = _ctx_1024t * jax.lax.rsqrt(jnp.mean(jnp.square(_ctx_1024t)) + 1e-12) * 0.953939
        ctx_1024 = -0.000392918 + 0.999932 * (_ctx_1024t + 0.3 * jax.random.normal(jax.random.fold_in(_rk, 611), (32, 1601, 256), jnp.float32))
        _validS = jnp.arange(64)[None, :] < _lenS[:, None]
        _validS2 = jnp.arange(1601)[None, :] < _lenS2[:, None]
        _causal = jnp.tril(jnp.ones((64, 64), dtype=bool))
        mask_BxS2_bk0 = jnp.logical_not(jnp.broadcast_to(_validS2[:, :], (32, 1601)))
        return (x, ctx_1024, mask_BxS2_bk0)
    x, ctx_1024, mask_BxS2_bk0 = _rec_inputs()

    def _L0_xattn_setup():
        import jax, jax.numpy as jnp
        import numpy as np
        DIM = 256
        DIM_LATENT = 256
        DIM_HEAD = 64
        INNER = max(DIM, DIM_LATENT)
        HEADS = INNER // DIM_HEAD
        SCALE = DIM_HEAD ** (-0.5)
        LN_EPS = 1e-05
        RMS_EPS = 1e-08

        def layernorm(x, g, b):
            mu = jnp.mean(x, axis=-1, keepdims=True)
            var = jnp.mean(jnp.square(x - mu), axis=-1, keepdims=True)
            return (x - mu) * jax.lax.rsqrt(var + LN_EPS) * g + b

        def rmsnorm(x, gamma):
            n = jnp.linalg.norm(x, axis=-1, keepdims=True) * x.shape[-1] ** (-0.5)
            return x / jnp.maximum(n, RMS_EPS) * gamma
        key = jax.random.key(seed)
        ks = jax.random.split(key, 8)
        b, n, nl = (8, 512, 128)
        x = jax.random.normal(ks[0], (b, n, DIM), dtype=jnp.float32)
        latents = jax.random.normal(ks[1], (b, nl, DIM_LATENT), dtype=jnp.float32)
        mask = jax.random.randint(ks[2], (b, n), 0, 2).astype(bool)
        init = lambda k, shape, fan_in: jax.random.normal(k, shape, jnp.float32) * fan_in ** (-0.5)
        return {'x': x, 'latents': latents, 'mask': mask, 'ln_x_g': jnp.ones((DIM,), jnp.float32), 'ln_x_b': jnp.zeros((DIM,), jnp.float32), 'ln_l_g': jnp.ones((DIM_LATENT,), jnp.float32), 'ln_l_b': jnp.zeros((DIM_LATENT,), jnp.float32), 'q_gamma': jnp.ones((DIM_HEAD,), jnp.float32), 'k_gamma': jnp.ones((DIM_HEAD,), jnp.float32), 'W_q': init(ks[3], (DIM_LATENT, INNER), DIM_LATENT), 'W_kv': init(ks[4], (DIM, 2 * INNER), DIM), 'W_out': init(ks[5], (INNER, DIM_LATENT), INNER), 'b_out': jnp.zeros((DIM_LATENT,), jnp.float32)}
    _L0_xattn_all = _L0_xattn_setup()
    _L0_xattn_in = {k: v for k, v in _L0_xattn_all.items() if k in ('ln_x_g', 'ln_x_b', 'ln_l_g', 'ln_l_b', 'q_gamma', 'k_gamma', 'W_q', 'W_kv', 'W_out', 'b_out')}
    del _L0_xattn_all

    def _L0_attn_setup():
        import jax, jax.numpy as jnp
        import numpy as np
        import math
        NUM_BUCKETS = 32
        MAX_DISTANCE = 128
        N_HEAD = 16
        HEAD_DIM = 64
        HIDDEN = 256

        def _rel_buckets(S):
            half = NUM_BUCKETS // 2
            max_exact = half // 2
            coeff = (half - max_exact) / math.log(MAX_DISTANCE / max_exact)
            pos = jnp.arange(S, dtype=jnp.int32)
            rel = pos[None, :] - pos[:, None]
            arel = jnp.abs(rel)
            base = jnp.where(rel > 0, half, 0)
            distant = max_exact + (jnp.log(jnp.maximum(arel, 1).astype(jnp.float32) / max_exact) * coeff).astype(jnp.int32)
            distant = jnp.minimum(distant, half - 1)
            return base + jnp.where(arel < max_exact, arel, distant)
        key = jax.random.key(seed)
        k1, k2, k3, k4 = jax.random.split(key, 4)
        B, S = (2, 512)
        std = 1.0 / math.sqrt(HIDDEN)
        x = jax.random.normal(k1, (B, S, HIDDEN), dtype=jnp.float32)
        emb_weight = jax.random.normal(k2, (NUM_BUCKETS, N_HEAD), dtype=jnp.float32) * 0.5
        qkv_w = jax.random.normal(k3, (3 * N_HEAD * HEAD_DIM, HIDDEN), dtype=jnp.float32) * std
        o_w = jax.random.normal(k4, (HIDDEN, N_HEAD * HEAD_DIM), dtype=jnp.float32) * std
        return {'x': x, 'emb_weight': emb_weight, 'qkv_w': qkv_w, 'o_w': o_w}
    _L0_attn_all = _L0_attn_setup()
    _L0_attn_in = {k: v for k, v in _L0_attn_all.items() if k in ('emb_weight', 'qkv_w', 'o_w')}
    del _L0_attn_all

    def _L0_ffn_setup():
        import jax, jax.numpy as jnp
        import numpy as np
        D_IN, D_HID = (256, 1024)

        def _ternary(key, shape):
            return jax.random.randint(key, shape, -1, 2).astype(jnp.float32)

        def _tlin(x, w, s):
            return jnp.einsum('bsi,oi->bso', x, w) * s
        key = jax.random.key(seed)
        ks = jax.random.split(key, 12)
        inv = lambda fan: 1.0 / np.sqrt(fan).astype(np.float32)
        return {'x': jax.random.normal(ks[0], (4, 512, D_IN), dtype=jnp.float32), 'w1_w': _ternary(ks[1], (D_HID, D_IN)), 'w1_s': jax.random.uniform(ks[2], (D_HID,), dtype=jnp.float32) * inv(D_IN), 'w2_w': _ternary(ks[3], (D_HID, D_IN)), 'w2_s': jax.random.uniform(ks[4], (D_HID,), dtype=jnp.float32) * inv(D_IN), 'h1_w': _ternary(ks[5], (D_HID, D_HID)), 'h1_s': jax.random.uniform(ks[6], (D_HID,), dtype=jnp.float32) * inv(D_HID), 'h2_w': _ternary(ks[7], (D_HID, D_HID)), 'h2_s': jax.random.uniform(ks[8], (D_HID,), dtype=jnp.float32) * inv(D_HID), 'w3_w': _ternary(ks[9], (D_IN, D_HID)), 'w3_s': jax.random.uniform(ks[10], (D_IN,), dtype=jnp.float32) * inv(D_HID)}
    _L0_ffn_all = _L0_ffn_setup()
    _L0_ffn_in = {k: v for k, v in _L0_ffn_all.items() if k in ('w1_w', 'w1_s', 'w2_w', 'w2_s', 'h1_w', 'h1_s', 'h2_w', 'h2_s', 'w3_w', 'w3_s')}
    del _L0_ffn_all
    return {'x': x, 'ctx_1024': ctx_1024, 'mask_BxS2_bk0': mask_BxS2_bk0, 'L0_xattn_ln_x_g': _L0_xattn_in['ln_x_g'], 'L0_xattn_ln_x_b': _L0_xattn_in['ln_x_b'], 'L0_xattn_ln_l_g': _L0_xattn_in['ln_l_g'], 'L0_xattn_ln_l_b': _L0_xattn_in['ln_l_b'], 'L0_xattn_q_gamma': _L0_xattn_in['q_gamma'], 'L0_xattn_k_gamma': _L0_xattn_in['k_gamma'], 'L0_xattn_W_q': _L0_xattn_in['W_q'], 'L0_xattn_W_kv': _L0_xattn_in['W_kv'], 'L0_xattn_W_out': _L0_xattn_in['W_out'], 'L0_xattn_b_out': _L0_xattn_in['b_out'], 'L0_attn_emb_weight': _L0_attn_in['emb_weight'], 'L0_attn_qkv_w': _L0_attn_in['qkv_w'], 'L0_attn_o_w': _L0_attn_in['o_w'], 'L0_ffn_w1_w': _L0_ffn_in['w1_w'], 'L0_ffn_w1_s': _L0_ffn_in['w1_s'], 'L0_ffn_w2_w': _L0_ffn_in['w2_w'], 'L0_ffn_w2_s': _L0_ffn_in['w2_s'], 'L0_ffn_h1_w': _L0_ffn_in['h1_w'], 'L0_ffn_h1_s': _L0_ffn_in['h1_s'], 'L0_ffn_h2_w': _L0_ffn_in['h2_w'], 'L0_ffn_h2_s': _L0_ffn_in['h2_s'], 'L0_ffn_w3_w': _L0_ffn_in['w3_w'], 'L0_ffn_w3_s': _L0_ffn_in['w3_s']}

def reference(x, ctx_1024, mask_BxS2_bk0, L0_xattn_ln_x_g, L0_xattn_ln_x_b, L0_xattn_ln_l_g, L0_xattn_ln_l_b, L0_xattn_q_gamma, L0_xattn_k_gamma, L0_xattn_W_q, L0_xattn_W_kv, L0_xattn_W_out, L0_xattn_b_out, L0_attn_emb_weight, L0_attn_qkv_w, L0_attn_o_w, L0_ffn_w1_w, L0_ffn_w1_s, L0_ffn_w2_w, L0_ffn_w2_s, L0_ffn_h1_w, L0_ffn_h1_s, L0_ffn_h2_w, L0_ffn_h2_s, L0_ffn_w3_w, L0_ffn_w3_s):
    import jax
    import jax.numpy as jnp

    def _L0_xattn_ref(x, latents, mask, ln_x_g, ln_x_b, ln_l_g, ln_l_b, q_gamma, k_gamma, W_q, W_kv, W_out, b_out):
        import jax, jax.numpy as jnp
        import numpy as np
        DIM = 256
        DIM_LATENT = 256
        DIM_HEAD = 64
        INNER = max(DIM, DIM_LATENT)
        HEADS = INNER // DIM_HEAD
        SCALE = DIM_HEAD ** (-0.5)
        LN_EPS = 1e-05
        RMS_EPS = 1e-08

        def layernorm(x, g, b):
            mu = jnp.mean(x, axis=-1, keepdims=True)
            var = jnp.mean(jnp.square(x - mu), axis=-1, keepdims=True)
            return (x - mu) * jax.lax.rsqrt(var + LN_EPS) * g + b

        def rmsnorm(x, gamma):
            n = jnp.linalg.norm(x, axis=-1, keepdims=True) * x.shape[-1] ** (-0.5)
            return x / jnp.maximum(n, RMS_EPS) * gamma
        b, n, _ = x.shape
        nl = latents.shape[1]
        xn = layernorm(x, ln_x_g, ln_x_b)
        ln = layernorm(latents, ln_l_g, ln_l_b)
        q = ln @ W_q
        kv = jnp.concatenate([xn @ W_kv, ln @ W_kv], axis=1)
        k, v = (kv[..., :INNER], kv[..., INNER:])
        to_heads = lambda t: t.reshape(t.shape[0], t.shape[1], HEADS, DIM_HEAD).transpose(0, 2, 1, 3)
        q, k, v = (to_heads(q), to_heads(k), to_heads(v))
        qn = rmsnorm(q, q_gamma) * SCALE
        kn = rmsnorm(k, k_gamma)
        sim = jnp.einsum('bhid,bhjd->bhij', qn, kn)
        full_mask = jnp.pad(mask, ((0, 0), (0, nl)), constant_values=True)
        neg = -jnp.finfo(sim.dtype).max
        sim = jnp.where(full_mask[:, None, None, :], sim, neg)
        attn = jax.nn.softmax(sim.astype(jnp.float32), axis=-1).astype(sim.dtype)
        out = jnp.einsum('bhij,bhjd->bhid', attn, v)
        out = out.transpose(0, 2, 1, 3).reshape(b, nl, INNER)
        return out @ W_out + b_out

    def _L0_attn_ref(x, emb_weight, qkv_w, o_w):
        import jax, jax.numpy as jnp
        import numpy as np
        import math
        NUM_BUCKETS = 32
        MAX_DISTANCE = 128
        N_HEAD = 16
        HEAD_DIM = 64
        HIDDEN = 256

        def _rel_buckets(S):
            half = NUM_BUCKETS // 2
            max_exact = half // 2
            coeff = (half - max_exact) / math.log(MAX_DISTANCE / max_exact)
            pos = jnp.arange(S, dtype=jnp.int32)
            rel = pos[None, :] - pos[:, None]
            arel = jnp.abs(rel)
            base = jnp.where(rel > 0, half, 0)
            distant = max_exact + (jnp.log(jnp.maximum(arel, 1).astype(jnp.float32) / max_exact) * coeff).astype(jnp.int32)
            distant = jnp.minimum(distant, half - 1)
            return base + jnp.where(arel < max_exact, arel, distant)
        B, S, D = x.shape
        qkv = x @ qkv_w.T
        qkv = qkv.reshape(B, S, 3, N_HEAD, HEAD_DIM)
        q = qkv[:, :, 0].transpose(0, 2, 1, 3)
        k = qkv[:, :, 1].transpose(0, 2, 1, 3)
        v = qkv[:, :, 2].transpose(0, 2, 1, 3)
        bias = emb_weight[_rel_buckets(S)]
        bias = bias.transpose(2, 0, 1)[None]
        scale = HEAD_DIM ** (-0.5)
        scores = jnp.einsum('bhqd,bhkd->bhqk', q, k) * scale + bias
        attn = jax.nn.softmax(scores, axis=-1)
        a = jnp.einsum('bhqk,bhkd->bhqd', attn, v)
        a = a.transpose(0, 2, 1, 3).reshape(B, S, N_HEAD * HEAD_DIM)
        return a @ o_w.T

    def _L0_ffn_ref(x, w1_w, w1_s, w2_w, w2_s, h1_w, h1_s, h2_w, h2_s, w3_w, w3_s):
        import jax, jax.numpy as jnp
        import numpy as np
        D_IN, D_HID = (256, 1024)

        def _ternary(key, shape):
            return jax.random.randint(key, shape, -1, 2).astype(jnp.float32)

        def _tlin(x, w, s):
            return jnp.einsum('bsi,oi->bso', x, w) * s
        h = jax.nn.silu(_tlin(x, w1_w, w1_s)) * _tlin(x, w2_w, w2_s)
        h = jax.nn.gelu(_tlin(h, h1_w, h1_s), approximate=False)
        h = jax.nn.gelu(_tlin(h, h2_w, h2_s), approximate=False)
        return _tlin(h, w3_w, w3_s)
    x = x + _L0_xattn_ref(ctx_1024, _layernorm(x, axis=-1), mask_BxS2_bk0, L0_xattn_ln_x_g, L0_xattn_ln_x_b, L0_xattn_ln_l_g, L0_xattn_ln_l_b, L0_xattn_q_gamma, L0_xattn_k_gamma, L0_xattn_W_q, L0_xattn_W_kv, L0_xattn_W_out, L0_xattn_b_out)
    x = x + _L0_attn_ref(_layernorm(x, axis=-1), L0_attn_emb_weight, L0_attn_qkv_w, L0_attn_o_w)
    x = x + _L0_ffn_ref(_layernorm(x, axis=-1), L0_ffn_w1_w, L0_ffn_w1_s, L0_ffn_w2_w, L0_ffn_w2_s, L0_ffn_h1_w, L0_ffn_h1_s, L0_ffn_h2_w, L0_ffn_h2_s, L0_ffn_w3_w, L0_ffn_w3_s)
    return x

_drawn_inputs = setup_inputs


def setup_inputs(seed=0):
    import zlib

    import numpy as np

    out = dict(_drawn_inputs(seed))
    spreads = {'L0_xattn_ln_x_g': (1.0, 0.2),
     'L0_xattn_ln_x_b': (0.0, 0.1),
     'L0_xattn_ln_l_g': (1.0, 0.2),
     'L0_xattn_ln_l_b': (0.0, 0.1),
     'L0_xattn_q_gamma': (1.0, 0.2),
     'L0_xattn_k_gamma': (1.0, 0.2),
     'L0_xattn_b_out': (0.0, 0.1)}
    factors = {}
    for name, (base, spread) in spreads.items():
        noise = np.random.default_rng([zlib.crc32(name.encode()), seed]).standard_normal(out[name].shape)
        drawn = base * np.exp(spread * noise) if base else spread * noise
        out[name] = jnp.asarray(drawn.astype(out[name].dtype))
    for name, factor in factors.items():
        out[name] = (out[name] * factor).astype(out[name].dtype)
    return out
```

```python
from collections import namedtuple
from contextlib import ExitStack

import numpy as np

import concourse.bass as bass
from concourse import mybir

F32 = mybir.dt.float32
BF16 = mybir.dt.bfloat16
I32 = mybir.dt.int32
U8 = mybir.dt.uint8
ALU = mybir.AluOpType
ACT = mybir.ActivationFunctionType
AX = mybir.AxisListType
ds = bass.ds

P = 128
B, S, D = 32, 64, 256
SC = 1601
FC = D // P
ROWS = B * S
RT = ROWS // P
XH, DH = 4, 64
HP = XH // 2
KT = -(-SC // P)
FRONT = KT * P - SC
NT = B * KT
EC = 4
ER = NT // EC
G = 4
GT = G * P
LW = NT + 4 * G
AH = 16
AP_ = AH // 2
HID = 1024
HC = HID // P
BLK = 512
NB = ROWS // BLK
BR = BLK // P
NBUCK = 32
PIECE = 1024
NPIECE = 2 * FC + 2 * HC + HC * D // PIECE
LN_EPS = 1e-5
RMS_FLOOR = 1e-8 ** 2
MASKED = -1e30
SCALE = DH ** -0.5
PASSES = ((0, 0), (0, 1), (1, 0))


def flat(ap):
    return ap.rearrange("p a b -> p (a b)")


def build(nc, t, out):
    ctx = ExitStack()
    with ctx:
        def sb(name, shape, dt):
            return ctx.enter_context(nc.sbuf_tensor(name, shape, dt))

        xres = sb("xres", [P, RT, D], F32)
        wkx = sb("wkx", [P, 2, FC, D], BF16)
        wvx = sb("wvx", [P, 2, FC, D], BF16)
        wo = sb("wo", [P, 2, FC, D], BF16)
        wqk = sb("wqk", [P, 2, FC, 2 * AH * DH], BF16)
        wva = sb("wva", [P, 2, FC, AH * DH], BF16)
        woa = sb("woa", [P, 2, AP_, D], BF16)
        bias = sb("bias", [P, AP_, S], F32)
        ident = sb("ident", [P, P], BF16)
        onesb = sb("onesb", [P, P], BF16)
        headsum = sb("headsum", [P, HP, XH], F32)
        neghalf = sb("neghalf", [P, RT * 8], F32)
        maskb = sb("maskb", [P, NT + 1], F32)
        wl = sb("wl", [1, 2, LW], I32)
        wn = sb("wn", [1, 1], I32)
        lnx = sb("lnx", [P, 2, FC], F32)
        bkv = sb("bkv", [P, 2, HP], F32)
        bof = sb("bof", [1, D], F32)
        bo = sb("bo", [1, 2, D], BF16)
        w3s = sb("w3s", [P, D], F32)
        hs = sb("hs", [P, 4, HC], F32)
        stats = sb("stats", [P, RT, 6], F32)
        mv = sb("mv", [P, RT, 2], F32)
        var_eps = sb("ve", [P, RT], F32)
        rstd = sb("rstd", [P, RT], F32)
        sm1 = sb("sm1", [P, AH], F32)
        sm2 = sb("sm2", [P, AH], F32)
        sm3 = sb("sm3", [P, AH], F32)
        mt = sb("mt", [P, 3, RT], F32)
        fo = [sb(f"fo{i}", [P, D], F32) for i in range(2)]
        big = sb("big", [P, B * 3 * D], F32)
        tmp = sb("tmp", [P, 40 * 256], F32)

        ps = [ctx.enter_context(nc.psum_tensor(f"ps{i}", [P, 512], F32)) for i in range(8)]

        def carve(area, at, words, dt=F32):
            assert at + words <= area.shape[1], (at, words)
            piece = area[:, at:at + words]
            return piece if dt == F32 else piece.bitcast(dt)

        lnT = carve(big, 0, 4096, BF16).rearrange("p (l c n) -> p l c n", l=2, c=FC)
        qkraw = carve(big, 4096, 8192).rearrange("p (t n) -> p t n", t=RT)
        xn1 = carve(big, 4096, 4096).rearrange("p (t n) -> p t n", t=RT)
        vlat = carve(big, 12288, 4096, BF16).rearrange("p (t l n) -> p t l n", t=RT, l=2)
        qkhi = carve(big, 16384, 4096, BF16).rearrange("p (t n) -> p t n", t=RT)
        qklo = carve(big, 20480, 4096, BF16).rearrange("p (t n) -> p t n", t=RT)
        st_qkv = carve(big, 14336, 1536).rearrange("p (c n) -> p c n", c=FC)
        st_wo = carve(big, 15872, 512).rearrange("p (c n) -> p c n", c=FC)
        st_qk = carve(big, 16384, 4096).rearrange("p (c n) -> p c n", c=FC)
        st_va = carve(big, 20480, 2048).rearrange("p (c n) -> p c n", c=FC)
        st_oa = carve(big, 22528, 2048).rearrange("p (c n) -> p c n", c=AP_)
        wqkv = carve(tmp, 0, 1536, BF16).rearrange("p (l c n) -> p l c n", l=2, c=FC)
        wkg = carve(tmp, 7936 + 160, 1024).rearrange("p (c n) -> p c n", c=FC)
        lng = carve(tmp, 2048, 256)
        lnb = carve(tmp, 2304, 256)
        gq = carve(tmp, 2560, 64)
        gk = carve(tmp, 2624, 64)
        a_rn = carve(tmp, 2688, 512).rearrange("p (t n) -> p t n", t=2)
        a_rh = carve(tmp, 3200, 256, BF16).rearrange("p (t n) -> p t n", t=2)
        a_rl = carve(tmp, 3456, 256, BF16).rearrange("p (t n) -> p t n", t=2)
        sq2 = [carve(tmp, 3712 + 512 * i, 512) for i in range(2)]
        ss = carve(tmp, 4736, 128)
        rr = carve(tmp, 4864, 128)
        qpair = carve(tmp, 4992, 512, BF16).rearrange("p (b k n) -> p b k n", b=2, k=4)
        klt = carve(tmp, 5504, 256, BF16).rearrange("p (k n) -> p k n", k=4)
        pl_a = carve(tmp, 5760, 256)
        pls = carve(tmp, 9216, 256, BF16).rearrange("p (l n) -> p l n", l=2)
        mask8 = carve(tmp, 6016, 105, U8)[:, 0:NT + 1]
        maskbf = carve(tmp, 6124, 209, BF16)[:, 0:NT + 1]
        iota = carve(tmp, 6336, NT)[0:ER, :]
        codef = carve(tmp, 6752, 8)[0:ER, :]
        code = carve(tmp, 6760, 4, BF16)[0:ER, :]
        trif = carve(tmp, 6768, 128)[0:ER, 0:ER]
        tri = carve(tmp, 6896, 64, BF16)[0:ER, 0:ER]
        actf = carve(tmp, 6960, EC)[0:ER, :]
        actb = carve(tmp, 6964, EC // 2, BF16)[0:ER, :]
        pos = carve(tmp, 6968, EC)[0:ER, :]
        hot = carve(tmp, 6976, EC * NT // 2, BF16)[0:ER, :].rearrange("p (c n) -> p c n", c=EC)
        buck = carve(tmp, 7808, 128)[0:NBUCK, :]
        emb = carve(tmp, 7936, AH)[0:NBUCK, :]
        identf = carve(tmp, 7952, 128)

        acc = big[:, :].rearrange("p (b n) -> p b n", b=B)
        xt = [carve(tmp, 1024 * i, 1024).rearrange("p (i n) -> p i n", i=G) for i in range(2)]
        xch = [carve(tmp, 2048 + 512 * i, 512, BF16).rearrange("p (i n) -> p i n", i=G) for i in range(2)]
        xcl = [carve(tmp, 3072 + 512 * i, 512, BF16).rearrange("p (i n) -> p i n", i=G) for i in range(2)]
        xct = carve(tmp, 4096, 1024, BF16).rearrange("p (l c n) -> p l c n", l=2, c=FC)
        ksq = carve(tmp, 5120, 1024).rearrange("p (c n) -> p c n", c=HP)
        kct = carve(tmp, 6144, 1024, BF16).rearrange("p (l c n) -> p l c n", l=2, c=HP)
        pr = carve(tmp, 7168, 1024).rearrange("p (i n) -> p i n", i=G)
        prh = carve(tmp, 8192, 512, BF16).rearrange("p (i n) -> p i n", i=G)
        prl = carve(tmp, 8704, 512, BF16).rearrange("p (i n) -> p i n", i=G)
        qc = carve(tmp, 9216, 1024, BF16).rearrange("p (i k n) -> p i k n", i=G, k=4)
        cst, cmv, cve, crs = stats[:, 0:G, :], mv[:, 0:G, :], var_eps[:, 0:G], rstd[:, 0:G]

        def c_set(at, fields):
            got = {}
            for name, words, dt in fields:
                got[name] = carve(tmp, at, words, dt)
                at += words
            return got

        c_pb = [carve(tmp, 7168 + 512 * j, 512, BF16).rearrange("p (l b n) -> p l b n", l=2, b=2) for j in range(2)]
        c_fields = (("vl", 256, BF16), ("rl", 512, F32), ("uh", 512, BF16), ("ul", 512, BF16), ("ub", 256, F32),
                    ("ot", 256, F32), ("oth", 128, BF16), ("otl", 128, BF16))
        cs = [c_set(2560 * j, c_fields) for j in range(2)]
        c_vl = [c["vl"].rearrange("p (l n) -> p l n", l=2) for c in cs]
        c_rl = [c["rl"].rearrange("p (b n) -> p b n", b=2) for c in cs]
        c_uh, c_ul = ([c[k].rearrange("p (c b n) -> p c b n", c=FC, b=2) for c in cs] for k in ("uh", "ul"))
        c_ub, c_ot = ([c[k].rearrange("p (c b n) -> p c b n", c=HP, b=2) for c in cs] for k in ("ub", "ot"))
        c_oth, c_otl = ([c[k].rearrange("p (c n) -> p c n", c=HP) for c in cs] for k in ("oth", "otl"))

        wff = carve(big, 0, NPIECE * PIECE, BF16).rearrange("p (l n) -> p l n", l=2)
        wst = [carve(big, NPIECE * PIECE + PIECE * i, PIECE) for i in range(2)]

        def ff_weights(first, pieces, width):
            return wff[:, :, first * PIECE:(first + pieces) * PIECE].rearrange("p l (c n) -> p l c n", n=width)

        w1, w2 = ff_weights(0, FC, HID), ff_weights(FC, FC, HID)
        h1, h2 = ff_weights(2 * FC, HC, HID), ff_weights(2 * FC + HC, HC, HID)
        w3 = ff_weights(2 * FC + 2 * HC, HC * D // PIECE, D)
        rowT = carve(tmp, 0, 4096, BF16).rearrange("p (l c n) -> p l c n", l=2, c=FC)
        qkh = carve(tmp, 4096, 1024, BF16).rearrange("p (c n) -> p c n", n=P)
        qkl = carve(tmp, 5120, 1024, BF16).rearrange("p (c n) -> p c n", n=P)
        vh = carve(tmp, 6144, 512, BF16)
        vlo = carve(tmp, 6656, 512, BF16)
        sc = carve(tmp, 7168, 1024).rearrange("p (k n) -> p k n", n=S)
        sph = carve(tmp, 8192, 512, BF16).rearrange("p (c n) -> p c n", n=P)
        spl = carve(tmp, 8704, 512, BF16).rearrange("p (c n) -> p c n", n=P)
        ath, atl = sph, spl
        pT = carve(tmp, 9216, 1024, BF16).rearrange("p (l c n) -> p l c n", l=2, n=P)
        d_rn = carve(tmp, 7168, 512).rearrange("p (t n) -> p t n", t=2)
        d_rh = carve(tmp, 7680, 256, BF16).rearrange("p (t n) -> p t n", t=2)
        d_rl = carve(tmp, 7936, 256, BF16).rearrange("p (t n) -> p t n", t=2)
        hb = [carve(tmp, 4096, 4096, BF16).rearrange("p (l c n) -> p l c n", l=2, c=HC),
              wqk[:, :, :, :].rearrange("p l c (d n) -> p l (c d) n", n=BLK)]
        hf = [carve(tmp, 8192 + 512 * i, 512) for i in range(2)]
        sil = [carve(tmp, 9216 + 512 * i, 512) for i in range(2)]
        e_rn = carve(tmp, 8192, 512).rearrange("p (t n) -> p t n", t=2)
        e_rh = carve(tmp, 8704, 256, BF16).rearrange("p (t n) -> p t n", t=2)
        e_rl = carve(tmp, 8960, 256, BF16).rearrange("p (t n) -> p t n", t=2)

        q_scr = nc.dram_tensor("q_scr", [B, P, 4 * P], BF16, kind="Internal").ap()
        p_scr = nc.dram_tensor("p_scr", [RT, P, 2 * D], BF16, kind="Internal").ap()
        v_scr = nc.dram_tensor("v_scr", [RT, P, 2 * D], BF16, kind="Internal").ap()

        splits = [(st_qkv, wqkv), (wkg[:, :, 0:D], wkx), (wkg[:, :, D:2 * D], wvx), (st_wo, wo),
                  (st_qk, wqk), (st_va, wva), (st_oa, woa)]
        rows = [(xn1, a_rn, a_rh, a_rl, lnT), (xres, d_rn, d_rh, d_rl, rowT), (xres, e_rn, e_rh, e_rl, rowT)]

        names = """x_in work_in small_in wstage_in const_set qpair_zero gains
                maskbf maskb cnt act pos_ps pos_sb hot list_ps list_sb consts_bf
                bias_ps bias_sb bk_ps bk_sb wkg split_hi split_lo bo_hi bo_lo
                x1_st m_halves m_terms n_halves n_terms x1_ve x1_rs x1_n r_st r_ve r_rs r_n r_g r_b r_hi r_lo r_t r_e
                a_qkv a_raw a_sq a_ss a_vhi a_vlo a_ms a_rr a_qkn a_gq a_hi a_lo a_t a_qp a_kt a_s a_p a_phi a_plo
                a_qst a_pst a_vst
                acc_zero b_ld0 b_ld1 b_qld b_st b_ve b_rs b_n b_hi b_lo b_t b_eh b_el b_k b_ksq b_klo
                b_ss b_ms b_rr b_s b_sn b_p b_ph b_pl b_pv b_acc
                c_ld0 c_ld1 c_zero c_l c_lt c_rl c_uh c_ul c_ot c_ub c_os c_on c_oh c_ol c_o c_x
                f_ld f_hi f_lo
                d_qk d_qhi d_qlo d_v d_vhi d_vlo d_s d_sb d_mx d_sub d_ex d_sum d_ri d_pn d_phi d_plo
                gate d_pt d_peh d_pel d_pv d_ahi d_alo d_o d_x
                e_1 e_sil e_hf e_h1 e_g1 e_h2 e_g2 e_hi e_lo e_glo e_o e_os e_or e_out0 e_out1""".split()
        q = namedtuple("Semaphores", names)(*(ctx.enter_context(nc.semaphore(name)) for name in names))

        b_ld, c_ld, e_out = (q.b_ld0, q.b_ld1), (q.c_ld0, q.c_ld1), (q.e_out0, q.e_out1)

        block = ctx.enter_context(nc.Block())

        @block.sync
        def _(sp):
            for to, name in ((mask8, "mask"), (iota, "iota"), (codef, "code"), (trif, "tri"),
                             (identf, "ident"), (buck, "buck"), (emb, "emb"), (headsum[:, :, :], "headsum")):
                sp.dma_start(to, t[name]).then_inc(q.work_in, 16)
            sp.dma_start(xres[:, :, :], t["x"].rearrange("(t p) n -> p t n", p=P)).then_inc(q.x_in, 16)
            sp.dma_start(st_qkv, t["wqkv"].rearrange("(c p) n -> p c n", p=P)).then_inc(q.wstage_in, 16)
            for to, name in ((lng, "ln_l_g"), (lnb, "ln_l_b"), (gq, "q_gamma"), (gk, "k_gamma"), (w3s[:, :], "w3_s")):
                sp.dma_start(to, t[name].partition_broadcast(P)).then_inc(q.small_in, 16)
            for to, name in ((lnx[:, :, :], "lnx"), (bof[:, :], "b_out"), (hs[:, :, :], "hs")):
                sp.dma_start(to, t[name]).then_inc(q.small_in, 16)
            for to, name in ((st_wo, "wo"), (st_qk, "wqk"), (st_va, "wva"), (st_oa, "woa")):
                sp.dma_start(to, t[name].rearrange("(c p) n -> p c n", p=P)).then_inc(q.wstage_in, 16)
            sp.wait_ge(q.a_vlo, RT)
            sp.dma_start(v_scr.rearrange("t p n -> p t n"),
                         vlat.rearrange("p t l n -> p t (l n)")).then_inc(q.a_vst, 16)
            with sp.Fori(0, RT) as n:
                sp.wait_ge(q.a_qp, 2 * n + 2)
                sp.dma_start(q_scr[ds(n * 2, 2)].rearrange("b p n -> p b n"),
                             qpair.rearrange("p b k n -> p b (k n)")).then_inc(q.a_qst, 16)
                sp.wait_ge(q.a_plo, n + 1)
                sp.dma_start(p_scr[ds(n, 1)].rearrange("t p n -> p (t n)"),
                             pls.rearrange("p l n -> p (l n)")).then_inc(q.a_pst, 16)
            sp.wait_ge(q.a_qst, 16 * RT)
            sp.wait_ge(q.a_pst, 16 * RT)
            sp.wait_ge(q.a_vst, 16)
            sp.wait_ge(q.pos_sb, 3)
            sp.wait_ge(q.list_sb, 2)
            count = sp.value_load(wn[0:1, 0:1], min_val=1, max_val=NT)

            def load_x(w, h, split):
                rows_at = []
                for i in range(G):
                    bi = sp.value_load(wl[0:1, 0, ds(w + i, 1)], min_val=0, max_val=B - 1)
                    ki = sp.value_load(wl[0:1, 1, ds(w + i, 1)], min_val=0, max_val=KT)
                    rows_at.append(sp.snap(bi * SC + ki * P))
                if split is not None:
                    sp.wait_ge(q.b_lo, split)
                for i in range(G):
                    sp.dma_start(xt[h][:, i, :], t["ctx"][ds(rows_at[i], P), :]).then_inc(b_ld[h], 16)

            def load_q(w):
                for i in range(G):
                    bi = sp.value_load(wl[0:1, 0, ds(w + i, 1)], min_val=0, max_val=B - 1)
                    sp.dma_start(qc[:, i].rearrange("p k n -> p (k n)"),
                                 q_scr[ds(bi, 1)].rearrange("b p n -> p (b n)")).then_inc(q.b_qld, 16)

            load_x(0, 0, None)
            load_x(G, 1, None)
            with sp.Fori(0, count, 2 * G) as w:
                for h in range(2):
                    sp.wait_ge(q.b_s, w + h * G)
                    load_q(w + h * G)
                    load_x(w + (h + 2) * G, h, w + (h + 1) * G)
            sp.wait_ge(q.b_lo, count + 2 * G)
            sp.sem_inc(q.gate, 1)
            sp.wait_ge(q.b_klo, count + G)
            sp.wait_ge(q.b_ksq, count + G)
            sp.wait_ge(q.b_acc, count)

            def load_c(n, j):
                for b in range(2):
                    r = slice(b * S, b * S + S)
                    sp.dma_start(c_pb[j][r, :, b, :], p_scr[ds(n, 1), r].rearrange("t p (l n) -> p (t l) n", l=2)
                                 ).then_inc(c_ld[j], 16)
                sp.dma_start(c_vl[j].rearrange("p l n -> p (l n)"),
                             v_scr[ds(n, 1)].rearrange("t p n -> p (t n)")).then_inc(c_ld[j], 16)

            sp.wait_ge(q.c_zero, 4)
            for j in range(2):
                load_c(j, j)
            with sp.Fori(2, RT - 1, 2) as n:
                for j in range(2):
                    sp.wait_ge(q.c_x, n + (j - 1))
                    load_c(n + j, j)
            sp.wait_ge(q.c_x, RT)
            with sp.Fori(0, NPIECE - 1, 2) as k:
                for j in range(2):
                    sp.wait_ge(q.f_lo, k)
                    sp.dma_start(wst[j], t["wff"][ds(k + j, 1)].rearrange("t p n -> p (t n)")).then_inc(q.f_ld, 16)
            with sp.Fori(0, RT - 1, 2) as n:
                for j in range(2):
                    sp.wait_ge(q.e_or, n + j + 1)
                    sp.dma_start(out[ds((n + j) * P, P), :], fo[j][:, :]).then_inc(e_out[j], 16)
            for j in range(2):
                sp.wait_ge(e_out[j], 16 * RT // 2)

        @block.gpsimd
        def _(po):
            po.memset(neghalf[:, :], -0.5).then_inc(q.const_set, 1)
            po.memset(onesb[:, :], 1.0).then_inc(q.const_set, 1)
            po.memset(wl[:, :, :], 0).then_inc(q.const_set, 1)
            po.memset(qpair.rearrange("p b k n -> p (b k n)"), 0.0).then_inc(q.qpair_zero, 1)
            po.wait_ge(q.small_in, 16 * 8)
            po.tensor_tensor(gq, gq, gk, ALU.mult).then_inc(q.gains, 1)
            po.wait_ge(q.gains, 1)
            po.tensor_scalar(gq, gq, SCALE, None, ALU.mult).then_inc(q.gains, 1)
            po.wait_ge(q.const_set, 3)
            po.wait_ge(q.x1_ve, 1)
            po.tensor_tensor(rstd[:, :], var_eps[:, :], neghalf[:, 0:RT], ALU.pow).then_inc(q.x1_rs, 1)

            def rows_norm(k):
                po.wait_ge(q.r_ve, k + 1)
                po.tensor_tensor(rstd[:, :], var_eps[:, :], neghalf[:, 0:RT], ALU.pow).then_inc(q.r_rs, 1)

            def rows_low(k):
                _, rn, rh, rl, _ = rows[k]
                with po.Fori(0, RT - 1, 2) as n:
                    for j in range(2):
                        if k == 0:
                            po.wait_ge(q.r_n, n + j + 1)
                            po.tensor_tensor(rn[:, j], rn[:, j], lng, ALU.mult).then_inc(q.r_g, 1)
                            po.wait_ge(q.r_g, n + j + 1)
                            po.tensor_tensor(rn[:, j], rn[:, j], lnb, ALU.add).then_inc(q.r_b, 1)
                        po.wait_ge(q.r_hi, n + (k * RT + j + 1))
                        po.tensor_tensor(rl[:, j], rn[:, j], rh[:, j], ALU.subtract).then_inc(q.r_lo, 1)

            rows_norm(0)
            rows_low(0)
            po.wait_ge(q.a_ms, 1)
            po.tensor_tensor(rr, ss, neghalf[:, :], ALU.pow).then_inc(q.a_rr, 1)
            with po.Fori(0, RT) as n:
                row = qkraw[:, ds(n, 1), 0:D].rearrange("p t (h d) -> p (t h) d", h=XH)
                po.wait_ge(q.a_qkn, n + 1)
                po.tensor_tensor(row, row, gq.rearrange("p (h d) -> p h d", h=1).broadcast_to([P, XH, DH]),
                                 ALU.mult).then_inc(q.a_gq, 1)
                po.wait_ge(q.a_hi, n + 1)
                po.tensor_tensor(flat(qklo[:, ds(n, 1), :]), flat(qkraw[:, ds(n, 1), :]),
                                 flat(qkhi[:, ds(n, 1), :]), ALU.subtract).then_inc(q.a_lo, 1)
            with po.Fori(0, RT) as n:
                po.wait_ge(q.a_phi, n + 1)
                po.tensor_tensor(pls[:, 1], pl_a, pls[:, 0], ALU.subtract).then_inc(q.a_plo, 1)
            po.wait_ge(q.a_pst, 16 * RT)
            po.wait_ge(q.pos_sb, 3)
            count = po.value_load(wn[0:1, 0:1], min_val=1, max_val=NT)

            def b_front(w1, h):
                po.wait_ge(q.b_ve, w1)
                po.tensor_tensor(crs, cve, neghalf[:, 0:G], ALU.pow).then_inc(q.b_rs, G)
                po.wait_ge(q.b_hi, w1)
                po.tensor_tensor(flat(xcl[h]), flat(xt[h]), flat(xch[h]), ALU.subtract).then_inc(q.b_lo, G)

            def b_back(w1):
                po.wait_ge(q.b_ms, w1)
                po.tensor_tensor(sm2[:, :], sm1[:, :], neghalf[:, 0:AH], ALU.pow).then_inc(q.b_rr, G)

            b_front(G, 0)
            b_front(2 * G, 1)
            with po.Fori(0, count, 2 * G) as w:
                for h in range(2):
                    b_back(w + (h + 1) * G)
                    b_front(w + (h + 3) * G, h)
            with po.Fori(0, RT - 1, 2) as n:
                for j in range(2):
                    po.wait_ge(q.c_uh, n + (j + 1))
                    for c in range(FC):
                        po.tensor_tensor(c_ul[j][:, c], acc[:, ds(2 * n + 2 * j, 2), c * D:c * D + D], c_uh[j][:, c],
                                         ALU.subtract).then_inc(q.c_ul, 1)
            rows_norm(1)
            rows_low(1)

            def d_pair(n):
                po.wait_ge(q.d_mx, n + 1)
                po.tensor_tensor(sc, sc, sm1[:, :].rearrange("p (k o) -> p k o", o=1).broadcast_to([P, AH, S]),
                                 ALU.subtract).then_inc(q.d_sub, 1)
                po.wait_ge(q.d_ri, n + 1)
                po.tensor_tensor(sc, sc, sm3[:, :].rearrange("p (k o) -> p k o", o=1).broadcast_to([P, AH, S]),
                                 ALU.mult).then_inc(q.d_pn, 1)

            with po.Fori(0, NPIECE // 2) as n:
                d_pair(n)
                for j in range(2):
                    po.wait_ge(q.f_ld, 32 * n + 32)
                    po.tensor_copy(wff[:, 0, ds((2 * n + j) * PIECE, PIECE)], wst[j]).then_inc(q.f_hi, 1)
                    po.wait_ge(q.f_hi, 2 * n + (j + 1))
                    po.tensor_tensor(wff[:, 1, ds((2 * n + j) * PIECE, PIECE)], wst[j],
                                     wff[:, 0, ds((2 * n + j) * PIECE, PIECE)], ALU.subtract).then_inc(q.f_lo, 1)
            with po.Fori(NPIECE // 2, RT) as n:
                d_pair(n)
            rows_norm(2)
            rows_low(2)
            with po.Fori(0, NB) as n:
                for m in range(HC):
                    po.wait_ge(q.e_hi, HC * n + (m + 1))
                    po.tensor_tensor(hb[0][:, 1, m], hf[m % 2], hb[0][:, 0, m], ALU.subtract).then_inc(q.e_lo, 1)

        @block.scalar
        def _(act):
            act.wait_ge(q.wstage_in, 16 * 5)
            for k, (full, parts) in enumerate(splits):
                if k == 1:
                    act.wait_ge(q.wkg, FC)
                act.activation(parts[:, 0], full, ACT.Copy).then_inc(q.split_hi, 1)
            act.wait_ge(q.small_in, 16 * 8)
            act.activation(bo[:, 0, :], bof[:, :], ACT.Copy).then_inc(q.bo_hi, 1)

            def rows_high(k):
                _, rn, rh, _, xT = rows[k]
                ready = q.r_b if k == 0 else q.r_n

                def store(n, j):
                    act.wait_ge(q.r_t, n + (k * RT + 1))
                    act.activation(xT[:, :, :, ds(n * P, P)],
                                   ps[j][:, :].bitcast(BF16)[:, 0:4 * P].rearrange("p (l c n) -> p l c n", l=2, c=FC),
                                   ACT.Copy).then_inc(q.r_e, 1)

                with act.Fori(0, RT - 1, 2) as n:
                    for j in range(2):
                        act.wait_ge(ready, n + (j + 1 if k == 0 else k * RT + j + 1))
                        act.activation(rh[:, j], rn[:, j], ACT.Copy).then_inc(q.r_hi, 1)
                    for j in range(2):
                        store(n + j, j)

            rows_high(0)
            with act.Fori(0, RT - 1, 2) as n:
                for j in range(2):
                    act.wait_ge(q.a_qkv, n + (j + 1))
                    act.wait_ge(q.a_ss, n + j)
                    act.activation(sq2[j], ps[2 * j][:, :], ACT.Square).then_inc(q.a_sq, 1)
                    act.activation(vlat[:, ds(n + j, 1), 0, :].rearrange("p t n -> p (t n)"),
                                   ps[2 * j + 1][:, 0:D], ACT.Copy).then_inc(q.a_vhi, 1)
            with act.Fori(0, RT) as n:
                act.wait_ge(q.a_gq, n + 1)
                act.activation(flat(qkhi[:, ds(n, 1), :]), flat(qkraw[:, ds(n, 1), :]), ACT.Copy).then_inc(q.a_hi, 1)
            with act.Fori(0, RT) as n:
                act.wait_ge(q.a_t, n + 1)
                act.activation(klt, ps[6][:, :].rearrange("p (k n) -> p k n", k=4), ACT.Copy).then_inc(q.a_kt, 1)
                act.wait_ge(q.a_s, n + 1)
                act.wait_ge(q.a_plo, n)
                act.activation(pl_a, ps[5][:, 0:D], ACT.Exp).then_inc(q.a_p, 1)
                act.wait_ge(q.a_p, n + 1)
                act.wait_ge(q.a_pst, 16 * n)
                act.activation(pls[:, 0], pl_a, ACT.Copy).then_inc(q.a_phi, 1)
            act.wait_ge(q.a_pst, 16 * RT)
            act.wait_ge(q.a_qst, 16 * RT)
            act.wait_ge(q.pos_sb, 3)
            act.wait_ge(q.list_sb, 2)
            act.wait_ge(q.maskb, 1)
            act.wait_ge(q.bk_sb, 1)
            count = act.value_load(wn[0:1, 0:1], min_val=1, max_val=NT)

            def b_high(w1, h):
                act.wait_ge(q.b_n, w1)
                act.activation(flat(xch[h]), flat(xt[h]), ACT.Copy).then_inc(q.b_hi, G)

            def b_tokens(w1):
                act.wait_ge(q.b_t, w1)
                act.activation(xct[:, 0].rearrange("p c n -> p (c n)"), ps[0][:, :].bitcast(BF16),
                               ACT.Copy).then_inc(q.b_eh, G)

            def b_keys(w1):
                act.wait_ge(q.b_k, w1)
                for c in range(HP):
                    act.activation(kct[:, 0, c], ps[2 + c][:, :], ACT.Identity,
                                   bias=bkv[:, 0, c:c + 1])
                    act.activation(ksq[:, c], ps[2 + c][:, :], ACT.Square,
                                   bias=bkv[:, 0, c:c + 1]).then_inc(q.b_ksq, G // HP)

            def b_exp(w):
                act.wait_ge(q.b_sn, w + G)
                for i in range(G):
                    bi = act.value_load(wl[0:1, 0, ds(w + i, 1)], min_val=0, max_val=B - 1)
                    ki = act.value_load(wl[0:1, 1, ds(w + i, 1)], min_val=0, max_val=KT)
                    act.activation(pr[:, i], pr[:, i], ACT.Exp, bias=maskb[:, ds(bi * KT + ki, 1)]).then_inc(q.b_p, 1)

            def b_exp_high(w):
                act.wait_ge(q.b_p, w + G)
                act.wait_ge(q.b_pv, w)
                act.activation(flat(prh), flat(pr), ACT.Copy).then_inc(q.b_ph, G)

            b_high(G, 0)
            b_tokens(G)
            b_keys(G)
            b_high(2 * G, 1)
            with act.Fori(0, count, 2 * G) as w:
                for h in range(2):
                    b_exp(w + h * G)
                    b_tokens(w + (h + 2) * G)
                    b_exp_high(w + h * G)
                    act.wait_ge(q.b_ss, w + (h + 1) * G)
                    act.wait_ge(q.b_s, w + (h + 1) * G)
                    b_keys(w + (h + 2) * G)
                    act.wait_ge(q.b_pv, w + (h + 1) * G)
                    b_high(w + (h + 3) * G, h)
            act.wait_ge(q.b_acc, count)
            act.wait_ge(q.b_lo, count + 2 * G)
            act.wait_ge(q.b_t, count + G)
            with act.Fori(0, RT - 1, 2) as n:
                for j in range(2):
                    if j == 0:
                        act.wait_ge(q.c_ot, n)
                    for c in range(FC):
                        last = act.activation(c_uh[j][:, c], acc[:, ds(2 * n + 2 * j, 2), c * D:c * D + D], ACT.Copy)
                    last.then_inc(q.c_uh, 1)
                for j in range(2):
                    act.wait_ge(q.c_on, 4 * n + (4 * j + 4))
                    act.activation(c_oth[j], c_ot[j].rearrange("p c b n -> p c (b n)"), ACT.Copy).then_inc(q.c_oh, 1)
            rows_high(1)

            def d_qk(n, c):
                act.wait_ge(q.d_qk, 4 * n + (c + 1))
                act.activation(qkh[:, 4 * c:4 * c + 4].rearrange("p c n -> p (c n)"), ps[c][:, :], ACT.Copy,
                               scale=SCALE if c < 2 else 1.0).then_inc(q.d_qhi, 1)

            def d_v(n):
                for k in range(2):
                    act.wait_ge(q.d_v, 2 * n + (k + 1))
                    act.activation(vh[:, k * 512:k * 512 + 512], ps[4 + k][:, :], ACT.Copy).then_inc(q.d_vhi, 1)

            def d_pair(n, last):
                if not last:
                    act.wait_ge(q.d_s, n + 1)
                    d_qk(n + 1, 0)
                    d_qk(n + 1, 1)
                act.wait_ge(q.d_sub, n + 1)
                act.activation(flat(sc), flat(sc), ACT.Exp).then_inc(q.d_ex, 1)
                if not last:
                    d_qk(n + 1, 2)
                    d_qk(n + 1, 3)
                act.wait_ge(q.d_pn, n + 1)
                act.wait_ge(q.d_o, n)
                act.activation(flat(sph), flat(sc), ACT.Copy).then_inc(q.d_phi, 1)
                act.wait_ge(q.d_pt, 2 * n + 1)
                act.activation(pT[:, 0].rearrange("p c n -> p (c n)"), ps[4][:, :].bitcast(BF16),
                               ACT.Copy).then_inc(q.d_peh, 1)
                act.wait_ge(q.d_pv, n + 1)
                for k in range(2):
                    act.activation(ath[:, :, k * S:k * S + S], ps[6 + k][:, :].rearrange("p (c n) -> p c n", c=AP_),
                                   ACT.Copy).then_inc(q.d_ahi, 1)
                if not last:
                    d_v(n + 1)

            for c in range(4):
                d_qk(0, c)
            d_v(0)
            with act.Fori(0, RT - 1) as n:
                d_pair(n, False)
            d_pair(RT - 1, True)
            rows_high(2)
            with act.Fori(0, NB) as n:
                for m in range(HC):
                    act.wait_ge(q.e_1, HC * n + (m + 1))
                    if m < 2:
                        act.wait_ge(q.e_hf, HC * n)
                    else:
                        act.wait_ge(q.e_hf, HC * n + (m - 1))
                    act.activation(sil[m % 2], ps[2 * (m % 2)][:, :], ACT.Silu,
                                   scale=hs[:, 0, m:m + 1]).then_inc(q.e_sil, 1)
                for layer, (ready, done) in enumerate(((q.e_h1, q.e_g1), (q.e_h2, q.e_g2))):
                    for m in range(HC):
                        act.wait_ge(ready, HC * n + (m + 1))
                        act.activation(hb[1 - layer][:, 0, m], ps[4 + m % 2][:, :], ACT.Gelu,
                                       scale=hs[:, 2 + layer, m:m + 1])
                        if m < 2 and layer == 0:
                            act.wait_ge(q.e_lo, HC * n + HC)
                        else:
                            act.wait_ge(q.e_glo, 2 * HC * n + (HC * layer + m - 1))
                        act.activation(hf[m % 2], ps[4 + m % 2][:, :], ACT.Gelu,
                                       scale=hs[:, 2 + layer, m:m + 1]).then_inc(done, 1)

        @block.vector
        def _(v):
            rows_moments, group_moments = (q.m_halves, q.m_terms), (q.n_halves, q.n_terms)

            def moments(st, to, var, sems, k, done, step=1):
                halves, terms = sems
                n = st.shape[1]
                dif, dev, spread = mt[:, 0, 0:n], mt[:, 1, 0:n], mt[:, 2, 0:n]
                v.tensor_tensor(to[:, :, 0], st[:, :, 1], st[:, :, 4], ALU.add).then_inc(halves, step)
                v.tensor_tensor(dif, st[:, :, 1], st[:, :, 4], ALU.subtract).then_inc(halves, step)
                v.tensor_tensor(dev, st[:, :, 2], st[:, :, 5], ALU.add).then_inc(halves, step)
                v.wait_ge(halves, 3 * k)
                v.tensor_scalar(to[:, :, 0], to[:, :, 0], 0.5, None, ALU.mult).then_inc(terms, step)
                v.scalar_tensor_tensor(spread, dif, 0.25, dif, ALU.mult, ALU.mult).then_inc(terms, step)
                v.tensor_scalar(dev, dev, 1.0 / D, LN_EPS, ALU.mult, ALU.add).then_inc(terms, step)
                v.wait_ge(terms, 3 * k)
                v.tensor_tensor(var, dev, spread, ALU.add).then_inc(done, step)

            v.wait_ge(q.work_in, 16 * 8)
            v.tensor_copy(maskbf, mask8).then_inc(q.maskbf, 1)
            v.wait_ge(q.maskbf, 1)
            v.tensor_scalar(maskb[:, :], maskbf, 1.0, -MASKED, ALU.subtract, ALU.mult).then_inc(q.maskb, 1)
            v.tensor_copy(tri, trif).then_inc(q.consts_bf, 1)
            v.tensor_copy(code, codef).then_inc(q.consts_bf, 1)
            v.tensor_copy(ident[:, :], identf).then_inc(q.consts_bf, 1)
            v.wait_ge(q.x_in, 16)
            with v.Fori(0, RT) as n:
                v.bn_stats(flat(stats[:, ds(n, 1), :]), flat(xres[:, ds(n, 1), :])).then_inc(q.x1_st, 1)
            v.wait_ge(q.x1_st, RT)
            moments(stats, mv, var_eps[:, :], rows_moments, 1, q.x1_ve)
            v.wait_ge(q.cnt, 1)
            v.tensor_scalar(actf, ps[6][0:ER, 0:EC], 1.0, None, ALU.min).then_inc(q.act, 1)
            v.tensor_scalar(actb, ps[6][0:ER, 0:EC], 1.0, None, ALU.min).then_inc(q.act, 1)
            v.wait_ge(q.pos_ps, 1)
            v.tensor_copy(pos, ps[6][0:ER, 8:8 + EC]).then_inc(q.pos_sb, 1)
            v.tensor_scalar(wn[:, :], ps[6][0:1, 16:17], 1.0, 2.0 * G - 1, ALU.max, ALU.add).then_inc(q.pos_sb, 1)
            v.wait_ge(q.pos_sb, 2)
            v.tensor_scalar(wn[:, :], wn[:, :], -2 * G, None, ALU.bitwise_and).then_inc(q.pos_sb, 1)
            for c in range(EC):
                v.tensor_scalar(hot[:, c], iota, pos[:, c:c + 1], actf[:, c:c + 1],
                                ALU.is_equal, ALU.mult).then_inc(q.hot, 1)
            v.wait_ge(q.const_set, 3)
            v.wait_ge(q.list_ps, 2)
            for k in range(2):
                v.tensor_copy(wl[:, k, 0:NT], ps[6 + k][0:1, 0:NT]).then_inc(q.list_sb, 1)
            v.wait_ge(q.bias_ps, 1)
            for k in range(2):
                for h in range(2):
                    r = slice(h * S, h * S + S)
                    v.tensor_copy(bias[r, :, k * 32:k * 32 + 32],
                                  ps[k][r, :].rearrange("p (j c h) -> p c h j", c=AP_, h=2)[:, :, h, :]
                                  ).then_inc(q.bias_sb, 1)
            v.wait_ge(q.small_in, 16 * 8)
            v.wait_ge(q.wstage_in, 16 * 5)
            for c in range(FC):
                v.tensor_scalar(wkg[:, c], st_qkv[:, c, D:3 * D], lnx[:, 0, c:c + 1], None, ALU.mult).then_inc(q.wkg, 1)
            v.wait_ge(q.wkg, FC)
            for k, (full, parts) in enumerate(splits):
                v.wait_ge(q.split_hi, k + 1)
                v.tensor_tensor(parts[:, 1], full, parts[:, 0], ALU.subtract).then_inc(q.split_lo, 1)
            v.wait_ge(q.bk_ps, 1)
            v.tensor_copy(bkv[:, :, :].rearrange("p k h -> p (k h)"), ps[6][:, 0:2 * HP]).then_inc(q.bk_sb, 1)
            v.wait_ge(q.bo_hi, 1)
            v.tensor_tensor(bo[:, 1, :], bof[:, :], bo[:, 0, :], ALU.subtract).then_inc(q.bo_lo, 1)
            v.wait_ge(q.x1_rs, 1)
            with v.Fori(0, RT) as n:
                v.tensor_scalar(flat(xn1[:, ds(n, 1), :]), flat(xres[:, ds(n, 1), :]), mv[:, ds(n, 1), 0],
                                rstd[:, ds(n, 1)], ALU.subtract, ALU.mult).then_inc(q.x1_n, 1)
            v.wait_ge(q.x1_n, RT)

            def rows_norm(k):
                src, rn, _, _, _ = rows[k]
                with v.Fori(0, RT) as n:
                    v.bn_stats(flat(stats[:, ds(n, 1), :]), flat(src[:, ds(n, 1), :])).then_inc(q.r_st, 1)
                v.wait_ge(q.r_st, (k + 1) * RT)
                moments(stats, mv, var_eps[:, :], rows_moments, k + 2, q.r_ve)
                v.wait_ge(q.r_rs, k + 1)
                for j in range(2):
                    v.tensor_scalar(rn[:, j], src[:, j], mv[:, j, 0:1], rstd[:, j:j + 1],
                                    ALU.subtract, ALU.mult).then_inc(q.r_n, 1)
                with v.Fori(2, RT - 1, 2) as n:
                    for j in range(2):
                        v.wait_ge(q.r_lo, n + (k * RT + j - 1))
                        v.tensor_scalar(rn[:, j], flat(src[:, ds(n + j, 1), :]), mv[:, ds(n + j, 1), 0],
                                        rstd[:, ds(n + j, 1)], ALU.subtract, ALU.mult).then_inc(q.r_n, 1)

            rows_norm(0)
            with v.Fori(0, RT - 1, 2) as n:
                for j in range(2):
                    v.wait_ge(q.a_sq, n + (j + 1))
                    v.tensor_copy(flat(qkraw[:, ds(n + j, 1), :]), ps[2 * j][:, :]).then_inc(q.a_raw, 1)
                    v.wait_ge(q.a_vhi, n + (j + 1))
                    v.tensor_tensor(vlat[:, ds(n + j, 1), 1, :].rearrange("p t n -> p (t n)"), ps[2 * j + 1][:, 0:D],
                                    vlat[:, ds(n + j, 1), 0, :].rearrange("p t n -> p (t n)"),
                                    ALU.subtract).then_inc(q.a_vlo, 1)
                    v.tensor_reduce(ss[:, ds((n + j) * 8, 8)], sq2[j].rearrange("p (h d) -> p h d", d=DH),
                                    AX.X, ALU.add).then_inc(q.a_ss, 1)
            v.wait_ge(q.a_ss, RT)
            v.tensor_scalar(ss, ss, 1.0 / DH, RMS_FLOOR, ALU.mult, ALU.max).then_inc(q.a_ms, 1)
            v.wait_ge(q.a_rr, 1)
            v.wait_ge(q.a_raw, RT)
            with v.Fori(0, RT) as n:
                row = qkraw[:, ds(n, 1), :].rearrange("p t (h d) -> p (t h) d", d=DH)
                v.tensor_tensor(row, row, rr[:, ds(n * 8, 8)].rearrange("p (h o) -> p h o", o=1)
                                .broadcast_to([P, 8, DH]), ALU.mult).then_inc(q.a_qkn, 1)
            v.wait_ge(q.qpair_zero, 1)
            with v.Fori(0, RT) as n:
                v.wait_ge(q.a_t, n + 1)
                v.wait_ge(q.a_qst, 16 * n)
                v.wait_ge(q.a_s, n)
                for h in range(2):
                    r = slice(h * S, h * S + S)
                    v.tensor_copy(qpair[r, :, :, h * S:h * S + S],
                                  ps[4][r, :].rearrange("p (k b n) -> p b k n", k=4, b=2)
                                  ).then_inc(q.a_qp, 1)
            v.wait_ge(q.a_pst, 16 * RT)
            v.wait_ge(q.a_vst, 16)
            v.memset(big[:, :], 0.0).then_inc(q.acc_zero, 1)
            count = v.value_load(wn[0:1, 0:1], min_val=1, max_val=NT)

            def b_norm(w1, h):
                v.wait_ge(b_ld[h], 8 * w1 + (1 - h) * 8 * G)
                for i in range(G):
                    v.bn_stats(cst[:, i], xt[h][:, i]).then_inc(q.b_st, 1)
                v.wait_ge(q.b_st, w1)
                moments(cst, cmv, cve, group_moments, w1, q.b_ve, G)
                v.wait_ge(q.b_rs, w1)
                for i in range(G):
                    v.tensor_scalar(xt[h][:, i], xt[h][:, i], cmv[:, i, 0:1], crs[:, i:i + 1],
                                    ALU.subtract, ALU.mult).then_inc(q.b_n, 1)

            def b_keys(w1):
                v.wait_ge(q.b_t, w1)
                v.tensor_copy(xct[:, 1].rearrange("p c n -> p (c n)"), ps[1][:, :].bitcast(BF16)).then_inc(q.b_el, G)
                for c in range(HP):
                    v.wait_ge(q.b_ksq, w1 - G // HP * (HP - 1 - c))
                    v.scalar_tensor_tensor(kct[:, 1, c], ps[2 + c][:, :], bkv[:, 0, c:c + 1], kct[:, 0, c],
                                           ALU.add, ALU.subtract).then_inc(q.b_klo, G // HP)

            def b_scores(w1):
                v.wait_ge(q.b_ss, w1)
                v.tensor_scalar(sm1[:, :], ps[4][:, 0:AH], 1.0 / DH, RMS_FLOOR, ALU.mult, ALU.max).then_inc(q.b_ms, G)
                v.wait_ge(q.b_rr, w1)
                v.wait_ge(q.b_s, w1)
                for k in range(2):
                    v.tensor_tensor(pr[:, 2 * k:2 * k + 2].rearrange("p i (h n) -> p (i h) n", n=S),
                                    ps[5 + k][:, :].rearrange("p (k n) -> p k n", n=S),
                                    sm2[:, 8 * k:8 * k + 8].rearrange("p (k o) -> p k o", o=1).broadcast_to([P, 8, S]),
                                    ALU.mult).then_inc(q.b_sn, G // 2)

            def b_sums(w):
                v.wait_ge(q.b_ph, w + G)
                v.tensor_tensor(flat(prl), flat(pr), flat(prh), ALU.subtract).then_inc(q.b_pl, G)
                for i in range(G):
                    bi = v.value_load(wl[0:1, 0, ds(w + i, 1)], min_val=0, max_val=B - 1)
                    v.wait_ge(q.b_pv, w + (i + 1))
                    v.wait_ge(q.b_acc, w + i)
                    v.tensor_tensor(acc[:, ds(bi, 1), 0:2 * D].rearrange("p b n -> p (b n)"),
                                    acc[:, ds(bi, 1), 0:2 * D].rearrange("p b n -> p (b n)"),
                                    ps[7 if i % 2 == 0 else 5][:, :], ALU.add)
                    v.tensor_tensor(acc[:, ds(bi, 1), 2 * D:3 * D].rearrange("p b n -> p (b n)"),
                                    acc[:, ds(bi, 1), 2 * D:3 * D].rearrange("p b n -> p (b n)"),
                                    ps[4][:, D:2 * D] if i % 2 == 0 else ps[6][:, 0:D], ALU.add).then_inc(q.b_acc, 1)

            v.wait_ge(q.acc_zero, 1)
            b_norm(G, 0)
            b_keys(G)
            b_norm(2 * G, 1)
            with v.Fori(0, count, 2 * G) as w:
                for h in range(2):
                    b_scores(w + (h + 1) * G)
                    b_keys(w + (h + 2) * G)
                    b_norm(w + (h + 3) * G, h)
                    b_sums(w + h * G)
            v.wait_ge(q.b_acc, count)

            def c_sums(n, j):
                both = ds(2 * n, 2)
                v.wait_ge(q.c_l, n + 1)
                v.tensor_tensor(c_rl[j], ps[j][:, :].rearrange("p (b n) -> p b n", b=2), acc[:, both, 2 * D:3 * D],
                                ALU.add).then_inc(q.c_lt, 1)
                v.wait_ge(q.c_lt, n + 1)
                v.reciprocal(c_rl[j], c_rl[j]).then_inc(q.c_rl, 1)

            def c_rest(n, j):
                v.wait_ge(q.c_ot, n + 1)
                for h2 in range(2):
                    r = slice(h2 * DH, h2 * DH + DH)
                    for hp in range(HP):
                        h = 2 * hp + h2
                        head = slice(h * S, h * S + S)
                        v.scalar_tensor_tensor(c_ub[j][r, hp], acc[r, ds(2 * n, 2), 2 * D + h * S:2 * D + h * S + S],
                                               bkv[r, 1, hp:hp + 1],
                                               ps[2 + 2 * hp + j][r, 0:P].rearrange("p (b n) -> p b n", b=2),
                                               ALU.mult, ALU.add).then_inc(q.c_ub, 1)
                v.wait_ge(q.c_ub, 4 * n + 4)
                for h2 in range(2):
                    r = slice(h2 * DH, h2 * DH + DH)
                    for hp in range(HP):
                        h = 2 * hp + h2
                        v.tensor_tensor(c_ot[j][r, hp], c_ub[j][r, hp], c_rl[j][r, :, h * S:h * S + S],
                                        ALU.mult).then_inc(q.c_on, 1)
                v.wait_ge(q.c_oh, n + 1)
                v.tensor_tensor(c_otl[j], c_ot[j].rearrange("p c b n -> p c (b n)"), c_oth[j],
                                ALU.subtract).then_inc(q.c_ol, 1)
                v.wait_ge(q.c_o, n + 1)
                v.tensor_tensor(flat(xres[:, ds(n, 1), :]), flat(xres[:, ds(n, 1), :]), ps[6 + j][:, 0:D],
                                ALU.add).then_inc(q.c_x, 1)

            for j in range(2):
                for b in range(2):
                    v.memset(c_pb[j][b * S:b * S + S, :, 1 - b, :], 0.0).then_inc(q.c_zero, 1)
            c_sums(0, 0)
            with v.Fori(0, RT - 2, 2) as n:
                c_sums(n + 1, 1)
                c_rest(n, 0)
                c_sums(n + 2, 0)
                c_rest(n + 1, 1)
            c_sums(RT - 1, 1)
            c_rest(RT - 2, 0)
            c_rest(RT - 1, 1)
            v.wait_ge(q.c_x, RT)

            rows_norm(1)

            def d_qk(n, c):
                v.wait_ge(q.d_qhi, 4 * n + (c + 1))
                v.scalar_tensor_tensor(qkl[:, 4 * c:4 * c + 4].rearrange("p c n -> p (c n)"), ps[c][:, :],
                                       SCALE if c < 2 else 1.0,
                                       qkh[:, 4 * c:4 * c + 4].rearrange("p c n -> p (c n)"),
                                       ALU.mult, ALU.subtract).then_inc(q.d_qlo, 1)

            def d_v(n):
                for k in range(2):
                    v.wait_ge(q.d_vhi, 2 * n + (k + 1))
                    v.tensor_tensor(vlo[:, k * 512:k * 512 + 512], ps[4 + k][:, :], vh[:, k * 512:k * 512 + 512],
                                    ALU.subtract).then_inc(q.d_vlo, 1)

            def d_pair(n, last):
                v.wait_ge(q.d_s, n + 1)
                for k in range(2):
                    v.tensor_tensor(sc[:, 8 * k:8 * k + 8].rearrange("p (c b) n -> p c b n", b=2),
                                    ps[6 + k][:, :].rearrange("p (c b n) -> p c b n", c=4, b=2),
                                    bias[:, 4 * k:4 * k + 4, :].rearrange("p c (o n) -> p c o n", o=1)
                                    .broadcast_to([P, 4, 2, S]), ALU.add).then_inc(q.d_sb, 1)
                v.wait_ge(q.d_sb, 2 * n + 2)
                v.tensor_reduce(sm1[:, :], sc, AX.X, ALU.max).then_inc(q.d_mx, 1)
                if not last:
                    d_qk(n + 1, 0)
                    d_qk(n + 1, 1)
                v.wait_ge(q.d_ex, n + 1)
                v.tensor_reduce(sm2[:, :], sc, AX.X, ALU.add).then_inc(q.d_sum, 1)
                v.wait_ge(q.d_sum, n + 1)
                v.reciprocal(sm3[:, :], sm2[:, :]).then_inc(q.d_ri, 1)
                if not last:
                    d_qk(n + 1, 2)
                    d_qk(n + 1, 3)
                v.wait_ge(q.d_phi, n + 1)
                v.tensor_tensor(spl.rearrange("p c n -> p (c n)"), flat(sc), sph.rearrange("p c n -> p (c n)"),
                                ALU.subtract).then_inc(q.d_plo, 1)
                v.wait_ge(q.d_pt, 2 * n + 2)
                v.tensor_copy(pT[:, 1].rearrange("p c n -> p (c n)"), ps[5][:, :].bitcast(BF16)).then_inc(q.d_pel, 1)
                for k in range(2):
                    v.wait_ge(q.d_ahi, 2 * n + (k + 1))
                    v.tensor_tensor(atl[:, :, k * S:k * S + S], ps[6 + k][:, :].rearrange("p (c n) -> p c n", c=AP_),
                                    ath[:, :, k * S:k * S + S], ALU.subtract).then_inc(q.d_alo, 1)
                v.wait_ge(q.d_o, n + 1)
                v.tensor_tensor(flat(xres[:, ds(n, 1), :]), flat(xres[:, ds(n, 1), :]), ps[0][:, 0:D],
                                ALU.add).then_inc(q.d_x, 1)
                if not last:
                    d_v(n + 1)

            for c in range(4):
                d_qk(0, c)
            d_v(0)
            with v.Fori(0, RT - 1) as n:
                d_pair(n, False)
            d_pair(RT - 1, True)
            v.wait_ge(q.d_x, RT)

            rows_norm(2)
            with v.Fori(0, NB) as n:
                for m in range(HC):
                    v.wait_ge(q.e_sil, HC * n + (m + 1))
                    if m < 2:
                        v.wait_ge(q.e_glo, 2 * HC * n)
                    else:
                        v.wait_ge(q.e_lo, HC * n + (m - 1))
                    v.scalar_tensor_tensor(hf[m % 2], ps[2 * (m % 2) + 1][:, :], hs[:, 1, m:m + 1], sil[m % 2],
                                           ALU.mult, ALU.mult).then_inc(q.e_hf, 1)
                    v.wait_ge(q.e_o, BR * n)
                    v.wait_ge(q.e_hf, HC * n + (m + 1))
                    v.tensor_copy(hb[0][:, 0, m], hf[m % 2]).then_inc(q.e_hi, 1)
                for layer, ready in enumerate((q.e_g1, q.e_g2)):
                    for m in range(HC):
                        v.wait_ge(ready, HC * n + (m + 1))
                        v.tensor_tensor(hb[1 - layer][:, 1, m], hf[m % 2], hb[1 - layer][:, 0, m],
                                        ALU.subtract).then_inc(q.e_glo, 1)
                for r in range(BR):
                    v.wait_ge(q.e_o, BR * n + (r + 1))
                    v.wait_ge(e_out[r % 2], 8 * BR * n + 8 * (r - r % 2))
                    v.tensor_tensor(fo[r % 2][:, :], ps[6 + r % 2][:, 0:D], w3s[:, :], ALU.mult).then_inc(q.e_os, 1)
                    v.wait_ge(q.e_os, BR * n + (r + 1))
                    v.tensor_tensor(fo[r % 2][:, :], fo[r % 2][:, :], flat(xres[:, ds(n * BR + r, 1), :]),
                                    ALU.add).then_inc(q.e_or, 1)

        @block.tensor
        def _(pe):
            def product(to, pairs, start=True, fresh=True):
                last, k = None, 0
                for left, right in pairs:
                    for l, r in PASSES:
                        last = pe.matmul(to, left(l), right(r), start=start and k == 0,
                                         stop=k == len(pairs) * len(PASSES) - 1, skip_group_check=not fresh)
                        k += 1
                return last

            pe.wait_ge(q.maskbf, 1)
            pe.wait_ge(q.const_set, 3)
            for c in range(EC):
                last = pe.matmul(ps[6][0:ER, c:c + 1], maskbf[:, 1 + c * ER:1 + (c + 1) * ER], onesb[:, 0:1],
                                 start=True, stop=True)
            last.then_inc(q.cnt, 1)
            pe.wait_ge(q.act, 2)
            pe.wait_ge(q.consts_bf, 3)
            for c in range(EC):
                pe.matmul(ps[6][0:ER, 8 + c:9 + c], tri, actb[:, c:c + 1], start=True, stop=c == 0)
                for b in range(c):
                    pe.matmul(ps[6][0:ER, 8 + c:9 + c], onesb[0:ER, 0:ER], actb[:, b:b + 1], start=False, stop=b == c - 1)
            for c in range(EC):
                last = pe.matmul(ps[6][0:1, 16:17], onesb[0:ER, 0:1], actb[:, c:c + 1], start=c == 0, stop=c == EC - 1)
            last.then_inc(q.pos_ps, 1)
            pe.wait_ge(q.hot, EC)
            pe.wait_ge(q.pos_sb, 2)
            for k in range(2):
                for c in range(EC):
                    last = pe.matmul(ps[6 + k][0:1, 0:NT], code[:, k * EC + c:k * EC + c + 1], hot[:, c],
                                     start=c == 0, stop=c == EC - 1)
                last.then_inc(q.list_ps, 1)
            pe.wait_ge(q.work_in, 16 * 8)
            for j in range(S):
                for h in range(2):
                    last = pe.matmul(ps[j // 32][h * S:h * S + S, (j % 32) * AH:(j % 32) * AH + AH],
                                     buck[:, S - 1 - j:2 * S - 1 - j], emb, start=True, stop=True)
            last.then_inc(q.bias_ps, 1)
            pe.wait_ge(q.small_in, 16 * 8)
            pe.wait_ge(q.wstage_in, 16 * 5)
            pe.wait_ge(q.list_sb, 2)
            for h in range(2 * HP):
                for c in range(FC):
                    last = pe.matmul(ps[6][:, h:h + 1], st_qkv[:, c, D + h * P:D + (h + 1) * P], lnx[:, 1, c:c + 1],
                                     start=c == 0, stop=c == FC - 1)
            last.then_inc(q.bk_ps, 1)

            def rows_transpose(k):
                _, _, rh, rl, _ = rows[k]

                def tile(n, j):
                    pe.wait_ge(q.r_lo, n + (k * RT + 1))
                    for l, part in enumerate((rh, rl)):
                        for c in range(FC):
                            at = (l * FC + c) * P
                            last = pe.transpose(ps[j][:, :].bitcast(BF16)[:, at:at + P], part[:, j, c * P:(c + 1) * P],
                                                ident[:, :])
                    last.then_inc(q.r_t, 1)

                for j in range(2):
                    tile(j, j)
                with pe.Fori(2, RT - 1, 2) as n:
                    for j in range(2):
                        pe.wait_ge(q.r_e, n + (k * RT + j - 1))
                        tile(n + j, j)
                pe.wait_ge(q.r_e, (k + 1) * RT)

            pe.wait_ge(q.bias_sb, 4)
            rows_transpose(0)
            pe.wait_ge(q.split_lo, len(splits))
            with pe.Fori(0, RT - 1, 2) as n:
                for j in range(2):
                    if j == 0:
                        pe.wait_ge(q.a_ss, n)
                        pe.wait_ge(q.a_vlo, n)
                        pe.wait_ge(q.a_raw, n)
                    cols = ds((n + j) * P, P)
                    product(ps[2 * j][:, :], [(lambda l, c=c: lnT[:, l, c, cols], lambda r, c=c: wqkv[:, r, c, 0:2 * D])
                                              for c in range(FC)])
                    product(ps[2 * j + 1][:, 0:D], [(lambda l, c=c: lnT[:, l, c, cols],
                                                     lambda r, c=c: wqkv[:, r, c, 2 * D:3 * D])
                                                    for c in range(FC)]).then_inc(q.a_qkv, 1)

            def a_transpose(n):
                for kind in range(2):
                    for l, part in enumerate((qkhi, qklo)):
                        for h in range(HP):
                            last = pe.matmul(ps[4 + 2 * kind][:, (2 * l + h) * P:(2 * l + h + 1) * P],
                                             flat(part[:, ds(n, 1), kind * D + h * P:kind * D + (h + 1) * P]),
                                             ident[:, :], start=True, stop=True)
                last.then_inc(q.a_t, 1)

            def a_scores(n):
                pe.wait_ge(q.a_kt, n + 1)
                pe.wait_ge(q.a_qp, 2 * n + 2)
                pe.wait_ge(q.a_p, n)
                for b in range(2):
                    for h in range(HP):
                        last = product(ps[5][b * S:b * S + S, h * P:(h + 1) * P],
                                       [(lambda l: klt[:, 2 * l + h, b * S:b * S + S],
                                         lambda r: qpair[:, b, 2 * r + h, :])])
                last.then_inc(q.a_s, 1)

            pe.wait_ge(q.a_lo, 1)
            pe.wait_ge(q.bk_sb, 1)
            a_transpose(0)
            with pe.Fori(0, RT - 1) as n:
                pe.wait_ge(q.a_lo, n + 2)
                pe.wait_ge(q.a_kt, n + 1)
                pe.wait_ge(q.a_qp, 2 * n + 2)
                a_transpose(n + 1)
                a_scores(n)
            a_scores(RT - 1)

            pe.wait_ge(q.pos_sb, 3)
            count = pe.value_load(wn[0:1, 0:1], min_val=1, max_val=NT)

            def b_transpose(w1, h):
                pe.wait_ge(q.b_lo, w1)
                for l, part in enumerate((xch[h], xcl[h])):
                    for c in range(FC):
                        for i in range(G):
                            at = c * GT + i * P
                            last = pe.transpose(ps[l][:, :].bitcast(BF16)[:, at:at + P], part[:, i, c * P:(c + 1) * P],
                                                ident[:, :])
                last.then_inc(q.b_t, G)

            def b_keys(w1):
                pe.wait_ge(q.b_eh, w1)
                pe.wait_ge(q.b_el, w1)
                for h in range(HP):
                    last = product(ps[2 + h][:, :], [(lambda l, c=c: wkx[:, l, c, h * P:(h + 1) * P],
                                                      lambda r, c=c: xct[:, r, c, :]) for c in range(FC)])
                last.then_inc(q.b_k, G)

            def b_scores(w):
                pe.wait_ge(q.b_ksq, w + G)
                pe.wait_ge(q.b_acc, w)
                for i in range(G):
                    for h in range(HP):
                        last = pe.matmul(ps[4][:, XH * i:XH * i + XH], ksq[:, h, i * P:(i + 1) * P], headsum[:, h, :],
                                         start=h == 0, stop=h == HP - 1)
                last.then_inc(q.b_ss, G)
                pe.wait_ge(q.b_klo, w + G)
                pe.wait_ge(q.b_qld, 16 * w + 16 * G)
                for i in range(G):
                    for h in range(HP):
                        at = (i % 2) * D + h * P
                        last = product(ps[5 + i // 2][:, at:at + P],
                                       [(lambda l: kct[:, l, h, i * P:(i + 1) * P], lambda r: qc[:, i, 2 * r + h, :])])
                last.then_inc(q.b_s, G)

            def b_products(w, h):
                pe.wait_ge(q.b_ph, w + G)
                pe.wait_ge(q.b_pl, w + G)
                parts, probs = (xch[h], xcl[h]), (prh, prl)
                for i in range(G):
                    if i >= 2:
                        pe.wait_ge(q.b_acc, w + (i - 1))
                    to, sums = (ps[7], ps[4][:, D:2 * D]) if i % 2 == 0 else (ps[5], ps[6][:, 0:D])
                    for r in range(2):
                        pe.matmul(sums, onesb[:, :], probs[r][:, i], start=r == 0, stop=r == 1)
                    for c in range(FC):
                        last = product(to[:, c * D:(c + 1) * D], [(lambda l: parts[l][:, i, c * P:(c + 1) * P],
                                                                   lambda r: probs[r][:, i])])
                    last.then_inc(q.b_pv, 1)

            b_transpose(G, 0)
            b_keys(G)
            with pe.Fori(0, count, 2 * G) as w:
                for h in range(2):
                    b_scores(w + h * G)
                    b_transpose(w + (h + 2) * G, 1 - h)
                    b_keys(w + (h + 2) * G)
                    b_products(w + h * G, h)

            def c_sums(n, j):
                pe.wait_ge(c_ld[j], 24 * n + (48 - 24 * j))
                for r in range(2):
                    last = pe.matmul(ps[j][:, :], onesb[:, :], c_pb[j][:, r].rearrange("p b n -> p (b n)"),
                                     start=r == 0, stop=r == 1)
                last.then_inc(q.c_l, 1)

            def c_heads(n, j):
                pe.wait_ge(q.c_ul, 2 * n + 2)
                us = (c_uh[j], c_ul[j])
                for h2 in range(2):
                    for hp in range(HP):
                        h = 2 * hp + h2
                        head = slice(h * DH, h * DH + DH)
                        last = product(ps[2 + 2 * hp + j][h2 * DH:h2 * DH + DH, 0:P],
                                       [(lambda l, c=c: wvx[:, l, c, head], lambda r, c=c: us[r][:, c, :, head])
                                        for c in range(FC)] +
                                       [(lambda l: c_vl[j][:, l, head], lambda r: c_pb[j][:, r, :, head])])
                last.then_inc(q.c_ot, 1)

            def c_out(n, j):
                pe.wait_ge(q.c_ol, n + 1)
                parts = (c_oth[j], c_otl[j])
                for r in range(2):
                    pe.matmul(ps[6 + j][:, 0:D], onesb[0:1, :], bo[0:1, r, :], start=r == 0, stop=False)
                product(ps[6 + j][:, 0:D], [(lambda l, c=c: parts[l][:, c, :], lambda r, c=c: wo[:, r, c, :])
                                            for c in range(HP)], start=False).then_inc(q.c_o, 1)

            pe.wait_ge(q.bo_lo, 1)
            c_sums(0, 0)
            with pe.Fori(0, RT - 2, 2) as n:
                c_sums(n + 1, 1)
                c_heads(n, 0)
                c_out(n, 0)
                c_sums(n + 2, 0)
                c_heads(n + 1, 1)
                c_out(n + 1, 1)
            c_sums(RT - 1, 1)
            c_heads(RT - 2, 0)
            c_out(RT - 2, 0)
            c_heads(RT - 1, 1)
            c_out(RT - 1, 1)
            pe.wait_ge(q.c_x, RT)

            rows_transpose(1)

            def d_qk(n):
                for k in range(4):
                    for c4 in range(4):
                        m = 4 * k + c4
                        last = product(ps[k][:, c4 * P:(c4 + 1) * P],
                                       [(lambda l, c=c: wqk[:, l, c, m * P:(m + 1) * P],
                                         lambda r, c=c: rowT[:, r, c, ds(n * P, P)]) for c in range(FC)])
                    last.then_inc(q.d_qk, 1)

            def d_v(n):
                for k in range(2):
                    product(ps[4 + k][:, :], [(lambda l, c=c: rowT[:, l, c, ds(n * P, P)],
                                               lambda r, c=c: wva[:, r, c, k * 512:k * 512 + 512])
                                              for c in range(FC)]).then_inc(q.d_v, 1)

            def d_scores(n):
                pe.wait_ge(q.d_qlo, 4 * n + 4)
                pe.sem_inc(q.gate, 1)
                parts = (qkh, qkl)
                for hp in range(AP_):
                    for b in range(2):
                        for l, r in PASSES:
                            for h2 in range(2):
                                c = (hp + 4 * h2) % AP_
                                rows_, cols = slice(h2 * DH, h2 * DH + DH), slice(b * S, b * S + S)
                                last = pe.matmul(ps[6 + c // 4][rows_, (c % 4) * P + b * S:(c % 4) * P + b * S + S],
                                                 parts[l][rows_, c, cols], parts[r][rows_, AP_ + c, cols],
                                                 start=(l, r) == PASSES[0], stop=(l, r) == PASSES[-1])
                last.then_inc(q.d_s, 1)

            def d_pair(n, last_pair):
                pe.wait_ge(q.d_ahi, 2 * n)
                pe.wait_ge(q.d_alo, 2 * n)
                d_scores(n)
                if not last_pair:
                    pe.wait_ge(q.d_x, n)
                    d_qk(n + 1)
                pe.wait_ge(q.d_phi, n + 1)
                pe.wait_ge(q.d_plo, n + 1)
                pe.wait_ge(q.d_vlo, 2 * n + 2)
                for l, part in enumerate((sph, spl)):
                    for c in range(AP_):
                        last = pe.transpose(ps[4 + l][:, :].bitcast(BF16)[:, c * P:(c + 1) * P], part[:, c, :], ident[:, :])
                    last.then_inc(q.d_pt, 1)
                pe.wait_ge(q.d_peh, n + 1)
                pe.wait_ge(q.d_pel, n + 1)
                pe.sem_inc(q.gate, 1)
                values = (vh, vlo)
                for c in range(AP_):
                    for h2 in range(2):
                        head = (2 * c + h2) * DH
                        for l, r in PASSES:
                            for b in range(2):
                                rows_ = slice(b * S, b * S + S)
                                last = pe.matmul(ps[6 + b][h2 * DH:h2 * DH + DH, c * S:c * S + S],
                                                 values[l][rows_, head:head + DH], pT[rows_, r, c, h2 * S:h2 * S + S],
                                                 start=(l, r) == PASSES[0], stop=(l, r) == PASSES[-1])
                last.then_inc(q.d_pv, 1)
                pe.wait_ge(q.d_ahi, 2 * n + 2)
                pe.wait_ge(q.d_alo, 2 * n + 2)
                if not last_pair:
                    pe.wait_ge(q.d_qlo, 4 * n + 5)
                atts = (ath, atl)
                product(ps[0][:, 0:D], [(lambda l, c=c: atts[l][:, c, :], lambda r, c=c: woa[:, r, c, :])
                                        for c in range(AP_)]).then_inc(q.d_o, 1)
                if not last_pair:
                    d_v(n + 1)

            d_qk(0)
            d_v(0)
            with pe.Fori(0, RT - 1) as n:
                d_pair(n, False)
            d_pair(RT - 1, True)
            pe.wait_ge(q.d_x, RT)

            rows_transpose(2)
            pe.wait_ge(q.f_lo, NPIECE)
            with pe.Fori(0, NB) as n:
                for m in range(HC):
                    if m >= 2:
                        pe.wait_ge(q.e_hf, HC * n + (m - 1))
                    for k, w in enumerate((w1, w2)):
                        last = product(ps[2 * (m % 2) + k][:, :],
                                       [(lambda l, c=c: w[:, l, c, m * P:(m + 1) * P],
                                         lambda r, c=c: rowT[:, r, c, ds(n * BLK, BLK)]) for c in range(FC)])
                    last.then_inc(q.e_1, 1)
                for layer, (w, ready, done) in enumerate(((h1, q.e_g1, q.e_h1), (h2, q.e_g2, q.e_h2))):
                    for m in range(HC):
                        if m < 2:
                            pe.wait_ge(q.e_g2 if layer == 0 else q.e_g1, HC * n + HC * layer)
                        else:
                            pe.wait_ge(ready, HC * n + (m - 1))
                        k = 0
                        for c in range(HC):
                            if m == 0:
                                if layer == 0:
                                    pe.wait_ge(q.e_lo, HC * n + (c + 1))
                                else:
                                    pe.wait_ge(q.e_glo, 2 * HC * n + (c + 1))
                            for l, r in PASSES:
                                last = pe.matmul(ps[4 + m % 2][:, :], w[:, l, c, m * P:(m + 1) * P],
                                                 hb[layer][:, r, c], start=k == 0, stop=k == 3 * HC - 1)
                                k += 1
                        last.then_inc(done, 1)
                pe.wait_ge(q.e_glo, 2 * HC * n + 2 * HC)
                for r_ in range(BR):
                    pe.wait_ge(q.e_os, BR * n + max(r_ - 1, 0))
                    product(ps[6 + r_ % 2][:, 0:D],
                            [(lambda l, c=c: hb[0][:, l, c, r_ * P:(r_ + 1) * P], lambda r, c=c: w3[:, r, c, :])
                             for c in range(HC)]).then_inc(q.e_o, 1)


def rel_buckets():
    half, exact, far = NBUCK // 2, NBUCK // 4, 128
    table = np.zeros((NBUCK, P), np.float32)
    for m in range(2 * S - 1):
        rel = S - 1 - m
        dist = abs(rel)
        if dist >= exact:
            coeff = (half - exact) / np.log(far / exact)
            dist = min(half - 1, exact + int(np.log(np.float32(dist) / np.float32(exact)) * np.float32(coeff)))
        table[(half if rel > 0 else 0) + dist, m] = 1.0
    return table


def kernel(**inputs):
    import concourse.bacc as bacc
    from concourse.bass_utils import run_bass_kernel_spmd

    g = {k: np.asarray(v) for k, v in inputs.items()}
    x, mask = g["x"], g["mask_BxS2_bk0"]
    n = "L0_xattn_"
    f, a_ = "L0_ffn_", "L0_attn_"
    qkv = g[a_ + "qkv_w"]

    def chunks(w):
        wt = w.T
        per = PIECE // wt.shape[1]
        return wt.reshape(-1, per, P, wt.shape[1]).transpose(0, 2, 1, 3).reshape(-1, P, PIECE)

    padded = np.zeros((B, KT * P), np.bool_)
    padded[:, FRONT:] = mask
    cols = padded.reshape(B * KT, P).T
    tiles = np.arange(NT).reshape(EC, ER).T
    arrays = {
        "x": x.reshape(ROWS, D),
        "ctx": np.concatenate([np.zeros((P + FRONT, D), np.float32), g["ctx_1024"].reshape(B * SC, D)]),
        "mask": np.concatenate([np.zeros((P, 1), np.bool_), cols], axis=1),
        "iota": np.broadcast_to(np.arange(NT, dtype=np.float32), (ER, NT)),
        "code": np.concatenate([tiles // KT, tiles % KT + 1], axis=1).astype(np.float32),
        "tri": np.triu(np.ones((ER, ER), np.float32), 1),
        "ident": np.eye(P, dtype=np.float32),
        "buck": rel_buckets(),
        "emb": g[a_ + "emb_weight"],
        "headsum": (np.arange(HP * P).reshape(HP, P).T[:, :, None] // DH == np.arange(XH)).astype(np.float32),
        "ln_l_g": g[n + "ln_l_g"], "ln_l_b": g[n + "ln_l_b"],
        "q_gamma": g[n + "q_gamma"], "k_gamma": g[n + "k_gamma"],
        "lnx": np.stack([g[n + "ln_x_g"].reshape(FC, P).T, g[n + "ln_x_b"].reshape(FC, P).T], axis=1),
        "b_out": g[n + "b_out"].reshape(1, D),
        "w3_s": g[f + "w3_s"],
        "hs": np.stack([g[f + k].reshape(HC, P).T for k in ("w1_s", "w2_s", "h1_s", "h2_s")], axis=1),
        "wqkv": np.concatenate([g[n + "W_q"], g[n + "W_kv"]], axis=1),
        "wo": g[n + "W_out"],
        "wqk": qkv[0:2 * AH * DH].T, "wva": qkv[2 * AH * DH:].T, "woa": g[a_ + "o_w"].T,
        "wff": np.concatenate([chunks(g[f + k]) for k in ("w1_w", "w2_w", "h1_w", "h2_w", "w3_w")]),
    }
    arrays = {k: np.ascontiguousarray(v) for k, v in arrays.items()}

    nc = bacc.Bacc("TRN2", target_bir_lowering=False, num_devices=1)
    t = {k: nc.dram_tensor("in_" + k, v.shape, mybir.dt.from_np(v.dtype), kind="ExternalInput").ap()
         for k, v in arrays.items()}
    out = nc.dram_tensor("out", [ROWS, D], F32, kind="ExternalOutput").ap()
    build(nc, t, out)
    result = run_bass_kernel_spmd(nc, [{"in_" + k: v for k, v in arrays.items()}], core_ids=[0])
    return result.results[0]["out"].reshape(B, S, D)
```

```python
from collections import namedtuple
from contextlib import ExitStack

import numpy as np

import concourse.bass as bass
from concourse import mybir

F32 = mybir.dt.float32
BF16 = mybir.dt.bfloat16
I32 = mybir.dt.int32
U8 = mybir.dt.uint8
ALU = mybir.AluOpType
ACT = mybir.ActivationFunctionType
AX = mybir.AxisListType
ds = bass.ds

P = 128
B, S, D = 32, 64, 256
SC = 1601
FC = D // P
ROWS = B * S
RT = ROWS // P
XH, DH = 4, 64
HP = XH // 2
KT = -(-SC // P)
FRONT = KT * P - SC
NT = B * KT
EC = 4
ER = NT // EC
G = 4
GT = G * P
LW = NT + 4 * G
BB = 5
assert B <= 1 << BB and NT % G == 0 and G * BB < 24
AH = 16
AP_ = AH // 2
HID = 1024
HC = HID // P
BLK = 512
NB = ROWS // BLK
BR = BLK // P
NBUCK = 32
ATW = FC * 3 * AH * DH + AP_ * D
ATP = ATW // RT
FFW = 2 * FC * HID + 2 * HC * HID + HC * D
PIECE = FFW // RT
LN_EPS = 1e-5
RMS_FLOOR = 1e-8 ** 2
MASKED = -1e30
SCALE = DH ** -0.5
QK_BANKS = (0, 1, 6, 7)
PASSES = ((0, 0), (0, 1), (1, 0))


def flat(ap):
    return ap.rearrange("p a b -> p (a b)")


def build(nc, t, out):
    ctx = ExitStack()
    with ctx:
        def sb(name, shape, dt):
            return ctx.enter_context(nc.sbuf_tensor(name, shape, dt))

        xres = sb("xres", [P, RT, D], F32)
        wkx = sb("wkx", [P, 2, FC, D], BF16)
        wvx = sb("wvx", [P, 2, FC, D], BF16)
        wo = sb("wo", [P, 2, FC, D], BF16)
        wat = sb("wat", [P, 2, ATW], BF16)
        wqk = wat[:, :, 0:FC * 2 * AH * DH].rearrange("p l (c n) -> p l c n", c=FC)
        wva = wat[:, :, FC * 2 * AH * DH:FC * 3 * AH * DH].rearrange("p l (c n) -> p l c n", c=FC)
        woa = wat[:, :, FC * 3 * AH * DH:ATW].rearrange("p l (c n) -> p l c n", c=AP_)
        bias = sb("bias", [P, AP_, S], F32)
        ident = sb("ident", [P, P], BF16)
        onesb = sb("onesb", [P, P], BF16)
        headsum = sb("headsum", [P, HP, XH], F32)
        neghalf = sb("neghalf", [P, RT * 8], F32)
        maskb = sb("maskb", [P, NT + 1], F32)
        wl = sb("wl", [1, 4, LW], I32)
        wn = sb("wn", [1, 1], I32)
        lnx = sb("lnx", [P, 2, FC], F32)
        bk = sb("bk", [P, HP], F32)
        bv = sb("bv", [P, D], F32)
        bof = sb("bof", [1, D], F32)
        bo = sb("bo", [1, 2, D], BF16)
        w3s = sb("w3s", [P, D], F32)
        hs = sb("hs", [P, 4, HC], F32)
        stats = sb("stats", [P, RT, 6], F32)
        mv = sb("mv", [P, RT, 2], F32)
        var_eps = sb("ve", [P, RT], F32)
        rstd = sb("rstd", [P, RT], F32)
        sm1 = sb("sm1", [P, AH], F32)
        sm2 = sb("sm2", [P, AH], F32)
        sm3 = sb("sm3", [P, AH], F32)
        lowmax = sb("lowmax", [P, RT], F32)
        lowany = sb("lowany", [P, 1], BF16)
        lown = sb("lown", [1, 1], I32)
        mt = sb("mt", [P, 3, RT], F32)
        big = sb("big", [P, B * 3 * D], F32)
        tmp = sb("tmp", [P, 40 * 256], F32)

        ps = [ctx.enter_context(nc.psum_tensor(f"ps{i}", [P, 512], F32)) for i in range(8)]

        def carve(area, at, words, dt=F32):
            assert at + words <= area.shape[1], (at, words)
            piece = area[:, at:at + words]
            return piece if dt == F32 else piece.bitcast(dt)

        mask8 = carve(tmp, 0, 105, U8)[:, 0:NT + 1]
        maskbf = carve(tmp, 108, 209, BF16)[:, 0:NT + 1]
        iota = carve(tmp, 320, NT)[0:ER, :]
        codef = carve(tmp, 736, 8)[0:ER, :]
        code = carve(tmp, 744, 4, BF16)[0:ER, :]
        trif = carve(tmp, 752, 128)[0:ER, 0:ER]
        tri = carve(tmp, 880, 64, BF16)[0:ER, 0:ER]
        actf = carve(tmp, 944, EC)[0:ER, :]
        actb = carve(tmp, 948, EC // 2, BF16)[0:ER, :]
        pos = carve(tmp, 952, EC)[0:ER, :]
        hot = carve(tmp, 960, EC * NT // 2, BF16)[0:ER, :].rearrange("p (c n) -> p c n", c=EC)
        buck = carve(tmp, 1792, 128)[0:NBUCK, :]
        emb = carve(tmp, 1920, AH)[0:NBUCK, :]
        identf = carve(tmp, 1936, 128)
        tile1 = carve(tmp, 2064, NT)[0:1, :]
        row128 = carve(tmp, 2480, NT)[0:1, :]
        lnx_b = carve(tmp, 2896, FC * P).rearrange("p (c n) -> p c n", c=FC)
        wkg = carve(tmp, 3152, 1024).rearrange("p (c n) -> p c n", c=FC)
        xn1 = carve(big, 0, 4096).rearrange("p (t n) -> p t n", t=RT)
        st_qkv = carve(big, 4096, 1536).rearrange("p (c n) -> p c n", c=FC)
        head_of_acc = carve(big, 0, 4096 + 1536)
        wqkv = carve(tmp, 4992, 1536, BF16).rearrange("p (l c n) -> p l c n", l=2, c=FC)
        lng = carve(tmp, 6528, 256)
        lnb = carve(tmp, 6784, 256)
        gq = carve(tmp, 7040, 64)
        gk = carve(tmp, 7104, 64)
        a_rn = carve(tmp, 7168, 512).rearrange("p (t n) -> p t n", t=2)
        a_rh = carve(tmp, 7680, 256, BF16).rearrange("p (t n) -> p t n", t=2)
        a_rl = carve(tmp, 7936, 256, BF16).rearrange("p (t n) -> p t n", t=2)
        sq2 = [carve(tmp, 8192 + 512 * i, 512) for i in range(2)]
        ss = carve(tmp, 9216, 128)
        rr = carve(tmp, 9344, 128)
        a_at = B * 2 * D + B * HP + 4 * P + RT * XH

        def by_turns(at, words, dt=F32):
            return [carve(big, a_at + at + words * i, words, dt) for i in range(2)]

        qkraw = by_turns(0, 512)
        qkhi, qklo = by_turns(1024, 256, BF16), by_turns(1536, 256, BF16)
        qpair = [x.rearrange("p (b k n) -> p b k n", b=2, k=4) for x in by_turns(2048, 512, BF16)]
        klt = [x.rearrange("p (k n) -> p k n", k=4) for x in by_turns(3072, 256, BF16)]
        pl_a = by_turns(3584, 256)
        pls = [x.rearrange("p (l n) -> p l n", l=2) for x in by_turns(4096, 256, BF16)]
        vst = [x.rearrange("p (l n) -> p l n", l=2) for x in by_turns(4608, 256, BF16)]
        aT = [x.rearrange("p (l c n) -> p l c n", l=2, c=FC) for x in by_turns(5120, 256, BF16)]
        st_wo = carve(big, a_at + 5632, 512).rearrange("p (c n) -> p c n", c=FC)
        st_at = by_turns(6144, ATP)

        acc = carve(big, 0, B * 2 * D).rearrange("p (b n) -> p b n", b=B)
        accs = carve(big, B * 2 * D, B * HP).rearrange("p (b k) -> p b k", b=B)
        acc_all = carve(big, 0, B * 2 * D + B * HP)
        sel = carve(big, B * 2 * D + B * HP, 4 * P).rearrange("p (h b n) -> p h b n", h=2, b=2)
        csum = carve(big, B * 2 * D + B * HP + 4 * P, RT * XH).rearrange("p (t h) -> p t h", t=RT)
        xt = [carve(tmp, 1024 * i, 1024).rearrange("p (i n) -> p i n", i=G) for i in range(2)]
        xch = [carve(tmp, 2048 + 512 * i, 512, BF16).rearrange("p (i n) -> p i n", i=G) for i in range(2)]
        xcl = [carve(tmp, 3072 + 512 * i, 512, BF16).rearrange("p (i n) -> p i n", i=G) for i in range(2)]
        xct = carve(tmp, 4096, 1024, BF16).rearrange("p (l c n) -> p l c n", l=2, c=FC)
        ksq = carve(tmp, 5120, 1024).rearrange("p (c n) -> p c n", c=HP)
        kct = carve(tmp, 6144, 1024, BF16).rearrange("p (l c n) -> p l c n", l=2, c=HP)
        pr = carve(tmp, 7168, 1024).rearrange("p (i n) -> p i n", i=G)
        prh = carve(tmp, 8192, 512, BF16).rearrange("p (i n) -> p i n", i=G)
        prl = carve(tmp, 8704, 512, BF16).rearrange("p (i n) -> p i n", i=G)
        qc = carve(tmp, 9216, 1024, BF16).rearrange("p (i k n) -> p i k n", i=G, k=4)
        cst, cmv, cve, crs = stats[:, 0:G, :], mv[:, 0:G, :], var_eps[:, 0:G], rstd[:, 0:G]

        def c_set(at, fields):
            got = {}
            for name, words, dt in fields:
                got[name] = carve(tmp, at, words, dt)
                at += words
            return got

        c_pb = [carve(tmp, 7168 + 512 * j, 512, BF16).rearrange("p (l h b n) -> p l h b n", l=2, h=XH, b=2) for j in range(2)]
        c_fields = (("vl", 256, BF16), ("uh", 512, BF16), ("ul", 512, BF16), ("ub", 256, F32),
                    ("ot", 256, F32), ("oth", 128, BF16), ("otl", 128, BF16), ("otT", 256, BF16))
        cs = [c_set(2560 * j, c_fields) for j in range(2)]
        c_ot, c_ub, c_oth, c_otl = ([c[k] for c in cs] for k in ("ot", "ub", "oth", "otl"))
        c_vl = [c["vl"].rearrange("p (l n) -> p l n", l=2) for c in cs]
        c_uh, c_ul = ([c[k].rearrange("p (c h b n) -> p c h b n", c=FC, h=XH, b=2) for c in cs] for k in ("uh", "ul"))
        c_otT = [c["otT"].rearrange("p (l c n) -> p l c n", l=2, c=HP) for c in cs]

        wff = carve(big, 0, FFW, BF16).rearrange("p (l n) -> p l n", l=2)
        wst = carve(big, FFW, PIECE)
        fo = [carve(big, FFW + i * D, D) for i in range(2)]

        def ff_weights(first, chunks, width):
            return wff[:, :, first:first + chunks * width].rearrange("p l (c n) -> p l c n", n=width)

        w1, w2 = ff_weights(0, FC, HID), ff_weights(FC * HID, FC, HID)
        h1, h2 = ff_weights(2 * FC * HID, HC, HID), ff_weights((2 * FC + HC) * HID, HC, HID)
        w3 = ff_weights(2 * (FC + HC) * HID, HC, D)
        rowT = carve(tmp, 0, 4096, BF16).rearrange("p (l c n) -> p l c n", l=2, c=FC)
        qkh = carve(tmp, 4096, 1024, BF16).rearrange("p (c n) -> p c n", n=P)
        qkl = carve(tmp, 5120, 1024, BF16).rearrange("p (c n) -> p c n", n=P)
        vh = [carve(tmp, 6144, 512, BF16), wkx[:, :, :, :].rearrange("p l c n -> p (l c n)")]
        vlo = [carve(tmp, 6656, 512, BF16), wvx[:, :, :, :].rearrange("p l c n -> p (l c n)")]
        sc = carve(tmp, 7168, 1024).rearrange("p (k n) -> p k n", n=S)
        sph = carve(tmp, 8192, 512, BF16).rearrange("p (c n) -> p c n", n=P)
        spl = carve(tmp, 8704, 512, BF16).rearrange("p (c n) -> p c n", n=P)
        ath, atl = sph, spl
        pT = carve(tmp, 9216, 1024, BF16).rearrange("p (l c n) -> p l c n", l=2, n=P)
        d_rn = carve(tmp, 7168, 512).rearrange("p (t n) -> p t n", t=2)
        d_rh = carve(tmp, 7680, 256, BF16).rearrange("p (t n) -> p t n", t=2)
        d_rl = carve(tmp, 7936, 256, BF16).rearrange("p (t n) -> p t n", t=2)
        hb = [carve(tmp, 4096, 4096, BF16).rearrange("p (l c n) -> p l c n", l=2, c=HC),
              wat[:, :, 0:HC * BLK].rearrange("p l (c n) -> p l c n", n=BLK)]
        hf = [carve(tmp, 8192 + 512 * i, 512) for i in range(2)]
        sil = [carve(tmp, 9216 + 512 * i, 512) for i in range(2)]
        e_rn = carve(tmp, 8192, 512).rearrange("p (t n) -> p t n", t=2)
        e_rh = carve(tmp, 8704, 256, BF16).rearrange("p (t n) -> p t n", t=2)
        e_rl = carve(tmp, 8960, 256, BF16).rearrange("p (t n) -> p t n", t=2)

        def acc_heads(n, c):
            return acc[:, ds(n * 2, 2), c * D:(c + 1) * D].rearrange("p b (h i) -> p h b i", h=XH)

        q_scr = nc.dram_tensor("q_scr", [B, P, 4 * P], BF16, kind="Internal").ap()
        p_scr = nc.dram_tensor("p_scr", [RT, P, 2 * D], BF16, kind="Internal").ap()
        v_scr = nc.dram_tensor("v_scr", [RT, P, 2 * D], BF16, kind="Internal").ap()

        splits = [(st_qkv, wqkv), (wkg[:, :, 0:D], wkx), (wkg[:, :, D:2 * D], wvx), (st_wo, wo)]
        rows = [None, (d_rn, d_rh, d_rl), (e_rn, e_rh, e_rl)]
        RUN, LAST = range(6, RT - 2, 2), RT + 5
        AHEAD = RT

        def runs(k, behind):
            return not isinstance(k, int) or 0 <= k - behind < RT

        names = """x_in work_in small_in wstage_in const_set gains
                maskbf act ps_set pos_sb hot list_sb consts_bf
                bias_ps bias_sb bk_ps bk_sb wkg split_hi split_lo w_ld0 w_ld1 w_hi w_lo bo_hi bo_lo
                m_halves m_terms n_halves n_terms x1_n r_st r_ve r_rs r_n r_g r_hi r_lo r_t r_e
                a_qkv a_raw a_sq a_ss a_vhi a_vlo a_ms a_rr a_qkn a_gq a_hi a_lo a_t a_qp a_kt a_s a_p a_phi a_plo
                a_qst a_pst a_vst
                acc_zero b_ld0 b_ld1 b_qld b_st b_ve b_rs b_n b_hi b_lo b_lo2 b_t b_tl b_eh b_el b_k b_ksq b_klo
                b_ss b_ms b_rr b_s b_sn b_p b_ph b_pl b_pv b_acc
                c_ld0 c_ld1 c_zero c_sel c_sums c_csum c_uh c_ul c_ub c_ot c_step c_on c_oh c_ol c_t c_te c_o c_x
                f_ld f_hi f_lo f_max f_any f_count f_known
                d_qk d_qhi d_qlo d_v d_vhi d_vlo d_s d_sb d_stat d_sub d_ex d_pn d_phi d_plo
                gate d_pt d_peh d_pel d_pv d_ahi d_alo d_o d_x
                e_1 e_sil e_hf e_h1 e_g1 e_h2 e_g2 e_hi e_lo e_glo e_o e_os e_or e_out0 e_out1""".split()
        q = namedtuple("Semaphores", names)(*(ctx.enter_context(nc.semaphore(name)) for name in names))

        w_ld, b_ld, c_ld, e_out = (q.w_ld0, q.w_ld1), (q.b_ld0, q.b_ld1), (q.c_ld0, q.c_ld1), (q.e_out0, q.e_out1)

        block = ctx.enter_context(nc.Block())

        @block.sync
        def _(sp):
            for to, name in ((mask8, "mask"), (iota, "iota"), (codef, "code"), (trif, "tri"),
                             (identf, "ident"), (buck, "buck"), (emb, "emb"), (headsum[:, :, :], "headsum")):
                sp.dma_start(to, t[name]).then_inc(q.work_in, 16)
            sp.dma_start(xres[:, :, :], t["x"].rearrange("(t p) n -> p t n", p=P)).then_inc(q.x_in, 16)
            for to, name in ((st_qkv, "wqkv"), (st_wo, "wo")):
                sp.dma_start(to, t[name].rearrange("(c p) n -> p c n", p=P)).then_inc(q.wstage_in, 16)
            for to, name in ((lng, "ln_l_g"), (lnb, "ln_l_b"), (gq, "q_gamma"), (gk, "k_gamma"), (w3s[:, :], "w3_s")):
                sp.dma_start(to, t[name].partition_broadcast(P)).then_inc(q.small_in, 16)
            for to, name in ((lnx[:, :, :], "lnx"), (bof[:, :], "b_out"), (hs[:, :, :], "hs")):
                sp.dma_start(to, t[name]).then_inc(q.small_in, 16)

            def load_w(k, p):
                sp.dma_start(st_at[p], t["wat"][ds(k, 1)].rearrange("t p n -> p (t n)")).then_inc(w_ld[p], 16)

            def a_step(k, p):
                if runs(k, -1):
                    if not isinstance(k, int) or k > 0:
                        sp.wait_ge(q.w_lo, k)
                    load_w(k + 1, 1 - p)
                if runs(k, 4):
                    sp.wait_ge(q.a_qp, 2 * k - 6)
                    sp.wait_ge(q.a_qst, 16 * k - 64)
                    sp.dma_start(q_scr[ds(k * 2 - 8, 2)].rearrange("b p n -> p b n"),
                                 qpair[p].rearrange("p b k n -> p b (k n)")).then_inc(q.a_qst, 16)
                if runs(k, 5):
                    sp.wait_ge(q.a_plo, k - 4)
                    sp.sem_inc(q.gate, 1)
                    sp.wait_ge(q.a_pst, 16 * k - 80)
                    sp.dma_start(p_scr[ds(k - 5, 1)].rearrange("t p n -> p (t n)"),
                                 pls[1 - p].rearrange("p l n -> p (l n)")).then_inc(q.a_pst, 16)
                if runs(k, 1):
                    sp.wait_ge(q.a_vlo, k)
                    sp.sem_inc(q.gate, 1)
                    sp.wait_ge(q.a_vst, 16 * k - 16)
                    sp.dma_start(v_scr[ds(k - 1, 1)].rearrange("t p n -> p (t n)"),
                                 vst[1 - p].rearrange("p l n -> p (l n)")).then_inc(q.a_vst, 16)

            def load_x(w, h, split):
                rows_at = []
                for i in range(G):
                    rows_at.append(sp.value_load(wl[0:1, 2, ds(w + i, 1)], min_val=0, max_val=(B - 1) * SC + KT * P))
                if split is not None:
                    sp.wait_ge(q.b_lo, split)
                    sp.wait_ge(q.b_lo2, split)
                for i in range(G):
                    sp.dma_start(xt[h][:, i, :], t["ctx"][ds(rows_at[i], P), :]).then_inc(b_ld[h], 16)

            load_w(0, 0)
            sp.wait_ge(q.list_sb, 4 + G)
            sp.wait_ge(q.bias_ps, 1)
            sp.wait_ge(q.bk_ps, 1)
            sp.wait_ge(q.split_lo, len(splits))
            sp.dma_start(sel, t["sel"]).then_inc(q.c_sel, 16)
            load_x(0, 0, None)
            load_x(G, 1, None)
            for k in range(0, RUN.start):
                a_step(k, k % 2)
            with sp.Fori(RUN.start, RUN.stop - 1, 2) as k:
                for p in range(2):
                    a_step(k + p, p)
            for k in range(RUN.stop, LAST):
                a_step(k, k % 2)
            sp.wait_ge(q.a_qst, 16 * RT)
            sp.wait_ge(q.a_pst, 16 * RT)
            sp.wait_ge(q.a_vst, 16 * RT)
            count = sp.value_load(wn[0:1, 0:1], min_val=1, max_val=NT)

            def load_q(w):
                for i in range(G):
                    bi = sp.value_load(wl[0:1, 0, ds(w + i, 1)], min_val=0, max_val=B - 1)
                    sp.dma_start(qc[:, i].rearrange("p k n -> p (k n)"),
                                 q_scr[ds(bi, 1)].rearrange("b p n -> p (b n)")).then_inc(q.b_qld, 16)

            with sp.Fori(0, count, 2 * G) as w:
                for h in range(2):
                    sp.wait_ge(q.b_s, w + h * G)
                    load_q(w + h * G)
                    load_x(w + (h + 2) * G, h, w + (h + 1) * G)
            sp.wait_ge(q.b_lo, count + 2 * G)
            sp.wait_ge(q.b_lo2, count + 2 * G)
            sp.sem_inc(q.gate, 1)
            sp.wait_ge(q.b_klo, count + G)
            sp.wait_ge(q.b_ksq, count + G)
            sp.wait_ge(q.b_acc, count)

            def load_c(n, j):
                for b in range(2):
                    r = slice(b * S, b * S + S)
                    sp.dma_start(c_pb[j][r, :, :, b, :].rearrange("p l h n -> p (l h) n"),
                                 p_scr[ds(n, 1), r].rearrange("t p (k n) -> p (t k) n", n=S)).then_inc(c_ld[j], 16)
                sp.dma_start(c_vl[j].rearrange("p l n -> p (l n)"),
                             v_scr[ds(n, 1)].rearrange("t p n -> p (t n)")).then_inc(c_ld[j], 16)

            sp.wait_ge(q.c_zero, 4)
            for j in range(2):
                load_c(j, j)
            with sp.Fori(2, RT - 1, 2) as n:
                for j in range(2):
                    sp.wait_ge(q.c_ot, n + (j - 1))
                    load_c(n + j, j)
            sp.wait_ge(q.c_x, RT)
            with sp.Fori(0, RT) as k:
                sp.wait_ge(q.f_lo, k)
                sp.dma_start(wst, t["wff"][ds(k, 1)].rearrange("t p n -> p (t n)")).then_inc(q.f_ld, 16)
            with sp.Fori(0, RT - 1, 2) as n:
                for j in range(2):
                    sp.wait_ge(q.e_or, n + j + 1)
                    sp.dma_start(out[ds((n + j) * P, P), :], fo[j][:, :]).then_inc(e_out[j], 16)
            for j in range(2):
                sp.wait_ge(e_out[j], 16 * RT // 2)

        @block.gpsimd
        def _(po):
            po.memset(neghalf[:, :], -0.5).then_inc(q.const_set, 1)
            po.memset(onesb[:, :], 1.0).then_inc(q.const_set, 1)
            po.memset(wl[:, :, :], 0).then_inc(q.const_set, 1)
            for j in range(2):
                po.memset(qpair[j].rearrange("p b k n -> p (b k n)"), 0.0).then_inc(q.const_set, 1)
            po.memset(big[:, 4096 + 1536:B * 2 * D + B * HP], 0.0).then_inc(q.acc_zero, 1)
            po.wait_ge(q.small_in, 16 * 8)
            po.tensor_tensor(gq, gq, gk, ALU.mult).then_inc(q.gains, 1)
            po.wait_ge(q.gains, 1)
            po.tensor_scalar(gq, gq, SCALE, None, ALU.mult).then_inc(q.gains, 1)
            po.wait_ge(q.const_set, 5)

            def rows_norm(k):
                po.wait_ge(q.r_ve, k + 2)
                po.tensor_tensor(rstd[:, :], var_eps[:, :], neghalf[:, 0:RT], ALU.pow).then_inc(q.r_rs, 1)

            def rows_low(k):
                rn, rh, rl = rows[k]
                with po.Fori(0, RT - 1, 2) as n:
                    for j in range(2):
                        po.wait_ge(q.r_hi, n + (k * RT + j + 1))
                        po.tensor_tensor(rl[:, j], rn[:, j], rh[:, j], ALU.subtract).then_inc(q.r_lo, 1)

            rows_norm(-1)
            rows_norm(0)

            def a_step(k, p):
                if runs(k, 2):
                    po.wait_ge(q.a_ms, k - 1)
                    po.tensor_tensor(rr[:, ds(k * 8 - 16, 8)], ss[:, ds(k * 8 - 16, 8)], neghalf[:, 0:8],
                                     ALU.pow).then_inc(q.a_rr, 1)
                if runs(k, 5):
                    po.wait_ge(q.a_phi, k - 4)
                    po.tensor_tensor(pls[1 - p][:, 1], pl_a[1 - p], pls[1 - p][:, 0], ALU.subtract).then_inc(q.a_plo, 1)
                if runs(k, 2):
                    row = qkraw[p][:, 0:D].rearrange("p (h d) -> p h d", h=XH)
                    po.wait_ge(q.a_qkn, k - 1)
                    po.tensor_tensor(row, row, gq.rearrange("p (h d) -> p h d", h=1).broadcast_to([P, XH, DH]),
                                     ALU.mult).then_inc(q.a_gq, 1)
                if runs(k, -2):
                    po.wait_ge(q.r_hi, k + 3)
                    if not isinstance(k, int) or k >= 0:
                        po.wait_ge(q.r_t, k + 1)
                    po.tensor_tensor(a_rl[:, p], a_rn[:, p], a_rh[:, p], ALU.subtract).then_inc(q.r_lo, 1)
                if runs(k, 2):
                    po.wait_ge(q.a_hi, k - 1)
                    po.tensor_tensor(qklo[p], qkraw[p], qkhi[p], ALU.subtract).then_inc(q.a_lo, 1)

            for k in range(-2, RUN.start):
                a_step(k, k % 2)
            with po.Fori(RUN.start, RUN.stop - 1, 2) as k:
                for p in range(2):
                    a_step(k + p, p)
            def b_scale(w1):
                po.wait_ge(q.b_ms, w1)
                po.tensor_tensor(sm2[:, :], sm1[:, :], neghalf[:, 0:AH], ALU.pow).then_inc(q.b_rr, G)

            def b_deviations(w1):
                po.wait_ge(q.b_ve, w1)
                po.tensor_tensor(crs, cve, neghalf[:, 0:G], ALU.pow).then_inc(q.b_rs, G)

            for k in range(RUN.stop, LAST):
                a_step(k, k % 2)
                if k in (AHEAD, AHEAD + 1):
                    b_deviations((k - AHEAD + 1) * G)
            po.wait_ge(q.r_n, RT)
            po.wait_ge(q.bk_ps, 1)
            po.wait_ge(q.split_lo, len(splits))
            po.memset(head_of_acc, 0.0).then_inc(q.acc_zero, 1)
            po.wait_ge(q.pos_sb, 3)
            count = po.value_load(wn[0:1, 0:1], min_val=1, max_val=NT)

            def b_low(w1, h):
                half = slice(0, G // 2)
                po.wait_ge(q.b_hi, w1 - G // 2)
                po.tensor_tensor(flat(xcl[h][:, half]), flat(xt[h][:, half]), flat(xch[h][:, half]),
                                 ALU.subtract).then_inc(q.b_lo, G)

            b_low(G, 0)
            b_low(2 * G, 1)
            b_scale(G)
            with po.Fori(0, count, 2 * G) as w:
                for h in range(2):
                    b_deviations(w + (h + 3) * G)
                    b_low(w + (h + 3) * G, h)
                    b_scale(w + (h + 2) * G)
            po.wait_ge(q.c_csum, 1)
            with po.Fori(0, RT - 1, 2) as n:
                for j in range(2):
                    po.wait_ge(q.c_uh, n + (j + 1))
                    for c in range(FC):
                        po.tensor_tensor(c_ul[j][:, c], acc_heads(n + j, c), c_uh[j][:, c], ALU.subtract).then_inc(q.c_ul, 1)
                    if j == 0:
                        po.wait_ge(q.c_on, n)
                    po.tensor_tensor(c_ub[j].rearrange("p (h d) -> p h d", h=XH),
                                     bv[:, :].rearrange("p (h d) -> p h d", h=XH),
                                     csum[:, ds(n + j, 1), :].rearrange("p t (h o) -> p (t h) o", o=1)
                                     .broadcast_to([P, XH, DH]), ALU.mult).then_inc(q.c_ub, 1)
            rows_norm(1)
            rows_low(1)

            with po.Fori(0, RT) as n:
                po.wait_ge(q.f_hi, n + 1)
                po.tensor_tensor(wff[:, 1, ds(n * PIECE, PIECE)], wst, wff[:, 0, ds(n * PIECE, PIECE)],
                                 ALU.subtract).then_inc(q.f_lo, 1)
            rows_norm(2)
            rows_low(2)
            with po.Fori(0, NB) as n:
                for m in range(HC):
                    po.wait_ge(q.e_hi, HC * n + (m + 1))
                    po.tensor_tensor(hb[0][:, 1, m], hf[m % 2], hb[0][:, 0, m], ALU.subtract).then_inc(q.e_lo, 1)

        @block.scalar
        def _(act):
            act.wait_ge(q.wstage_in, 16 * 2)
            for k, (full, parts) in enumerate(splits):
                if k == 1:
                    act.wait_ge(q.wkg, FC)
                act.activation(parts[:, 0], full, ACT.Copy).then_inc(q.split_hi, 1)
            act.wait_ge(q.small_in, 16 * 8)
            act.activation(bo[:, 0, :], bof[:, :], ACT.Copy).then_inc(q.bo_hi, 1)

            def rows_high(k):
                rn, rh, _ = rows[k]

                def store(n, j):
                    act.wait_ge(q.r_t, n + (k * RT + 1))
                    act.activation(rowT[:, :, :, ds(n * P, P)],
                                   ps[j][:, :].bitcast(BF16)[:, 0:4 * P].rearrange("p (l c n) -> p l c n", l=2, c=FC),
                                   ACT.Copy).then_inc(q.r_e, 1)

                with act.Fori(0, RT - 1, 2) as n:
                    for j in range(2):
                        act.wait_ge(q.r_n, n + (k * RT + j + 1))
                        act.activation(rh[:, j], rn[:, j], ACT.Copy).then_inc(q.r_hi, 1)
                    for j in range(2):
                        store(n + j, j)

            def a_step(k, p):
                loop = not isinstance(k, int)
                if runs(k, 5):
                    act.wait_ge(q.a_s, k - 4)
                    if loop or k > 6:
                        act.wait_ge(q.a_plo, k - 6)
                    act.activation(pl_a[1 - p], ps[5][:, 0:D], ACT.Exp).then_inc(q.a_p, 1)
                if runs(k, 4):
                    act.wait_ge(q.a_t, k - 3)
                    if loop or k > 5:
                        act.wait_ge(q.a_s, k - 5)
                    act.activation(klt[p], ps[6][:, :].rearrange("p (k n) -> p k n", k=4), ACT.Copy).then_inc(q.a_kt, 1)
                if runs(k, 0):
                    act.wait_ge(q.r_t, k + 1)
                    if loop or k > 1:
                        act.wait_ge(q.a_qkv, k - 1)
                    act.activation(aT[p].rearrange("p l c n -> p (l c n)"), ps[7][:, :].bitcast(BF16)[:, 0:4 * P],
                                   ACT.Copy).then_inc(q.r_e, 1)
                if runs(k, 0):
                    act.wait_ge(w_ld[p], 8 * k + (16 - 8 * p))
                    act.activation(wat[:, 0, ds(k * ATP, ATP)], st_at[p], ACT.Copy).then_inc(q.w_hi, 1)
                if runs(k, 5):
                    act.wait_ge(q.a_p, k - 4)
                    if loop or k > 6:
                        act.wait_ge(q.a_pst, 16 * k - 96)
                    act.activation(pls[1 - p][:, 0], pl_a[1 - p], ACT.Copy).then_inc(q.a_phi, 1)
                if runs(k, -2):
                    act.wait_ge(q.r_n, k + 3)
                    if loop or k >= 0:
                        act.wait_ge(q.r_t, k + 1)
                    act.activation(a_rh[:, p], a_rn[:, p], ACT.Copy).then_inc(q.r_hi, 1)
                if runs(k, 2):
                    act.wait_ge(q.a_gq, k - 1)
                    if loop or k > 3:
                        act.wait_ge(q.a_t, k - 3)
                    act.activation(qkhi[p], qkraw[p], ACT.Copy).then_inc(q.a_hi, 1)
                if runs(k, 1):
                    act.wait_ge(q.a_qkv, k)
                    if loop or k > 2:
                        act.wait_ge(q.a_ss, k - 2)
                    act.activation(sq2[1 - p], ps[2 * (1 - p)][:, :], ACT.Square).then_inc(q.a_sq, 1)
                    if loop or k > 2:
                        act.wait_ge(q.a_vst, 16 * k - 32)
                    act.activation(vst[1 - p][:, 0], ps[2 * (1 - p) + 1][:, 0:D], ACT.Copy).then_inc(q.a_vhi, 1)

            for k in range(-2, RUN.start):
                a_step(k, k % 2)
            with act.Fori(RUN.start, RUN.stop - 1, 2) as k:
                for p in range(2):
                    a_step(k + p, p)
            def b_high(w1, h, k, used):
                half = slice(k * G // 2, (k + 1) * G // 2)
                act.wait_ge(q.b_n, w1 - (1 - k) * G // 2)
                if used:
                    act.wait_ge(q.b_pv, w1 - 2 * G - (1 - k) * G // 2)
                act.activation(flat(xch[h][:, half]), flat(xt[h][:, half]), ACT.Copy).then_inc(q.b_hi, G // 2)

            for k in range(RUN.stop, LAST):
                a_step(k, k % 2)
                if k == AHEAD + 1:
                    b_high(G, 0, 0, False)
                    b_high(G, 0, 1, False)
                if k == AHEAD + 2:
                    b_high(2 * G, 1, 0, False)
            act.wait_ge(q.pos_sb, 3)
            act.wait_ge(q.list_sb, 4 + G)
            act.wait_ge(q.consts_bf, 1)
            act.wait_ge(q.bk_sb, 2)
            count = act.value_load(wn[0:1, 0:1], min_val=1, max_val=NT)

            def b_tokens(w1):
                act.wait_ge(q.b_t, w1)
                act.activation(xct[:, 0].rearrange("p c n -> p (c n)"), ps[0][:, :].bitcast(BF16),
                               ACT.Copy).then_inc(q.b_eh, G)

            def b_keys(w1):
                for c in range(HP):
                    act.wait_ge(q.b_k, w1 - (HP - 1 - c) * G // HP)
                    act.activation(kct[:, 0, c], ps[2 + c][:, :], ACT.Identity, bias=bk[:, c:c + 1])
                    act.activation(ksq[:, c], ps[2 + c][:, :], ACT.Square,
                                   bias=bk[:, c:c + 1]).then_inc(q.b_ksq, G // HP)

            def b_exp(w, columns):
                act.wait_ge(q.b_sn, w + G)
                for i in range(G):
                    act.activation(pr[:, i], pr[:, i], ACT.Exp, bias=maskb[:, ds(columns[i], 1)]).then_inc(q.b_p, 1)
                act.wait_ge(q.b_p, w + G)
                act.wait_ge(q.b_pv, w)
                act.activation(flat(prh), flat(pr), ACT.Copy).then_inc(q.b_ph, G)

            b_tokens(G)
            b_keys(G)
            with act.Fori(0, count, 2 * G) as w:
                for h in range(2):
                    at = w + h * G
                    columns = [act.value_load(wl[0:1, 1, ds(at + i, 1)], min_val=0, max_val=NT) for i in range(G)]
                    b_high(at + 2 * G, 1 - h, 1, True)
                    b_tokens(at + 2 * G)
                    b_exp(at, columns)
                    act.wait_ge(q.b_ss, at + G)
                    act.wait_ge(q.b_s, at + G)
                    b_keys(at + 2 * G)
                    b_high(at + 3 * G, h, 0, True)
            b_high(count + 2 * G, 1, 1, True)

            act.wait_ge(q.b_acc, count)
            act.wait_ge(q.b_lo, count + 2 * G)
            act.wait_ge(q.b_lo2, count + 2 * G)
            act.wait_ge(q.b_t, count + G)

            def c_high(n, j, first=False):
                if not first:
                    act.wait_ge(q.c_ot, n - 1)
                for c in range(FC):
                    last = act.activation(c_uh[j][:, c], acc_heads(n, c), ACT.Copy)
                last.then_inc(q.c_uh, 1)

            def c_out_high(n, j):
                act.wait_ge(q.c_on, n + 1)
                act.activation(c_oth[j], c_ot[j], ACT.Copy).then_inc(q.c_oh, 1)

            def c_transposed(n, j):
                act.wait_ge(q.c_t, n + 1)
                act.activation(c_otT[j].rearrange("p l c n -> p (l c n)"), ps[2 + j][:, :].bitcast(BF16)[:, 0:4 * P],
                               ACT.Copy).then_inc(q.c_te, 1)

            c_high(0, 0, first=True)
            c_high(1, 1, first=True)
            c_out_high(0, 0)
            with act.Fori(1, RT - 2, 2) as n:
                for j in range(2):
                    c_high(n + (j + 1), j)
                    c_transposed(n + (j - 1), j)
                    c_out_high(n + j, 1 - j)
            c_transposed(RT - 2, 0)
            c_out_high(RT - 1, 1)
            c_transposed(RT - 1, 1)
            rows_high(1)

            def d_qk(n, c):
                act.wait_ge(q.d_qk, 4 * n + (c + 1))
                act.activation(qkh[:, 4 * c:4 * c + 4].rearrange("p c n -> p (c n)"), ps[QK_BANKS[c]][:, :], ACT.Copy,
                               scale=SCALE if c < 2 else 1.0).then_inc(q.d_qhi, 1)

            def d_v(n, j):
                for k in range(2):
                    act.wait_ge(q.d_v, 2 * n + (k + 1))
                    act.activation(vh[j][:, k * 512:k * 512 + 512], ps[k][:, :], ACT.Copy).then_inc(q.d_vhi, 1)

            def d_tile(n, j, last=False):
                act.wait_ge(q.d_sub, n + 1)
                act.activation(flat(sc), flat(sc), ACT.Exp).then_inc(q.d_ex, 1)
                if not last:
                    act.wait_ge(q.d_s, n + 1)
                    d_qk(n + 1, 0)
                    d_qk(n + 1, 1)
                act.wait_ge(q.d_pn, n + 1)
                act.wait_ge(q.d_o, n)
                act.activation(flat(sph), flat(sc), ACT.Copy).then_inc(q.d_phi, 1)
                if not last:
                    d_qk(n + 1, 2)
                    d_qk(n + 1, 3)
                act.wait_ge(q.d_pt, 2 * n + 1)
                act.activation(pT[:, 0].rearrange("p c n -> p (c n)"), ps[4][:, :].bitcast(BF16),
                               ACT.Copy).then_inc(q.d_peh, 1)
                act.wait_ge(q.f_ld, 16 * n + 16)
                act.activation(wff[:, 0, ds(n * PIECE, PIECE)], wst, ACT.Copy).then_inc(q.f_hi, 1)
                if not last:
                    d_v(n + 1, 1 - j)
                act.wait_ge(q.d_pv, n + 1)
                for k in range(2):
                    act.activation(ath[:, :, k * S:k * S + S], ps[6 + k][:, :].rearrange("p (c n) -> p c n", c=AP_),
                                   ACT.Copy).then_inc(q.d_ahi, 1)

            for c in range(4):
                d_qk(0, c)
            d_v(0, 0)
            d_tile(0, 0)
            with act.Fori(1, RT - 2, 2) as n:
                for j in range(2):
                    d_tile(n + j, 1 - j)
            d_tile(RT - 1, 1, last=True)
            rows_high(2)
            with act.Fori(0, NB) as n:
                for m in range(HC):
                    act.wait_ge(q.e_1, HC * n + (m + 1))
                    if m < 2:
                        act.wait_ge(q.e_hf, HC * n)
                    else:
                        act.wait_ge(q.e_hf, HC * n + (m - 1))
                    act.activation(sil[m % 2], ps[2 * (m % 2)][:, :], ACT.Silu,
                                   scale=hs[:, 0, m:m + 1]).then_inc(q.e_sil, 1)
                for layer, (ready, done) in enumerate(((q.e_h1, q.e_g1), (q.e_h2, q.e_g2))):
                    for m in range(HC):
                        act.wait_ge(ready, HC * n + (m + 1))
                        act.activation(hb[1 - layer][:, 0, m], ps[4 + m % 2][:, :], ACT.Gelu,
                                       scale=hs[:, 2 + layer, m:m + 1])
                        if m < 2 and layer == 0:
                            act.wait_ge(q.e_lo, HC * n + HC)
                        else:
                            act.wait_ge(q.e_glo, 2 * HC * n + (HC * layer + m - 1))
                        act.activation(hf[m % 2], ps[4 + m % 2][:, :], ACT.Gelu,
                                       scale=hs[:, 2 + layer, m:m + 1]).then_inc(done, 1)

        @block.vector
        def _(v):
            rows_moments, group_moments = (q.m_halves, q.m_terms), (q.n_halves, q.n_terms)

            def moments(st, to, var, sems, k, done, step=1):
                halves, terms = sems
                n = st.shape[1]
                dif, dev, spread = mt[:, 0, 0:n], mt[:, 1, 0:n], mt[:, 2, 0:n]
                v.tensor_tensor(to[:, :, 0], st[:, :, 1], st[:, :, 4], ALU.add).then_inc(halves, step)
                v.tensor_tensor(dif, st[:, :, 1], st[:, :, 4], ALU.subtract).then_inc(halves, step)
                v.tensor_tensor(dev, st[:, :, 2], st[:, :, 5], ALU.add).then_inc(halves, step)
                v.wait_ge(halves, 3 * k)
                v.tensor_scalar(to[:, :, 0], to[:, :, 0], 0.5, None, ALU.mult).then_inc(terms, step)
                v.scalar_tensor_tensor(spread, dif, 0.25, dif, ALU.mult, ALU.mult).then_inc(terms, step)
                v.tensor_scalar(dev, dev, 1.0 / D, LN_EPS, ALU.mult, ALU.add).then_inc(terms, step)
                v.wait_ge(terms, 3 * k)
                v.tensor_tensor(var, dev, spread, ALU.add).then_inc(done, step)

            v.wait_ge(q.work_in, 16 * 8)
            v.tensor_copy(maskbf, mask8).then_inc(q.maskbf, 1)
            v.wait_ge(q.maskbf, 1)
            v.tensor_scalar(maskb[:, :], maskbf, 1.0, -MASKED, ALU.subtract, ALU.mult).then_inc(q.consts_bf, 1)
            v.tensor_copy(tri, trif).then_inc(q.consts_bf, 1)
            v.tensor_copy(code, codef).then_inc(q.consts_bf, 1)
            v.tensor_copy(ident[:, :], identf).then_inc(q.consts_bf, 1)
            v.wait_ge(q.ps_set, 1)
            v.tensor_scalar(actf, ps[6][0:ER, 0:EC], 1.0, None, ALU.min).then_inc(q.act, 1)
            v.tensor_scalar(actb, ps[6][0:ER, 0:EC], 1.0, None, ALU.min).then_inc(q.act, 1)
            v.wait_ge(q.ps_set, 2)
            v.tensor_copy(pos, ps[6][0:ER, 8:8 + EC]).then_inc(q.pos_sb, 1)
            v.tensor_scalar(wn[:, :], ps[6][0:1, 16:17], 1.0, 2.0 * G - 1, ALU.max, ALU.add).then_inc(q.pos_sb, 1)
            v.wait_ge(q.pos_sb, 2)
            v.tensor_scalar(wn[:, :], wn[:, :], -2 * G, None, ALU.bitwise_and).then_inc(q.pos_sb, 1)
            for c in range(EC):
                v.tensor_scalar(hot[:, c], iota, pos[:, c:c + 1], actf[:, c:c + 1],
                                ALU.is_equal, ALU.mult).then_inc(q.hot, 1)
            v.wait_ge(q.const_set, 5)
            v.wait_ge(q.ps_set, 4)
            batch = ps[6][0:1, 0:NT]
            v.tensor_copy(wl[:, 0, 0:NT], batch).then_inc(q.list_sb, 1)
            v.tensor_copy(tile1, ps[7][0:1, 0:NT]).then_inc(q.list_sb, 1)
            v.tensor_scalar(row128, ps[7][0:1, 0:NT], float(P), None, ALU.mult).then_inc(q.list_sb, 1)
            v.wait_ge(q.list_sb, 3)
            v.scalar_tensor_tensor(wl[:, 1, 0:NT], batch, float(KT), tile1, ALU.mult, ALU.add).then_inc(q.list_sb, 1)
            v.scalar_tensor_tensor(wl[:, 2, 0:NT], batch, float(SC), row128, ALU.mult, ALU.add).then_inc(q.list_sb, 1)
            groups = wl[:, :, 0:NT].rearrange("o k (g i) -> o k g i", i=G)
            for i in range(G - 1, 0, -1):
                high = groups[:, 0, :, G - 1] if i == G - 1 else groups[:, 3, :, 0]
                v.scalar_tensor_tensor(groups[:, 3, :, 0], high, float(1 << BB), groups[:, 0, :, i - 1],
                                       ALU.mult, ALU.add).then_inc(q.list_sb, 1)
                v.wait_ge(q.list_sb, 5 + G - i)
            v.wait_ge(q.x_in, 16)

            def rows_stats(k, src):
                with v.Fori(0, RT - 3, 4) as n:
                    for j in range(4):
                        v.bn_stats(flat(stats[:, ds(n + j, 1), :]), flat(src[:, ds(n + j, 1), :])).then_inc(q.r_st, 1)
                v.wait_ge(q.r_st, (k + 2) * RT)
                moments(stats, mv, var_eps[:, :], rows_moments, k + 2, q.r_ve)

            rows_stats(-1, xres)
            v.wait_ge(q.small_in, 16 * 8)
            v.wait_ge(q.wstage_in, 16 * 2)
            for c in range(FC):
                v.tensor_scalar(wkg[:, c], st_qkv[:, c, D:3 * D], lnx[:, 0, c:c + 1], None, ALU.mult).then_inc(q.wkg, 1)
            for c in range(FC):
                v.tensor_scalar(lnx_b[:, c], onesb[:, :], lnx[:, 1, c:c + 1], None, ALU.mult).then_inc(q.wkg, 1)
            v.wait_ge(q.r_rs, 1)
            with v.Fori(0, RT - 3, 4) as n:
                for j in range(4):
                    v.tensor_scalar(flat(xn1[:, ds(n + j, 1), :]), flat(xres[:, ds(n + j, 1), :]), mv[:, ds(n + j, 1), 0],
                                    rstd[:, ds(n + j, 1)], ALU.subtract, ALU.mult).then_inc(q.x1_n, 1)
                v.wait_ge(q.x1_n, n + 4)
                for j in range(4):
                    v.bn_stats(flat(stats[:, ds(n + j, 1), :]), flat(xn1[:, ds(n + j, 1), :])).then_inc(q.r_st, 1)
            v.wait_ge(q.r_st, 2 * RT)
            moments(stats, mv, var_eps[:, :], rows_moments, 2, q.r_ve)
            for k, (full, parts) in enumerate(splits):
                v.wait_ge(q.split_hi, k + 1)
                v.tensor_tensor(parts[:, 1], full, parts[:, 0], ALU.subtract).then_inc(q.split_lo, 1)
            v.wait_ge(q.bo_hi, 1)
            v.tensor_tensor(bo[:, 1, :], bof[:, :], bo[:, 0, :], ALU.subtract).then_inc(q.bo_lo, 1)
            v.wait_ge(q.bk_ps, 1)
            v.tensor_copy(bk[:, :], ps[6][:, 0:HP]).then_inc(q.bk_sb, 1)
            v.tensor_copy(bv[:, :], ps[7][:, 0:D]).then_inc(q.bk_sb, 1)
            v.wait_ge(q.bias_ps, 1)
            for k in range(2):
                for h in range(2):
                    r = slice(h * S, h * S + S)
                    v.tensor_copy(bias[r, :, k * 32:k * 32 + 32],
                                  ps[k][r, :].rearrange("p (j c h) -> p c h j", c=AP_, h=2)[:, :, h, :]
                                  ).then_inc(q.bias_sb, 1)

            def a_step(k, p):
                loop = not isinstance(k, int)
                if runs(k, 4):
                    v.wait_ge(q.a_t, k - 3)
                    if loop or k > 5:
                        v.wait_ge(q.a_qst, 16 * k - 80)
                        v.wait_ge(q.a_s, k - 5)
                    for h in range(2):
                        r = slice(h * S, h * S + S)
                        v.tensor_copy(qpair[p][r, :, :, h * S:h * S + S],
                                      ps[4][r, :].rearrange("p (k b n) -> p b k n", k=4, b=2)).then_inc(q.a_qp, 1)
                if runs(k, -2):
                    n = k + 2
                    if loop or k >= 0:
                        v.wait_ge(q.r_lo, k + 1)
                    v.scalar_tensor_tensor(a_rn[:, p], flat(xn1[:, ds(n, 1), :]), mv[:, ds(n, 1), 0], lng,
                                           ALU.subtract, ALU.mult).then_inc(q.r_g, 1)
                    v.wait_ge(q.r_g, k + 3)
                    v.scalar_tensor_tensor(a_rn[:, p], a_rn[:, p], rstd[:, ds(n, 1)], lnb,
                                           ALU.mult, ALU.add).then_inc(q.r_n, 1)
                if runs(k, 2):
                    row = qkraw[p].rearrange("p (h d) -> p h d", d=DH)
                    v.wait_ge(q.a_rr, k - 1)
                    v.tensor_tensor(row, row, rr[:, ds(k * 8 - 16, 8)].rearrange("p (h o) -> p h o", o=1)
                                    .broadcast_to([P, 8, DH]), ALU.mult).then_inc(q.a_qkn, 1)
                if runs(k, 0):
                    v.wait_ge(q.w_hi, k + 1)
                    v.tensor_tensor(wat[:, 1, ds(k * ATP, ATP)], st_at[p], wat[:, 0, ds(k * ATP, ATP)],
                                    ALU.subtract).then_inc(q.w_lo, 1)
                if runs(k, 1):
                    j = 1 - p
                    v.wait_ge(q.a_sq, k)
                    if loop or k > 2:
                        v.wait_ge(q.a_lo, k - 2)
                    v.tensor_copy(qkraw[j], ps[2 * j][:, :]).then_inc(q.a_raw, 1)
                    v.tensor_reduce(ss[:, ds(k * 8 - 8, 8)], sq2[j].rearrange("p (h d) -> p h d", d=DH),
                                    AX.X, ALU.add).then_inc(q.a_ss, 1)
                    v.wait_ge(q.a_vhi, k)
                    v.tensor_tensor(vst[j][:, 1], ps[2 * j + 1][:, 0:D], vst[j][:, 0], ALU.subtract).then_inc(q.a_vlo, 1)
                    v.wait_ge(q.a_ss, k)
                    v.tensor_scalar(ss[:, ds(k * 8 - 8, 8)], ss[:, ds(k * 8 - 8, 8)], 1.0 / DH, RMS_FLOOR,
                                    ALU.mult, ALU.max).then_inc(q.a_ms, 1)

            v.wait_ge(q.r_rs, 2)
            for k in range(-2, RUN.start):
                a_step(k, k % 2)
            with v.Fori(RUN.start, RUN.stop - 1, 2) as k:
                for p in range(2):
                    a_step(k + p, p)
            def b_moments(w1, h):
                v.wait_ge(b_ld[h], 8 * w1 + (1 - h) * 8 * G)
                for i in range(G):
                    v.bn_stats(cst[:, i], xt[h][:, i]).then_inc(q.b_st, 1)
                v.wait_ge(q.b_st, w1)
                moments(cst, cmv, cve, group_moments, w1, q.b_ve, G)

            def b_norm(w1, h):
                v.wait_ge(q.b_rs, w1)
                for i in range(G):
                    v.tensor_scalar(xt[h][:, i], xt[h][:, i], cmv[:, i, 0:1], crs[:, i:i + 1],
                                    ALU.subtract, ALU.mult).then_inc(q.b_n, 1)

            for k in range(RUN.stop, LAST):
                a_step(k, k % 2)
                if k in (AHEAD + 1, AHEAD + 2):
                    b_norm((k - AHEAD) * G, k - AHEAD - 1)
                if k in (AHEAD, AHEAD + 1):
                    b_moments((k - AHEAD + 1) * G, k - AHEAD)

            def rows_norm(k):
                rn, _, _ = rows[k]
                rows_stats(k, xres)
                v.wait_ge(q.r_rs, k + 2)
                for j in range(2):
                    v.tensor_scalar(rn[:, j], xres[:, j], mv[:, j, 0:1], rstd[:, j:j + 1],
                                    ALU.subtract, ALU.mult).then_inc(q.r_n, 1)
                with v.Fori(2, RT - 1, 2) as n:
                    for j in range(2):
                        v.wait_ge(q.r_lo, n + (k * RT + j - 1))
                        v.tensor_scalar(rn[:, j], flat(xres[:, ds(n + j, 1), :]), mv[:, ds(n + j, 1), 0],
                                        rstd[:, ds(n + j, 1)], ALU.subtract, ALU.mult).then_inc(q.r_n, 1)

            count = v.value_load(wn[0:1, 0:1], min_val=1, max_val=NT)

            def b_tokens(w1):
                v.wait_ge(q.b_tl, w1)
                v.tensor_copy(xct[:, 1].rearrange("p c n -> p (c n)"), ps[1][:, :].bitcast(BF16)).then_inc(q.b_el, G)

            def b_keys(w1, c):
                v.wait_ge(q.b_ksq, w1 - G // HP * (HP - 1 - c))
                v.scalar_tensor_tensor(kct[:, 1, c], ps[2 + c][:, :], bk[:, c:c + 1], kct[:, 0, c],
                                       ALU.add, ALU.subtract).then_inc(q.b_klo, G // HP)

            def b_mean_squares(w1):
                v.wait_ge(q.b_ss, w1)
                v.tensor_scalar(sm1[:, :], ps[6][:, 0:AH], 1.0 / DH, RMS_FLOOR, ALU.mult, ALU.max).then_inc(q.b_ms, G)

            def b_scores(w1):
                v.wait_ge(q.b_rr, w1)
                for k in range(2):
                    v.wait_ge(q.b_s, w1 - (1 - k) * G // 2)
                    v.tensor_tensor(pr[:, 2 * k:2 * k + 2].rearrange("p i (h n) -> p (i h) n", n=S),
                                    ps[5 + k][:, :].rearrange("p (k n) -> p k n", n=S),
                                    sm2[:, 8 * k:8 * k + 8].rearrange("p (k o) -> p k o", o=1).broadcast_to([P, 8, S]),
                                    ALU.mult).then_inc(q.b_sn, G // 2)

            def b_low_second(w1, h):
                half = slice(G // 2, G)
                v.wait_ge(q.b_hi, w1)
                v.tensor_tensor(flat(xcl[h][:, half]), flat(xt[h][:, half]), flat(xch[h][:, half]),
                                ALU.subtract).then_inc(q.b_lo2, G)

            def b_low(w):
                v.wait_ge(q.b_ph, w + G)
                v.tensor_tensor(flat(prl), flat(pr), flat(prh), ALU.subtract).then_inc(q.b_pl, G)

            def b_sum(w, i, batch):
                v.wait_ge(q.b_pv, w + (i + 1))
                v.wait_ge(q.b_acc, w + i)
                sums, ones = acc[:, ds(batch, 1), :], accs[:, ds(batch, 1), :]
                v.tensor_tensor(flat(sums), flat(sums), ps[7 if i % 2 == 0 else 0][:, :], ALU.add)
                v.tensor_tensor(flat(ones), flat(ones), ps[4 if i % 2 == 0 else 1][:, 0:HP], ALU.add).then_inc(q.b_acc, 1)

            v.wait_ge(q.acc_zero, 2)
            b_low_second(G, 0)
            b_tokens(G)
            for c in range(HP):
                b_keys(G, c)
            b_mean_squares(G)
            b_low_second(2 * G, 1)
            with v.Fori(0, count, 2 * G) as w:
                for h in range(2):
                    at = w + h * G
                    b_scores(at + G)
                    packed = v.value_load(wl[0:1, 3, ds(at, 1)], min_val=0, max_val=(1 << BB * G) - 1)
                    batches = [v.snap((packed >> BB * i) & (B - 1)) for i in range(G)]
                    b_tokens(at + 2 * G)
                    b_moments(at + 3 * G, h)
                    b_low(at)
                    b_norm(at + 3 * G, h)
                    b_keys(at + 2 * G, 0)
                    b_sum(at, 0, batches[0])
                    b_keys(at + 2 * G, 1)
                    b_sum(at, 1, batches[1])
                    b_mean_squares(at + 2 * G)
                    for i in range(2, G):
                        b_sum(at, i, batches[i])
                    b_low_second(at + 3 * G, h)
            v.wait_ge(q.b_acc, count)

            for j in range(2):
                for b in range(2):
                    v.memset(c_pb[j][b * S:b * S + S, :, :, 1 - b, :].rearrange("p l h n -> p (l h) n"), 0.0
                             ).then_inc(q.c_zero, 1)
            v.wait_ge(q.c_sums, 1)
            v.tensor_copy(csum.rearrange("p t (k h) -> p h t k", h=2),
                          ps[6][:, 0:RT * XH].rearrange("p (h t k) -> p h t k", h=2, t=RT)).then_inc(q.c_csum, 1)

            def c_normalise(n, j):
                v.wait_ge(q.c_ot, n + 1)
                v.tensor_tensor(sm1[:, 0:XH], ps[j][:, D:D + XH], flat(csum[:, ds(n, 1), :]), ALU.add).then_inc(q.c_step, 1)
                v.wait_ge(q.c_ub, n + 1)
                v.tensor_tensor(c_ot[j], ps[j][:, 0:D], c_ub[j], ALU.add).then_inc(q.c_step, 1)
                v.wait_ge(q.c_step, 3 * n + 2)
                v.reciprocal(sm2[:, 0:XH], sm1[:, 0:XH]).then_inc(q.c_step, 1)
                v.wait_ge(q.c_step, 3 * n + 3)
                heads_ = c_ot[j].rearrange("p (h d) -> p h d", h=XH)
                v.tensor_tensor(heads_, heads_, sm2[:, 0:XH].rearrange("p (h o) -> p h o", o=1)
                                .broadcast_to([P, XH, DH]), ALU.mult).then_inc(q.c_on, 1)

            def c_low(n, j):
                v.wait_ge(q.c_oh, n + 1)
                v.tensor_tensor(c_otl[j], c_ot[j], c_oth[j], ALU.subtract).then_inc(q.c_ol, 1)

            def c_residual(n, j):
                v.wait_ge(q.c_o, n + 1)
                v.tensor_tensor(flat(xres[:, ds(n, 1), :]), flat(xres[:, ds(n, 1), :]), ps[4 + j][:, 0:D],
                                ALU.add).then_inc(q.c_x, 1)

            for j in range(2):
                c_normalise(j, j)
                c_low(j, j)
            with v.Fori(2, RT - 1, 2) as n:
                for j in range(2):
                    c_normalise(n + j, j)
                    c_residual(n + (j - 2), j)
                    c_low(n + j, j)
            for j in range(2):
                c_residual(RT - 2 + j, j)
            v.wait_ge(q.c_x, RT)

            rows_norm(1)

            def d_qk(n, c):
                v.wait_ge(q.d_qhi, 4 * n + (c + 1))
                v.scalar_tensor_tensor(qkl[:, 4 * c:4 * c + 4].rearrange("p c n -> p (c n)"), ps[QK_BANKS[c]][:, :],
                                       SCALE if c < 2 else 1.0,
                                       qkh[:, 4 * c:4 * c + 4].rearrange("p c n -> p (c n)"),
                                       ALU.mult, ALU.subtract).then_inc(q.d_qlo, 1)

            def d_v(n, j):
                for k in range(2):
                    v.wait_ge(q.d_vhi, 2 * n + (k + 1))
                    v.tensor_tensor(vlo[j][:, k * 512:k * 512 + 512], ps[k][:, :], vh[j][:, k * 512:k * 512 + 512],
                                    ALU.subtract).then_inc(q.d_vlo, 1)

            def d_out(n):
                v.wait_ge(q.d_o, n + 1)
                v.tensor_tensor(flat(xres[:, ds(n, 1), :]), flat(xres[:, ds(n, 1), :]), ps[4][:, 0:D],
                                ALU.add).then_inc(q.d_x, 1)

            def d_low_max(n):
                v.wait_ge(q.f_lo, n + 1)
                v.tensor_reduce(lowmax[:, ds(n, 1)], wff[:, 1, ds(n * PIECE, PIECE)], AX.X, ALU.max,
                                apply_absolute_value=True).then_inc(q.f_max, 1)

            def heads(values):
                return values[:, :].rearrange("p (k o) -> p k o", o=1).broadcast_to([P, AH, S])

            def d_tile(n, j, first=False, last=False):
                v.wait_ge(q.d_s, n + 1)
                for k in range(2):
                    v.tensor_tensor(sc[:, 8 * k:8 * k + 8].rearrange("p (c b) n -> p c b n", b=2),
                                    ps[2 + k][:, :].rearrange("p (c b n) -> p c b n", c=4, b=2),
                                    bias[:, 4 * k:4 * k + 4, :].rearrange("p c (o n) -> p c o n", o=1)
                                    .broadcast_to([P, 4, 2, S]), ALU.add).then_inc(q.d_sb, 1)
                v.wait_ge(q.d_sb, 2 * n + 2)
                v.tensor_reduce(sm1[:, :], sc, AX.X, ALU.max).then_inc(q.d_stat, 1)
                v.wait_ge(q.d_stat, 3 * n + 1)
                v.tensor_tensor(sc, sc, heads(sm1), ALU.subtract).then_inc(q.d_sub, 1)
                if not first:
                    d_out(n - 1)
                v.wait_ge(q.d_ex, n + 1)
                v.tensor_reduce(sm2[:, :], sc, AX.X, ALU.add).then_inc(q.d_stat, 1)
                v.wait_ge(q.d_stat, 3 * n + 2)
                v.reciprocal(sm3[:, :], sm2[:, :]).then_inc(q.d_stat, 1)
                v.wait_ge(q.d_stat, 3 * n + 3)
                v.tensor_tensor(sc, sc, heads(sm3), ALU.mult).then_inc(q.d_pn, 1)
                if not last:
                    d_qk(n + 1, 0)
                    d_qk(n + 1, 1)
                v.wait_ge(q.d_phi, n + 1)
                v.tensor_tensor(spl.rearrange("p c n -> p (c n)"), flat(sc), sph.rearrange("p c n -> p (c n)"),
                                ALU.subtract).then_inc(q.d_plo, 1)
                if not last:
                    d_qk(n + 1, 2)
                    d_qk(n + 1, 3)
                v.wait_ge(q.d_pt, 2 * n + 2)
                v.tensor_copy(pT[:, 1].rearrange("p c n -> p (c n)"), ps[5][:, :].bitcast(BF16)).then_inc(q.d_pel, 1)
                if not first:
                    d_low_max(n - 1)
                if not last:
                    d_v(n + 1, 1 - j)
                for k in range(2):
                    v.wait_ge(q.d_ahi, 2 * n + (k + 1))
                    v.tensor_tensor(atl[:, :, k * S:k * S + S], ps[6 + k][:, :].rearrange("p (c n) -> p c n", c=AP_),
                                    ath[:, :, k * S:k * S + S], ALU.subtract).then_inc(q.d_alo, 1)

            for c in range(4):
                d_qk(0, c)
            d_v(0, 0)
            d_tile(0, 0, first=True)
            with v.Fori(1, RT - 2, 2) as n:
                for j in range(2):
                    d_tile(n + j, 1 - j)
            d_tile(RT - 1, 1, last=True)
            d_out(RT - 1)
            v.wait_ge(q.d_x, RT)

            rows_norm(2)
            d_low_max(RT - 1)
            v.wait_ge(q.f_max, RT)
            v.tensor_reduce(sm1[:, 0:1], lowmax[:, :], AX.X, ALU.max).then_inc(q.f_max, 1)
            v.wait_ge(q.f_max, RT + 1)
            v.tensor_scalar(lowany[:, :], sm1[:, 0:1], 0.0, None, ALU.is_gt).then_inc(q.f_any, 1)
            v.wait_ge(q.f_count, 1)
            v.tensor_copy(lown[:, :], ps[4][0:1, 0:1]).then_inc(q.f_known, 1)
            with v.Fori(0, NB) as n:
                for m in range(HC):
                    v.wait_ge(q.e_sil, HC * n + (m + 1))
                    if m < 2:
                        v.wait_ge(q.e_glo, 2 * HC * n)
                    else:
                        v.wait_ge(q.e_lo, HC * n + (m - 1))
                    v.scalar_tensor_tensor(hf[m % 2], ps[2 * (m % 2) + 1][:, :], hs[:, 1, m:m + 1], sil[m % 2],
                                           ALU.mult, ALU.mult).then_inc(q.e_hf, 1)
                    v.wait_ge(q.e_o, BR * n)
                    v.wait_ge(q.e_hf, HC * n + (m + 1))
                    v.tensor_copy(hb[0][:, 0, m], hf[m % 2]).then_inc(q.e_hi, 1)
                for layer, ready in enumerate((q.e_g1, q.e_g2)):
                    for m in range(HC):
                        v.wait_ge(ready, HC * n + (m + 1))
                        v.tensor_tensor(hb[1 - layer][:, 1, m], hf[m % 2], hb[1 - layer][:, 0, m],
                                        ALU.subtract).then_inc(q.e_glo, 1)
                for r in range(BR):
                    v.wait_ge(q.e_o, BR * n + (r + 1))
                    v.wait_ge(e_out[r % 2], 8 * BR * n + 8 * (r - r % 2))
                    v.tensor_tensor(fo[r % 2][:, :], ps[6 + r % 2][:, 0:D], w3s[:, :], ALU.mult).then_inc(q.e_os, 1)
                    v.wait_ge(q.e_os, BR * n + (r + 1))
                    v.tensor_tensor(fo[r % 2][:, :], fo[r % 2][:, :], flat(xres[:, ds(n * BR + r, 1), :]),
                                    ALU.add).then_inc(q.e_or, 1)

        @block.tensor
        def _(pe):
            def product(to, pairs, start=True, passes=PASSES):
                last, k = None, 0
                for left, right in pairs:
                    for l, r in passes:
                        last = pe.matmul(to, left(l), right(r), start=start and k == 0,
                                         stop=k == len(pairs) * len(passes) - 1)
                        k += 1
                return last

            pe.wait_ge(q.maskbf, 1)
            pe.wait_ge(q.const_set, 5)
            for c in range(EC):
                last = pe.matmul(ps[6][0:ER, c:c + 1], maskbf[:, 1 + c * ER:1 + (c + 1) * ER], onesb[:, 0:1],
                                 start=True, stop=True)
            last.then_inc(q.ps_set, 1)
            pe.wait_ge(q.act, 2)
            pe.wait_ge(q.consts_bf, 4)
            for c in range(EC):
                pe.matmul(ps[6][0:ER, 8 + c:9 + c], tri, actb[:, c:c + 1], start=True, stop=c == 0)
                for b in range(c):
                    pe.matmul(ps[6][0:ER, 8 + c:9 + c], onesb[0:ER, 0:ER], actb[:, b:b + 1], start=False, stop=b == c - 1)
            for c in range(EC):
                last = pe.matmul(ps[6][0:1, 16:17], onesb[0:ER, 0:1], actb[:, c:c + 1], start=c == 0, stop=c == EC - 1)
            last.then_inc(q.ps_set, 1)
            pe.wait_ge(q.hot, EC)
            pe.wait_ge(q.pos_sb, 2)
            for k in range(2):
                for c in range(EC):
                    last = pe.matmul(ps[6 + k][0:1, 0:NT], code[:, k * EC + c:k * EC + c + 1], hot[:, c],
                                     start=c == 0, stop=c == EC - 1)
                last.then_inc(q.ps_set, 1)
            pe.wait_ge(q.work_in, 16 * 8)
            for j in range(S):
                for h in range(2):
                    last = pe.matmul(ps[j // 32][h * S:h * S + S, (j % 32) * AH:(j % 32) * AH + AH],
                                     buck[:, S - 1 - j:2 * S - 1 - j], emb, start=True, stop=True)
            last.then_inc(q.bias_ps, 1)
            pe.wait_ge(q.small_in, 16 * 8)
            pe.wait_ge(q.wstage_in, 16 * 2)
            pe.wait_ge(q.list_sb, 4 + G)
            for h in range(HP):
                for c in range(FC):
                    pe.matmul(ps[6][:, h:h + 1], st_qkv[:, c, D + h * P:D + (h + 1) * P], lnx[:, 1, c:c + 1],
                              start=c == 0, stop=c == FC - 1)
            pe.wait_ge(q.wkg, 2 * FC)
            for c in range(FC):
                last = pe.matmul(ps[7][:, 0:D], lnx_b[:, c], st_qkv[:, c, 2 * D:3 * D], start=c == 0, stop=c == FC - 1)
            last.then_inc(q.bk_ps, 1)

            def rows_transpose(k):
                _, rh, rl = rows[k]

                def tile(n, j):
                    pe.wait_ge(q.r_lo, n + (k * RT + 1))
                    for l, part in enumerate((rh, rl)):
                        for c in range(FC):
                            at = (l * FC + c) * P
                            last = pe.transpose(ps[j][:, :].bitcast(BF16)[:, at:at + P], part[:, j, c * P:(c + 1) * P],
                                                ident[:, :])
                    last.then_inc(q.r_t, 1)

                for j in range(2):
                    tile(j, j)
                with pe.Fori(2, RT - 1, 2) as n:
                    for j in range(2):
                        pe.wait_ge(q.r_e, n + (k * RT + j - 1))
                        tile(n + j, j)
                pe.wait_ge(q.r_e, (k + 1) * RT)

            def a_step(k, p):
                loop = not isinstance(k, int)
                if runs(k, 0):
                    pe.wait_ge(q.r_lo, k + 1)
                    if loop or k > 0:
                        pe.wait_ge(q.r_e, k)
                    for l, part in enumerate((a_rh, a_rl)):
                        for c in range(FC):
                            at = (l * FC + c) * P
                            last = pe.transpose(ps[7][:, :].bitcast(BF16)[:, at:at + P], part[:, p, c * P:(c + 1) * P],
                                                ident[:, :])
                    last.then_inc(q.r_t, 1)
                if runs(k, 1):
                    j = 1 - p
                    pe.wait_ge(q.r_e, k)
                    if loop or k > 2:
                        pe.wait_ge(q.a_raw, k - 2)
                        pe.wait_ge(q.a_vlo, k - 2)
                    product(ps[2 * j][:, :], [(lambda l, c=c: aT[j][:, l, c, :], lambda r, c=c: wqkv[:, r, c, 0:2 * D])
                                              for c in range(FC)])
                    product(ps[2 * j + 1][:, 0:D], [(lambda l, c=c: aT[j][:, l, c, :],
                                                     lambda r, c=c: wqkv[:, r, c, 2 * D:3 * D])
                                                    for c in range(FC)]).then_inc(q.a_qkv, 1)
                if runs(k, 3):
                    j = 1 - p
                    pe.wait_ge(q.a_lo, k - 2)
                    if loop or k > 3:
                        pe.wait_ge(q.a_qp, 2 * k - 6)
                        pe.wait_ge(q.a_kt, k - 3)
                    for kind in range(2):
                        for l, part in enumerate((qkhi[j], qklo[j])):
                            for h in range(HP):
                                last = pe.matmul(ps[4 + 2 * kind][:, (2 * l + h) * P:(2 * l + h + 1) * P],
                                                 part[:, kind * D + h * P:kind * D + (h + 1) * P],
                                                 ident[:, :], start=True, stop=True)
                    last.then_inc(q.a_t, 1)
                if runs(k, 4):
                    pe.wait_ge(q.a_kt, k - 3)
                    pe.wait_ge(q.a_qp, 2 * k - 6)
                    if loop or k > 4:
                        pe.wait_ge(q.a_p, k - 4)
                    for b in range(2):
                        for h in range(HP):
                            last = product(ps[5][b * S:b * S + S, h * P:(h + 1) * P],
                                           [(lambda l: klt[p][:, 2 * l + h, b * S:b * S + S],
                                             lambda r: qpair[p][:, b, 2 * r + h, :])])
                    last.then_inc(q.a_s, 1)

            pe.wait_ge(q.bias_sb, 4)
            pe.wait_ge(q.bk_sb, 2)
            pe.wait_ge(q.split_lo, 1)
            for k in range(0, RUN.start):
                a_step(k, k % 2)
            with pe.Fori(RUN.start, RUN.stop - 1, 2) as k:
                for p in range(2):
                    a_step(k + p, p)
            for k in range(RUN.stop, LAST):
                a_step(k, k % 2)

            pe.wait_ge(q.pos_sb, 3)
            count = pe.value_load(wn[0:1, 0:1], min_val=1, max_val=NT)

            def b_transpose(w1, h):
                pe.wait_ge(q.b_lo, w1)
                pe.wait_ge(q.b_lo2, w1)
                for l, (part, done) in enumerate(((xch[h], q.b_t), (xcl[h], q.b_tl))):
                    for c in range(FC):
                        for i in range(G):
                            at = c * GT + i * P
                            last = pe.transpose(ps[l][:, :].bitcast(BF16)[:, at:at + P], part[:, i, c * P:(c + 1) * P],
                                                ident[:, :])
                    last.then_inc(done, G)

            def b_keys(w1):
                pe.wait_ge(q.b_eh, w1)
                for h in range(HP):
                    for k, (l, c) in enumerate(((0, 0), (0, 1), (1, 0), (1, 1))):
                        pe.matmul(ps[2 + h][:, :], wkx[:, l, c, h * P:(h + 1) * P], xct[:, 0, c, :],
                                  start=k == 0, stop=False)
                pe.wait_ge(q.b_el, w1)
                for h in range(HP):
                    for c in range(FC):
                        last = pe.matmul(ps[2 + h][:, :], wkx[:, 0, c, h * P:(h + 1) * P], xct[:, 1, c, :],
                                         start=False, stop=c == FC - 1)
                    last.then_inc(q.b_k, G // HP)

            def b_squares(w1):
                pe.wait_ge(q.b_ksq, w1)
                for i in range(G):
                    for h in range(HP):
                        last = pe.matmul(ps[6][:, XH * i:XH * i + XH], ksq[:, h, i * P:(i + 1) * P], headsum[:, h, :],
                                         start=h == 0, stop=h == HP - 1)
                last.then_inc(q.b_ss, G)

            def b_scores(w):
                pe.wait_ge(q.b_klo, w + G)
                pe.wait_ge(q.b_qld, 16 * w + 16 * G)
                for k in range(2):
                    if k == 1:
                        pe.wait_ge(q.b_ms, w + G)
                    for i in range(k * G // 2, (k + 1) * G // 2):
                        for h in range(HP):
                            at = (i % 2) * D + h * P
                            last = product(ps[5 + k][:, at:at + P],
                                           [(lambda l: kct[:, l, h, i * P:(i + 1) * P], lambda r: qc[:, i, 2 * r + h, :])])
                    last.then_inc(q.b_s, G // 2)

            def b_products(w, h):
                pe.wait_ge(q.b_ph, w + G)
                pe.wait_ge(q.b_pl, w + G)
                parts, probs = (xch[h], xcl[h]), (prh, prl)
                for i in range(G):
                    if i == G // 2:
                        b_squares(w + 2 * G)
                    if i >= 2:
                        pe.wait_ge(q.b_acc, w + (i - 1))
                    to, sums = (ps[7], ps[4]) if i % 2 == 0 else (ps[0], ps[1])
                    for h in range(HP):
                        for r in range(2):
                            pe.matmul(sums[:, h:h + 1], probs[r][:, i, h * P:(h + 1) * P], onesb[:, 0:1],
                                      start=r == 0, stop=r == 1)
                    for c in range(FC):
                        last = product(to[:, c * D:(c + 1) * D], [(lambda l: parts[l][:, i, c * P:(c + 1) * P],
                                                                   lambda r: probs[r][:, i])])
                    last.then_inc(q.b_pv, 1)

            pe.wait_ge(q.split_lo, len(splits))
            b_transpose(G, 0)
            b_keys(G)
            b_squares(G)
            with pe.Fori(0, count, 2 * G) as w:
                for h in range(2):
                    at = w + h * G
                    b_scores(at)
                    pe.wait_ge(q.b_acc, at)
                    b_transpose(at + 2 * G, 1 - h)
                    b_keys(at + 2 * G)
                    b_products(at, h)

            pe.wait_ge(q.c_sel, 16)
            pe.wait_ge(q.b_acc, count)
            for k in range(2):
                for b in range(2):
                    last = pe.matmul(ps[6][:, k * RT * HP:(k + 1) * RT * HP], sel[:, k, b, :],
                                     accs.rearrange("p (t b) k -> p b t k", b=2)[:, b], start=b == 0, stop=b == 1)
            last.then_inc(q.c_sums, 1)

            def c_heads(n, j, first=False):
                if not first:
                    pe.wait_ge(q.c_on, n - 1)
                pe.wait_ge(c_ld[j], 24 * n + (48 - 24 * j))
                pe.wait_ge(q.c_ul, 2 * n + 2)
                us = (c_uh[j], c_ul[j])
                for h in range(XH):
                    head = slice(h * DH, h * DH + DH)
                    latents = [c_pb[j][:, l, h].rearrange("p b n -> p (b n)") for l in range(2)]
                    product(ps[j][:, head],
                            [(lambda l, c=c: us[l][:, c, h].rearrange("p b n -> p (b n)"), lambda r, c=c: wvx[:, r, c, head])
                             for c in range(FC)] +
                            [(lambda l: latents[l], lambda r: c_vl[j][:, r, head])])
                    for l in range(2):
                        last = pe.matmul(ps[j][:, D + h:D + h + 1], latents[l], onesb[:, 0:1], start=l == 0, stop=l == 1)
                last.then_inc(q.c_ot, 1)

            def c_transpose(n, j):
                pe.wait_ge(q.c_ol, n + 1)
                for l, part in enumerate((c_oth[j], c_otl[j])):
                    for c in range(HP):
                        at = (l * HP + c) * P
                        last = pe.transpose(ps[2 + j][:, :].bitcast(BF16)[:, at:at + P], part[:, c * P:(c + 1) * P], ident[:, :])
                last.then_inc(q.c_t, 1)

            def c_out(n, j, first=False):
                pe.wait_ge(q.c_te, n + 1)
                if not first:
                    pe.wait_ge(q.c_x, n - 1)
                for r in range(2):
                    pe.matmul(ps[4 + j][:, 0:D], onesb[0:1, :], bo[0:1, r, :], start=r == 0, stop=False)
                product(ps[4 + j][:, 0:D], [(lambda l, c=c: c_otT[j][:, l, c, :], lambda r, c=c: wo[:, r, c, :])
                                            for c in range(HP)], start=False).then_inc(q.c_o, 1)

            pe.wait_ge(q.bo_lo, 1)
            c_heads(0, 0, first=True)
            c_heads(1, 1, first=True)
            c_transpose(0, 0)
            for j in range(2):
                c_heads(2 + j, j)
                c_transpose(1 + j, 1 - j)
                c_out(j, j, first=True)
            with pe.Fori(4, RT - 1, 2) as n:
                for j in range(2):
                    c_heads(n + j, j)
                    c_transpose(n + (j - 1), 1 - j)
                    c_out(n + (j - 2), j)
            c_transpose(RT - 1, 1)
            c_out(RT - 2, 0)
            c_out(RT - 1, 1)
            pe.wait_ge(q.c_x, RT)

            rows_transpose(1)

            def d_qk(n):
                for k in range(4):
                    for c4 in range(4):
                        m = 4 * k + c4
                        last = product(ps[QK_BANKS[k]][:, c4 * P:(c4 + 1) * P],
                                       [(lambda l, c=c: wqk[:, l, c, m * P:(m + 1) * P],
                                         lambda r, c=c: rowT[:, r, c, ds(n * P, P)]) for c in range(FC)])
                    last.then_inc(q.d_qk, 1)

            def d_v(n):
                for k in range(2):
                    product(ps[k][:, :], [(lambda l, c=c: rowT[:, l, c, ds(n * P, P)],
                                           lambda r, c=c: wva[:, r, c, k * 512:k * 512 + 512])
                                          for c in range(FC)]).then_inc(q.d_v, 1)

            def d_scores(n):
                pe.wait_ge(q.d_qlo, 4 * n + 4)
                pe.sem_inc(q.gate, 1)
                parts = (qkh, qkl)
                for hp in range(AP_):
                    for b in range(2):
                        for l, r in PASSES:
                            for h2 in range(2):
                                c = (hp + 4 * h2) % AP_
                                rows_, cols = slice(h2 * DH, h2 * DH + DH), slice(b * S, b * S + S)
                                last = pe.matmul(ps[2 + c // 4][rows_, (c % 4) * P + b * S:(c % 4) * P + b * S + S],
                                                 parts[l][rows_, c, cols], parts[r][rows_, AP_ + c, cols],
                                                 start=(l, r) == PASSES[0], stop=(l, r) == PASSES[-1])
                last.then_inc(q.d_s, 1)

            def d_out(n):
                pe.wait_ge(q.d_ahi, 2 * n + 2)
                pe.wait_ge(q.d_alo, 2 * n + 2)
                atts = (ath, atl)
                product(ps[4][:, 0:D], [(lambda l, c=c: atts[l][:, c, :], lambda r, c=c: woa[:, r, c, :])
                                        for c in range(AP_)]).then_inc(q.d_o, 1)

            def d_tile(n, j, first=False, last_tile=False):
                d_scores(n)
                if not first:
                    d_out(n - 1)
                if not last_tile:
                    pe.wait_ge(q.d_vlo, 2 * n + 2)
                    d_qk(n + 1)
                pe.wait_ge(q.d_phi, n + 1)
                pe.wait_ge(q.d_plo, n + 1)
                if not first:
                    pe.wait_ge(q.d_x, n)
                for l, part in enumerate((sph, spl)):
                    for c in range(AP_):
                        last = pe.transpose(ps[4 + l][:, :].bitcast(BF16)[:, c * P:(c + 1) * P], part[:, c, :], ident[:, :])
                    last.then_inc(q.d_pt, 1)
                if not last_tile:
                    pe.wait_ge(q.d_qlo, 4 * n + 8)
                    d_v(n + 1)
                pe.wait_ge(q.d_peh, n + 1)
                pe.wait_ge(q.d_pel, n + 1)
                pe.wait_ge(q.d_vlo, 2 * n + 2)
                pe.sem_inc(q.gate, 1)
                values = (vh[j], vlo[j])
                for c in range(AP_):
                    for h2 in range(2):
                        head = (2 * c + h2) * DH
                        for l, r in PASSES:
                            for b in range(2):
                                rows_ = slice(b * S, b * S + S)
                                last = pe.matmul(ps[6 + b][h2 * DH:h2 * DH + DH, c * S:c * S + S],
                                                 values[l][rows_, head:head + DH], pT[rows_, r, c, h2 * S:h2 * S + S],
                                                 start=(l, r) == PASSES[0], stop=(l, r) == PASSES[-1])
                last.then_inc(q.d_pv, 1)

            d_qk(0)
            pe.wait_ge(q.d_qlo, 4)
            d_v(0)
            d_tile(0, 0, first=True)
            with pe.Fori(1, RT - 2, 2) as n:
                for j in range(2):
                    d_tile(n + j, 1 - j)
            d_tile(RT - 1, 1, last_tile=True)
            d_out(RT - 1)
            pe.wait_ge(q.d_x, RT)

            rows_transpose(2)
            pe.wait_ge(q.f_any, 1)
            pe.matmul(ps[4][0:1, 0:1], lowany[:, :], onesb[:, 0:1], start=True, stop=True).then_inc(q.f_count, 1)
            pe.wait_ge(q.f_known, 1)
            low_parts = pe.value_load(lown[0:1, 0:1], min_val=0, max_val=P)

            def feed_forward(passes):
                swapped = [(r, l) for l, r in passes]
                with pe.Fori(0, NB) as n:
                    for m in range(HC):
                        if m >= 2:
                            pe.wait_ge(q.e_hf, HC * n + (m - 1))
                        for k, w in enumerate((w1, w2)):
                            last = product(ps[2 * (m % 2) + k][:, :],
                                           [(lambda l, c=c: w[:, l, c, m * P:(m + 1) * P],
                                             lambda r, c=c: rowT[:, r, c, ds(n * BLK, BLK)]) for c in range(FC)],
                                           passes=passes)
                        last.then_inc(q.e_1, 1)
                    for layer, (w, ready, done) in enumerate(((h1, q.e_g1, q.e_h1), (h2, q.e_g2, q.e_h2))):
                        for m in range(HC):
                            if m < 2:
                                pe.wait_ge(q.e_g2 if layer == 0 else q.e_g1, HC * n + HC * layer)
                            else:
                                pe.wait_ge(ready, HC * n + (m - 1))
                            k = 0
                            for c in range(HC):
                                if m == 0:
                                    if layer == 0:
                                        pe.wait_ge(q.e_lo, HC * n + (c + 1))
                                    else:
                                        pe.wait_ge(q.e_glo, 2 * HC * n + (c + 1))
                                for l, r in passes:
                                    last = pe.matmul(ps[4 + m % 2][:, :], w[:, l, c, m * P:(m + 1) * P],
                                                     hb[layer][:, r, c], start=k == 0, stop=k == len(passes) * HC - 1)
                                    k += 1
                            last.then_inc(done, 1)
                    pe.wait_ge(q.e_glo, 2 * HC * n + 2 * HC)
                    for r_ in range(BR):
                        pe.wait_ge(q.e_os, BR * n + max(r_ - 1, 0))
                        product(ps[6 + r_ % 2][:, 0:D],
                                [(lambda l, c=c: hb[0][:, l, c, r_ * P:(r_ + 1) * P], lambda r, c=c: w3[:, r, c, :])
                                 for c in range(HC)], passes=swapped).then_inc(q.e_o, 1)

            with pe.If(low_parts < 1):
                feed_forward(PASSES[0:2])
            with pe.If(low_parts > 0):
                feed_forward(PASSES)


def rel_buckets():
    half, exact, far = NBUCK // 2, NBUCK // 4, 128
    table = np.zeros((NBUCK, P), np.float32)
    for m in range(2 * S - 1):
        rel = S - 1 - m
        dist = abs(rel)
        if dist >= exact:
            coeff = (half - exact) / np.log(far / exact)
            dist = min(half - 1, exact + int(np.log(np.float32(dist) / np.float32(exact)) * np.float32(coeff)))
        table[(half if rel > 0 else 0) + dist, m] = 1.0
    return table


def kernel(**inputs):
    import concourse.bacc as bacc
    from concourse.bass_utils import run_bass_kernel_spmd

    g = {k: np.asarray(v) for k, v in inputs.items()}
    x, mask = g["x"], g["mask_BxS2_bk0"]
    n = "L0_xattn_"
    f, a_ = "L0_ffn_", "L0_attn_"
    qkv = g[a_ + "qkv_w"]

    def chunks(w):
        return w.T.reshape(-1, P, w.shape[0]).transpose(1, 0, 2).reshape(P, -1)

    padded = np.zeros((B, KT * P), np.bool_)
    padded[:, FRONT:] = mask
    cols = padded.reshape(B * KT, P).T
    tiles = np.arange(NT).reshape(EC, ER).T
    arrays = {
        "x": x.reshape(ROWS, D),
        "ctx": np.concatenate([np.zeros((P + FRONT, D), np.float32), g["ctx_1024"].reshape(B * SC, D)]),
        "mask": np.concatenate([np.zeros((P, 1), np.bool_), cols], axis=1),
        "iota": np.broadcast_to(np.arange(NT, dtype=np.float32), (ER, NT)),
        "code": np.concatenate([tiles // KT, tiles % KT + 1], axis=1).astype(np.float32),
        "tri": np.triu(np.ones((ER, ER), np.float32), 1),
        "ident": np.eye(P, dtype=np.float32),
        "buck": rel_buckets(),
        "emb": g[a_ + "emb_weight"],
        "sel": (np.arange(P)[:, None, None, None] ==
                np.arange(2)[None, :, None, None] * S + np.arange(P) % S).astype(np.float32)
        * (np.arange(2)[:, None] == np.arange(P) // S),
        "headsum": (np.arange(HP * P).reshape(HP, P).T[:, :, None] // DH == np.arange(XH)).astype(np.float32),
        "ln_l_g": g[n + "ln_l_g"], "ln_l_b": g[n + "ln_l_b"],
        "q_gamma": g[n + "q_gamma"], "k_gamma": g[n + "k_gamma"],
        "lnx": np.stack([g[n + "ln_x_g"].reshape(FC, P).T, g[n + "ln_x_b"].reshape(FC, P).T], axis=1),
        "b_out": g[n + "b_out"].reshape(1, D),
        "w3_s": g[f + "w3_s"],
        "hs": np.stack([g[f + k].reshape(HC, P).T for k in ("w1_s", "w2_s", "h1_s", "h2_s")], axis=1),
        "wqkv": np.concatenate([g[n + "W_q"], g[n + "W_kv"]], axis=1),
        "wo": g[n + "W_out"],
        "wat": np.concatenate([chunks(qkv[0:2 * AH * DH]), chunks(qkv[2 * AH * DH:]), chunks(g[a_ + "o_w"])], axis=1)
        .reshape(P, RT, ATP).transpose(1, 0, 2),
        "wff": np.concatenate([chunks(g[f + k]) for k in ("w1_w", "w2_w", "h1_w", "h2_w", "w3_w")], axis=1)
        .reshape(P, RT, PIECE).transpose(1, 0, 2),
    }
    arrays = {k: np.ascontiguousarray(v) for k, v in arrays.items()}

    nc = bacc.Bacc("TRN2", target_bir_lowering=False, num_devices=1)
    t = {k: nc.dram_tensor("in_" + k, v.shape, mybir.dt.from_np(v.dtype), kind="ExternalInput").ap()
         for k, v in arrays.items()}
    out = nc.dram_tensor("out", [ROWS, D], F32, kind="ExternalOutput").ap()
    build(nc, t, out)
    result = run_bass_kernel_spmd(nc, [{"in_" + k: v for k, v in arrays.items()}], core_ids=[0])
    return result.results[0]["out"].reshape(B, S, D)
```

```python
from collections import namedtuple
from contextlib import ExitStack

import numpy as np

import concourse.bass as bass
from concourse import mybir

F32 = mybir.dt.float32
BF16 = mybir.dt.bfloat16
I32 = mybir.dt.int32
U8 = mybir.dt.uint8
ALU = mybir.AluOpType
ACT = mybir.ActivationFunctionType
AX = mybir.AxisListType
ds = bass.ds

P = 128
B, S, D = 32, 64, 256
SC = 1601
FC = D // P
ROWS = B * S
RT = ROWS // P
XH, DH = 4, 64
HP = XH // 2
KT = -(-SC // P)
FRONT = KT * P - SC
NT = B * KT
EC = 4
ER = NT // EC
G = 4
GT = G * P
LW = NT + 4 * G
BB = 5
assert B <= 1 << BB and NT % G == 0 and G * BB < 24
AH = 16
AP_ = AH // 2
HID = 1024
HC = HID // P
BLK = 512
NB = ROWS // BLK
BR = BLK // P
NBUCK = 32
ATW = FC * 3 * AH * DH + AP_ * D
ATP = ATW // RT
FFW = 2 * FC * HID + 2 * HC * HID + HC * D
PIECE = FFW // RT
LN_EPS = 1e-5
RMS_FLOOR = 1e-8 ** 2
MASKED = -1e30
SCALE = DH ** -0.5
QK_BANKS = (0, 1, 6, 7)
PASSES = ((0, 0), (0, 1), (1, 0))


def flat(ap):
    return ap.rearrange("p a b -> p (a b)")


def build(nc, t, out):
    ctx = ExitStack()
    with ctx:
        def sb(name, shape, dt):
            return ctx.enter_context(nc.sbuf_tensor(name, shape, dt))

        xres = sb("xres", [P, RT, D], F32)
        wkx = sb("wkx", [P, 2, FC, D], BF16)
        wvx = sb("wvx", [P, 2, FC, D], BF16)
        wo = sb("wo", [P, 2, FC, D], BF16)
        wat = sb("wat", [P, 2, ATW], BF16)
        wqk = wat[:, :, 0:FC * 2 * AH * DH].rearrange("p l (c n) -> p l c n", c=FC)
        wva = wat[:, :, FC * 2 * AH * DH:FC * 3 * AH * DH].rearrange("p l (c n) -> p l c n", c=FC)
        woa = wat[:, :, FC * 3 * AH * DH:ATW].rearrange("p l (c n) -> p l c n", c=AP_)
        bias = sb("bias", [P, AP_, S], F32)
        ident = sb("ident", [P, P], BF16)
        onesb = sb("onesb", [P, P], BF16)
        headsum = sb("headsum", [P, HP, XH], F32)
        neghalf = sb("neghalf", [P, RT * 8], F32)
        maskb = sb("maskb", [P, NT + 1], F32)
        wl = sb("wl", [1, 4, LW], I32)
        wn = sb("wn", [1, 1], I32)
        lnx = sb("lnx", [P, 2, FC], F32)
        bk = sb("bk", [P, HP], F32)
        bv = sb("bv", [P, D], F32)
        bof = sb("bof", [1, D], F32)
        bo = sb("bo", [1, 2, D], BF16)
        w3s = sb("w3s", [P, D], F32)
        hs = sb("hs", [P, 4, HC], F32)
        stats = sb("stats", [P, RT, 6], F32)
        mv = sb("mv", [P, RT, 2], F32)
        var_eps = sb("ve", [P, RT], F32)
        rstd = sb("rstd", [P, RT], F32)
        sm1 = sb("sm1", [P, AH], F32)
        sm2 = sb("sm2", [P, AH], F32)
        sm3 = sb("sm3", [P, AH], F32)
        lowmax = sb("lowmax", [P, RT], F32)
        lowany = sb("lowany", [P, 1], BF16)
        lown = sb("lown", [1, 1], I32)
        mt = sb("mt", [P, 3, RT], F32)
        big = sb("big", [P, B * 3 * D], F32)
        d_rn = sb("d_rn", [P, D], F32)
        tmp = sb("tmp", [P, 40 * 256], F32)

        ps = [ctx.enter_context(nc.psum_tensor(f"ps{i}", [P, 512], F32)) for i in range(8)]

        def carve(area, at, words, dt=F32):
            assert at + words <= area.shape[1], (at, words)
            piece = area[:, at:at + words]
            return piece if dt == F32 else piece.bitcast(dt)

        mask8 = carve(tmp, 0, 105, U8)[:, 0:NT + 1]
        maskbf = carve(tmp, 108, 209, BF16)[:, 0:NT + 1]
        iota = carve(tmp, 320, NT)[0:ER, :]
        codef = carve(tmp, 736, 8)[0:ER, :]
        code = carve(tmp, 744, 4, BF16)[0:ER, :]
        trif = carve(tmp, 752, 128)[0:ER, 0:ER]
        tri = carve(tmp, 880, 64, BF16)[0:ER, 0:ER]
        actf = carve(tmp, 944, EC)[0:ER, :]
        actb = carve(tmp, 948, EC // 2, BF16)[0:ER, :]
        pos = carve(tmp, 952, EC)[0:ER, :]
        hot = carve(tmp, 960, EC * NT // 2, BF16)[0:ER, :].rearrange("p (c n) -> p c n", c=EC)
        buck = carve(tmp, 1792, 128)[0:NBUCK, :]
        emb = carve(tmp, 1920, AH)[0:NBUCK, :]
        identf = carve(tmp, 1936, 128)
        tile1 = carve(tmp, 2064, NT)[0:1, :]
        row128 = carve(tmp, 2480, NT)[0:1, :]
        lnx_b = carve(tmp, 2896, FC * P).rearrange("p (c n) -> p c n", c=FC)
        wkg = carve(tmp, 3152, 1024).rearrange("p (c n) -> p c n", c=FC)
        xn1 = carve(big, 0, 4096).rearrange("p (t n) -> p t n", t=RT)
        st_qkv = carve(big, 4096, 1536).rearrange("p (c n) -> p c n", c=FC)
        head_of_acc = carve(big, 0, 4096 + 1536)
        wqkv = carve(tmp, 4992, 1536, BF16).rearrange("p (l c n) -> p l c n", l=2, c=FC)
        lng = carve(tmp, 6528, 256)
        lnb = carve(tmp, 6784, 256)
        gq = carve(tmp, 7040, 64)
        gk = carve(tmp, 7104, 64)
        a_rn = carve(tmp, 7168, 512).rearrange("p (t n) -> p t n", t=2)
        a_rh = carve(tmp, 7680, 256, BF16).rearrange("p (t n) -> p t n", t=2)
        a_rl = carve(tmp, 7936, 256, BF16).rearrange("p (t n) -> p t n", t=2)
        sq2 = [carve(tmp, 8192 + 512 * i, 512) for i in range(2)]
        ss = carve(tmp, 9216, 128)
        rr = carve(tmp, 9344, 128)
        a_at = B * 2 * D + B * HP + 4 * P + RT * XH

        def by_turns(at, words, dt=F32):
            return [carve(big, a_at + at + words * i, words, dt) for i in range(2)]

        qkraw = by_turns(0, 512)
        qkhi, qklo = by_turns(1024, 256, BF16), by_turns(1536, 256, BF16)
        qpair = [x.rearrange("p (b k n) -> p b k n", b=2, k=4) for x in by_turns(2048, 512, BF16)]
        klt = [x.rearrange("p (k n) -> p k n", k=4) for x in by_turns(3072, 256, BF16)]
        pl_a = by_turns(3584, 256)
        pls = [x.rearrange("p (l n) -> p l n", l=2) for x in by_turns(4096, 256, BF16)]
        vst = [x.rearrange("p (l n) -> p l n", l=2) for x in by_turns(4608, 256, BF16)]
        aT = [x.rearrange("p (l c n) -> p l c n", l=2, c=FC) for x in by_turns(5120, 256, BF16)]
        st_wo = carve(big, a_at + 5632, 512).rearrange("p (c n) -> p c n", c=FC)
        st_at = by_turns(6144, ATP)

        acc = carve(big, 0, B * 2 * D).rearrange("p (b n) -> p b n", b=B)
        accs = carve(big, B * 2 * D, B * HP).rearrange("p (b k) -> p b k", b=B)
        sel = carve(big, B * 2 * D + B * HP, 4 * P).rearrange("p (h b n) -> p h b n", h=2, b=2)
        csum = carve(big, B * 2 * D + B * HP + 4 * P, RT * XH).rearrange("p (t h) -> p t h", t=RT)
        xt = [carve(tmp, 1024 * i, 1024).rearrange("p (i n) -> p i n", i=G) for i in range(2)]
        xch = [carve(tmp, 2048 + 512 * i, 512, BF16).rearrange("p (i n) -> p i n", i=G) for i in range(2)]
        xcl = [carve(tmp, 3072 + 512 * i, 512, BF16).rearrange("p (i n) -> p i n", i=G) for i in range(2)]
        xct = carve(tmp, 4096, 1024, BF16).rearrange("p (l c n) -> p l c n", l=2, c=FC)
        ksq = carve(tmp, 5120, 1024).rearrange("p (c n) -> p c n", c=HP)
        kct = carve(tmp, 6144, 1024, BF16).rearrange("p (l c n) -> p l c n", l=2, c=HP)
        pr = carve(tmp, 7168, 1024).rearrange("p (i n) -> p i n", i=G)
        prh = carve(tmp, 8192, 512, BF16).rearrange("p (i n) -> p i n", i=G)
        prl = carve(tmp, 8704, 512, BF16).rearrange("p (i n) -> p i n", i=G)
        qc = carve(tmp, 9216, 1024, BF16).rearrange("p (i k n) -> p i k n", i=G, k=4)
        cst, cmv, cve, crs = stats[:, 0:G, :], mv[:, 0:G, :], var_eps[:, 0:G], rstd[:, 0:G]

        def c_set(at, fields):
            got = {}
            for name, words, dt in fields:
                got[name] = carve(tmp, at, words, dt)
                at += words
            return got

        c_pb = [carve(tmp, 7168 + 512 * j, 512, BF16).rearrange("p (l h b n) -> p l h b n", l=2, h=XH, b=2) for j in range(2)]
        c_fields = (("vl", 256, BF16), ("uh", 512, BF16), ("ul", 512, BF16), ("ub", 256, F32),
                    ("ot", 256, F32), ("oth", 128, BF16), ("otl", 128, BF16), ("otT", 256, BF16))
        cs = [c_set(2560 * j, c_fields) for j in range(2)]
        c_ot, c_ub, c_oth, c_otl = ([c[k] for c in cs] for k in ("ot", "ub", "oth", "otl"))
        c_vl = [c["vl"].rearrange("p (l n) -> p l n", l=2) for c in cs]
        c_uh, c_ul = ([c[k].rearrange("p (c h b n) -> p c h b n", c=FC, h=XH, b=2) for c in cs] for k in ("uh", "ul"))
        c_otT = [c["otT"].rearrange("p (l c n) -> p l c n", l=2, c=HP) for c in cs]

        wff = carve(big, 0, FFW, BF16).rearrange("p (l n) -> p l n", l=2)
        wst = carve(big, FFW, PIECE)
        fo = [carve(big, FFW + i * D, D) for i in range(2)]

        def ff_weights(first, chunks, width):
            return wff[:, :, first:first + chunks * width].rearrange("p l (c n) -> p l c n", n=width)

        w1, w2 = ff_weights(0, FC, HID), ff_weights(FC * HID, FC, HID)
        h1, h2 = ff_weights(2 * FC * HID, HC, HID), ff_weights((2 * FC + HC) * HID, HC, HID)
        w3 = ff_weights(2 * (FC + HC) * HID, HC, D)
        rowT = carve(tmp, 0, 4096, BF16).rearrange("p (l c n) -> p l c n", l=2, c=FC)
        qkh = carve(tmp, 4096, 1024, BF16).rearrange("p (c n) -> p c n", n=P)
        qkl = carve(tmp, 5120, 1024, BF16).rearrange("p (c n) -> p c n", n=P)
        vh = [carve(tmp, 6144, 512, BF16), wkx[:, :, :, :].rearrange("p l c n -> p (l c n)")]
        vlo = [carve(tmp, 6656, 512, BF16), wvx[:, :, :, :].rearrange("p l c n -> p (l c n)")]
        sc = carve(tmp, 7168, 1024).rearrange("p (k n) -> p k n", n=S)
        sph = carve(tmp, 8192, 512, BF16).rearrange("p (c n) -> p c n", n=P)
        spl = carve(tmp, 8704, 512, BF16).rearrange("p (c n) -> p c n", n=P)
        ath, atl = (area.rearrange("p (c n) -> p c n", n=P) for area in
                    (wo[:, :, :, :].rearrange("p l c n -> p (l c n)"), carve(big, FFW + PIECE, 512, BF16)))
        pT = carve(tmp, 9216, 1024, BF16).rearrange("p (l c n) -> p l c n", l=2, n=P)
        d_rh, d_rl = maskb[:, 0:D // 2].bitcast(BF16), carve(big, FFW + PIECE + 512, D // 2, BF16)
        hb = [carve(tmp, 4096, 4096, BF16).rearrange("p (l c n) -> p l c n", l=2, c=HC),
              wat[:, :, 0:HC * BLK].rearrange("p l (c n) -> p l c n", n=BLK)]
        hf = [carve(tmp, 8192 + 512 * i, 512) for i in range(2)]
        sil = [carve(tmp, 9216 + 512 * i, 512) for i in range(2)]

        def acc_heads(n, c):
            return acc[:, ds(n * 2, 2), c * D:(c + 1) * D].rearrange("p b (h i) -> p h b i", h=XH)

        q_scr = nc.dram_tensor("q_scr", [B, P, 4 * P], BF16, kind="Internal").ap()
        p_scr = nc.dram_tensor("p_scr", [RT, P, 2 * D], BF16, kind="Internal").ap()
        v_scr = nc.dram_tensor("v_scr", [RT, P, 2 * D], BF16, kind="Internal").ap()

        splits = [(st_qkv, wqkv), (wkg[:, :, 0:D], wkx), (wkg[:, :, D:2 * D], wvx), (st_wo, wo)]
        D_RUN = range(1, RT - 3, 2)
        RUN, LAST = range(6, RT - 2, 2), RT + 5
        AHEAD = RT

        def runs(k, behind):
            return not isinstance(k, int) or 0 <= k - behind < RT

        def norms(k):
            return not isinstance(k, int) or k + 3 < RT + BR

        names = """x_in work_in small_in wstage_in const_set gains
                maskbf act ps_set pos_sb hot list_sb consts_bf
                bias_ps bias_sb bk_ps bk_sb wkg split_hi split_lo w_ld0 w_ld1 w_hi w_lo bo_hi bo_lo
                m_halves m_terms n_halves n_terms x1_n r_st r_ve r_rs r_n r_g r_hi r_lo r_t r_e
                a_qkv a_raw a_sq a_ss a_vhi a_vlo a_ms a_rr a_qkn a_gq a_hi a_lo a_t a_qp a_kt a_s a_p a_phi a_plo
                a_qst a_pst a_vst
                acc_zero b_ld0 b_ld1 b_qld b_st b_ve b_rs b_n b_hi b_lo b_lo2 b_t b_tl b_eh b_el b_k b_ksq b_khi b_klo
                b_ss b_ms b_rr b_s b_sn b_p b_ph b_pl b_pv b_acc
                c_ld0 c_ld1 c_zero c_sel c_sums c_csum c_uh c_ul c_ub c_ot c_step c_on c_oh c_ol c_t c_te c_o c_x
                f_ld f_hi f_lo f_max f_any f_count f_known
                d_qk d_qhi d_qlo d_v d_vhi d_vlo d_s d_sb d_stat d_sub d_ex d_pn d_phi d_plo
                gate d_pt d_peh d_pel d_pv d_ahi d_alo d_o d_x
                e_1 e_sil e_hf e_h1 e_g1 e_h2 e_g2 e_hi e_lo e_glo e_o e_os e_or e_out0 e_out1""".split()
        q = namedtuple("Semaphores", names)(*(ctx.enter_context(nc.semaphore(name)) for name in names))

        w_ld, b_ld, c_ld, e_out = (q.w_ld0, q.w_ld1), (q.b_ld0, q.b_ld1), (q.c_ld0, q.c_ld1), (q.e_out0, q.e_out1)

        block = ctx.enter_context(nc.Block())

        @block.sync
        def _(sp):
            for to, name in ((mask8, "mask"), (iota, "iota"), (codef, "code"), (trif, "tri"),
                             (identf, "ident"), (buck, "buck"), (emb, "emb"), (headsum[:, :, :], "headsum")):
                sp.dma_start(to, t[name]).then_inc(q.work_in, 16)
            sp.dma_start(xres[:, :, :], t["x"].rearrange("(t p) n -> p t n", p=P)).then_inc(q.x_in, 16)
            for to, name in ((st_qkv, "wqkv"), (st_wo, "wo")):
                sp.dma_start(to, t[name].rearrange("(c p) n -> p c n", p=P)).then_inc(q.wstage_in, 16)
            for to, name in ((lng, "ln_l_g"), (lnb, "ln_l_b"), (gq, "q_gamma"), (gk, "k_gamma"), (w3s[:, :], "w3_s")):
                sp.dma_start(to, t[name].partition_broadcast(P)).then_inc(q.small_in, 16)
            for to, name in ((lnx[:, :, :], "lnx"), (bof[:, :], "b_out"), (hs[:, :, :], "hs")):
                sp.dma_start(to, t[name]).then_inc(q.small_in, 16)

            def load_w(k, p):
                sp.dma_start(st_at[p], t["wat"][ds(k, 1)].rearrange("t p n -> p (t n)")).then_inc(w_ld[p], 16)

            def a_step(k, p):
                if runs(k, -1):
                    if not isinstance(k, int) or k > 0:
                        sp.wait_ge(q.w_lo, k)
                    load_w(k + 1, 1 - p)
                if runs(k, 4):
                    sp.wait_ge(q.a_qp, 2 * k - 6)
                    sp.wait_ge(q.a_qst, 16 * k - 64)
                    sp.dma_start(q_scr[ds(k * 2 - 8, 2)].rearrange("b p n -> p b n"),
                                 qpair[p].rearrange("p b k n -> p b (k n)")).then_inc(q.a_qst, 16)
                if runs(k, 5):
                    sp.wait_ge(q.a_plo, k - 4)
                    sp.sem_inc(q.gate, 1)
                    sp.wait_ge(q.a_pst, 16 * k - 80)
                    sp.dma_start(p_scr[ds(k - 5, 1)].rearrange("t p n -> p (t n)"),
                                 pls[1 - p].rearrange("p l n -> p (l n)")).then_inc(q.a_pst, 16)
                if runs(k, 1):
                    sp.wait_ge(q.a_vlo, k)
                    sp.sem_inc(q.gate, 1)
                    sp.wait_ge(q.a_vst, 16 * k - 16)
                    sp.dma_start(v_scr[ds(k - 1, 1)].rearrange("t p n -> p (t n)"),
                                 vst[1 - p].rearrange("p l n -> p (l n)")).then_inc(q.a_vst, 16)

            def load_x(w, h, split):
                rows_at = []
                for i in range(G):
                    rows_at.append(sp.value_load(wl[0:1, 2, ds(w + i, 1)], min_val=0, max_val=(B - 1) * SC + KT * P))
                if split is not None:
                    sp.wait_ge(q.b_lo, split)
                    sp.wait_ge(q.b_lo2, split)
                for i in range(G):
                    sp.dma_start(xt[h][:, i, :], t["ctx"][ds(rows_at[i], P), :]).then_inc(b_ld[h], 16)

            load_w(0, 0)
            sp.wait_ge(q.list_sb, 4 + G)
            sp.wait_ge(q.bias_ps, 1)
            sp.wait_ge(q.bk_ps, 1)
            sp.wait_ge(q.split_lo, len(splits))
            sp.dma_start(sel, t["sel"]).then_inc(q.c_sel, 16)
            load_x(0, 0, None)
            load_x(G, 1, None)
            for k in range(0, RUN.start):
                a_step(k, k % 2)
            with sp.Fori(RUN.start, RUN.stop - 1, 2) as k:
                for p in range(2):
                    a_step(k + p, p)
            for k in range(RUN.stop, LAST):
                a_step(k, k % 2)
            sp.wait_ge(q.a_qst, 16 * RT)
            sp.wait_ge(q.a_pst, 16 * RT)
            sp.wait_ge(q.a_vst, 16 * RT)
            count = sp.value_load(wn[0:1, 0:1], min_val=1, max_val=NT)

            def load_q(w):
                for i in range(G):
                    bi = sp.value_load(wl[0:1, 0, ds(w + i, 1)], min_val=0, max_val=B - 1)
                    sp.dma_start(qc[:, i].rearrange("p k n -> p (k n)"),
                                 q_scr[ds(bi, 1)].rearrange("b p n -> p (b n)")).then_inc(q.b_qld, 16)

            with sp.Fori(0, count, 2 * G) as w:
                for h in range(2):
                    sp.wait_ge(q.b_s, w + h * G)
                    load_q(w + h * G)
                    load_x(w + (h + 2) * G, h, w + (h + 1) * G)
            sp.wait_ge(q.b_lo, count + 2 * G)
            sp.wait_ge(q.b_lo2, count + 2 * G)
            sp.sem_inc(q.gate, 1)
            sp.wait_ge(q.b_klo, count + G)
            sp.wait_ge(q.b_ksq, count + G)
            sp.wait_ge(q.b_acc, count)

            def load_c(n, j):
                for b in range(2):
                    r = slice(b * S, b * S + S)
                    sp.dma_start(c_pb[j][r, :, :, b, :].rearrange("p l h n -> p (l h) n"),
                                 p_scr[ds(n, 1), r].rearrange("t p (k n) -> p (t k) n", n=S)).then_inc(c_ld[j], 16)
                sp.dma_start(c_vl[j].rearrange("p l n -> p (l n)"),
                             v_scr[ds(n, 1)].rearrange("t p n -> p (t n)")).then_inc(c_ld[j], 16)

            sp.wait_ge(q.c_zero, 4)
            for j in range(2):
                load_c(j, j)
            with sp.Fori(2, RT - 1, 2) as n:
                for j in range(2):
                    sp.wait_ge(q.c_ot, n + (j - 1))
                    load_c(n + j, j)
            sp.wait_ge(q.c_x, RT)
            with sp.Fori(0, RT) as k:
                sp.wait_ge(q.f_lo, k)
                sp.dma_start(wst, t["wff"][ds(k, 1)].rearrange("t p n -> p (t n)")).then_inc(q.f_ld, 16)
            with sp.Fori(0, RT - 1, 2) as n:
                for j in range(2):
                    sp.wait_ge(q.e_or, n + j + 1)
                    sp.dma_start(out[ds((n + j) * P, P), :], fo[j][:, :]).then_inc(e_out[j], 16)
            for j in range(2):
                sp.wait_ge(e_out[j], 16 * RT // 2)

        @block.gpsimd
        def _(po):
            po.memset(neghalf[:, :], -0.5).then_inc(q.const_set, 1)
            po.memset(onesb[:, :], 1.0).then_inc(q.const_set, 1)
            po.memset(wl[:, :, :], 0).then_inc(q.const_set, 1)
            for j in range(2):
                po.memset(qpair[j].rearrange("p b k n -> p (b k n)"), 0.0).then_inc(q.const_set, 1)
            po.memset(big[:, 4096 + 1536:B * 2 * D + B * HP], 0.0).then_inc(q.acc_zero, 1)
            po.wait_ge(q.small_in, 16 * 8)
            po.tensor_tensor(gq, gq, gk, ALU.mult).then_inc(q.gains, 1)
            po.wait_ge(q.gains, 1)
            po.tensor_scalar(gq, gq, SCALE, None, ALU.mult).then_inc(q.gains, 1)
            po.wait_ge(q.const_set, 5)

            def rows_norm(k):
                po.wait_ge(q.r_ve, k + 2)
                po.tensor_tensor(rstd[:, :], var_eps[:, :], neghalf[:, 0:RT], ALU.pow).then_inc(q.r_rs, 1)

            rows_norm(-1)
            rows_norm(0)

            def a_step(k, p):
                if runs(k, 2):
                    po.wait_ge(q.a_ms, k - 1)
                    po.tensor_tensor(rr[:, ds(k * 8 - 16, 8)], ss[:, ds(k * 8 - 16, 8)], neghalf[:, 0:8],
                                     ALU.pow).then_inc(q.a_rr, 1)
                if runs(k, 5):
                    po.wait_ge(q.a_phi, k - 4)
                    po.tensor_tensor(pls[1 - p][:, 1], pl_a[1 - p], pls[1 - p][:, 0], ALU.subtract).then_inc(q.a_plo, 1)
                if runs(k, 2):
                    row = qkraw[p][:, 0:D].rearrange("p (h d) -> p h d", h=XH)
                    po.wait_ge(q.a_qkn, k - 1)
                    po.tensor_tensor(row, row, gq.rearrange("p (h d) -> p h d", h=1).broadcast_to([P, XH, DH]),
                                     ALU.mult).then_inc(q.a_gq, 1)
                if runs(k, -2):
                    po.wait_ge(q.r_hi, k + 3)
                    if not isinstance(k, int) or k >= 0:
                        po.wait_ge(q.r_t, k + 1)
                    po.tensor_tensor(a_rl[:, p], a_rn[:, p], a_rh[:, p], ALU.subtract).then_inc(q.r_lo, 1)
                if runs(k, 2):
                    po.wait_ge(q.a_hi, k - 1)
                    po.tensor_tensor(qklo[p], qkraw[p], qkhi[p], ALU.subtract).then_inc(q.a_lo, 1)

            for k in range(-2, RUN.start):
                a_step(k, k % 2)
            with po.Fori(RUN.start, RUN.stop - 1, 2) as k:
                for p in range(2):
                    a_step(k + p, p)

            def b_scale(w1):
                po.wait_ge(q.b_ms, w1)
                po.tensor_tensor(sm2[:, :], sm1[:, :], neghalf[:, 0:AH], ALU.pow).then_inc(q.b_rr, G)

            def b_deviations(w1):
                po.wait_ge(q.b_ve, w1)
                po.tensor_tensor(crs, cve, neghalf[:, 0:G], ALU.pow).then_inc(q.b_rs, G)

            for k in range(RUN.stop, LAST):
                a_step(k, k % 2)
                if k in (AHEAD, AHEAD + 1):
                    b_deviations((k - AHEAD + 1) * G)
            po.wait_ge(q.r_n, RT)
            po.wait_ge(q.bk_ps, 1)
            po.wait_ge(q.split_lo, len(splits))
            po.memset(head_of_acc, 0.0).then_inc(q.acc_zero, 1)
            po.wait_ge(q.pos_sb, 3)
            count = po.value_load(wn[0:1, 0:1], min_val=1, max_val=NT)

            def b_low(w1, h):
                half = slice(0, G // 2)
                po.wait_ge(q.b_hi, w1 - G // 2)
                po.tensor_tensor(flat(xcl[h][:, half]), flat(xt[h][:, half]), flat(xch[h][:, half]),
                                 ALU.subtract).then_inc(q.b_lo, G)

            b_low(G, 0)
            b_low(2 * G, 1)
            b_scale(G)
            with po.Fori(0, count, 2 * G) as w:
                for h in range(2):
                    b_deviations(w + (h + 3) * G)
                    b_low(w + (h + 3) * G, h)
                    b_scale(w + (h + 2) * G)
            po.wait_ge(q.c_csum, 1)
            with po.Fori(0, RT - 1, 2) as n:
                for j in range(2):
                    po.wait_ge(q.c_uh, n + (j + 1))
                    for c in range(FC):
                        po.tensor_tensor(c_ul[j][:, c], acc_heads(n + j, c), c_uh[j][:, c], ALU.subtract).then_inc(q.c_ul, 1)
                    if j == 0:
                        po.wait_ge(q.c_on, n)
                    po.tensor_tensor(c_ub[j].rearrange("p (h d) -> p h d", h=XH),
                                     bv[:, :].rearrange("p (h d) -> p h d", h=XH),
                                     csum[:, ds(n + j, 1), :].rearrange("p t (h o) -> p (t h) o", o=1)
                                     .broadcast_to([P, XH, DH]), ALU.mult).then_inc(q.c_ub, 1)
            rows_norm(1)

            def block_deviations(count, at):
                po.wait_ge(q.r_ve, count)
                po.tensor_tensor(rstd[:, ds(at, BR)], var_eps[:, ds(at, BR)], neghalf[:, 0:BR], ALU.pow).then_inc(q.r_rs, 1)

            def d_step(k):
                if isinstance(k, int) and k == RT - 3:
                    block_deviations(4, 0)
                if norms(k):
                    po.wait_ge(q.r_hi, k + (RT + 4))
                    po.tensor_tensor(d_rl, d_rn[:, :], d_rh, ALU.subtract).then_inc(q.r_lo, 1)
                if runs(k, 0):
                    po.wait_ge(q.f_hi, k + 1)
                    po.tensor_tensor(wff[:, 1, ds(k * PIECE, PIECE)], wst, wff[:, 0, ds(k * PIECE, PIECE)],
                                     ALU.subtract).then_inc(q.f_lo, 1)

            for k in range(-3, D_RUN.start):
                d_step(k)
            with po.Fori(D_RUN.start, D_RUN.stop) as k:
                d_step(k)
            for k in range(D_RUN.stop, RT + 1):
                d_step(k)
            def e_block(n, ahead):
                for m in range(HC):
                    po.wait_ge(q.e_hi, HC * n + (m + 1))
                    po.tensor_tensor(hb[0][:, 1, m], hf[m % 2], hb[0][:, 0, m], ALU.subtract).then_inc(q.e_lo, 1)
                if ahead:
                    block_deviations(n + 5, n * BR + BR)
                    for i in range(BR):
                        po.wait_ge(q.r_hi, n * BR + (2 * RT + BR + i + 1))
                        po.tensor_tensor(d_rl, d_rn[:, :], d_rh, ALU.subtract).then_inc(q.r_lo, 1)

            with po.Fori(0, NB - 1) as n:
                e_block(n, True)
            e_block(NB - 1, False)

        @block.scalar
        def _(act):
            act.wait_ge(q.wstage_in, 16 * 2)
            for k, (full, parts) in enumerate(splits):
                if k == 1:
                    act.wait_ge(q.wkg, FC)
                act.activation(parts[:, 0], full, ACT.Copy).then_inc(q.split_hi, 1)
            act.wait_ge(q.small_in, 16 * 8)
            act.activation(bo[:, 0, :], bof[:, :], ACT.Copy).then_inc(q.bo_hi, 1)

            def a_step(k, p):
                loop = not isinstance(k, int)
                if runs(k, 5):
                    act.wait_ge(q.a_s, k - 4)
                    if loop or k > 6:
                        act.wait_ge(q.a_plo, k - 6)
                    act.activation(pl_a[1 - p], ps[5][:, 0:D], ACT.Exp).then_inc(q.a_p, 1)
                if runs(k, 4):
                    act.wait_ge(q.a_t, k - 3)
                    if loop or k > 5:
                        act.wait_ge(q.a_s, k - 5)
                    act.activation(klt[p], ps[6][:, :].rearrange("p (k n) -> p k n", k=4), ACT.Copy).then_inc(q.a_kt, 1)
                if runs(k, 0):
                    act.wait_ge(q.r_t, k + 1)
                    if loop or k > 1:
                        act.wait_ge(q.a_qkv, k - 1)
                    act.activation(aT[p].rearrange("p l c n -> p (l c n)"), ps[7][:, :].bitcast(BF16)[:, 0:4 * P],
                                   ACT.Copy).then_inc(q.r_e, 1)
                if runs(k, 0):
                    act.wait_ge(w_ld[p], 8 * k + (16 - 8 * p))
                    act.activation(wat[:, 0, ds(k * ATP, ATP)], st_at[p], ACT.Copy).then_inc(q.w_hi, 1)
                if runs(k, 5):
                    act.wait_ge(q.a_p, k - 4)
                    if loop or k > 6:
                        act.wait_ge(q.a_pst, 16 * k - 96)
                    act.activation(pls[1 - p][:, 0], pl_a[1 - p], ACT.Copy).then_inc(q.a_phi, 1)
                if runs(k, -2):
                    act.wait_ge(q.r_n, k + 3)
                    if loop or k >= 0:
                        act.wait_ge(q.r_t, k + 1)
                    act.activation(a_rh[:, p], a_rn[:, p], ACT.Copy).then_inc(q.r_hi, 1)
                if runs(k, 2):
                    act.wait_ge(q.a_gq, k - 1)
                    if loop or k > 3:
                        act.wait_ge(q.a_t, k - 3)
                    act.activation(qkhi[p], qkraw[p], ACT.Copy).then_inc(q.a_hi, 1)
                if runs(k, 1):
                    act.wait_ge(q.a_qkv, k)
                    if loop or k > 2:
                        act.wait_ge(q.a_ss, k - 2)
                    act.activation(sq2[1 - p], ps[2 * (1 - p)][:, :], ACT.Square).then_inc(q.a_sq, 1)
                    if loop or k > 2:
                        act.wait_ge(q.a_vst, 16 * k - 32)
                    act.activation(vst[1 - p][:, 0], ps[2 * (1 - p) + 1][:, 0:D], ACT.Copy).then_inc(q.a_vhi, 1)

            for k in range(-2, RUN.start):
                a_step(k, k % 2)
            with act.Fori(RUN.start, RUN.stop - 1, 2) as k:
                for p in range(2):
                    a_step(k + p, p)

            def b_high(w1, h, k, used):
                half = slice(k * G // 2, (k + 1) * G // 2)
                act.wait_ge(q.b_n, w1 - (1 - k) * G // 2)
                if used:
                    act.wait_ge(q.b_pv, w1 - 2 * G - (1 - k) * G // 2)
                act.activation(flat(xch[h][:, half]), flat(xt[h][:, half]), ACT.Copy).then_inc(q.b_hi, G // 2)

            for k in range(RUN.stop, LAST):
                a_step(k, k % 2)
                if k == AHEAD + 1:
                    b_high(G, 0, 0, False)
                    b_high(G, 0, 1, False)
                if k == AHEAD + 2:
                    b_high(2 * G, 1, 0, False)
            act.wait_ge(q.pos_sb, 3)
            act.wait_ge(q.list_sb, 4 + G)
            act.wait_ge(q.consts_bf, 1)
            act.wait_ge(q.bk_sb, 2)
            count = act.value_load(wn[0:1, 0:1], min_val=1, max_val=NT)

            def b_tokens(w1):
                act.wait_ge(q.b_t, w1)
                act.activation(xct[:, 0].rearrange("p c n -> p (c n)"), ps[0][:, :].bitcast(BF16),
                               ACT.Copy).then_inc(q.b_eh, G)

            def b_keys(w1):
                for c in range(HP):
                    act.wait_ge(q.b_k, w1 - (HP - 1 - c) * G // HP)
                    act.activation(ksq[:, c], ps[2 + c][:, :], ACT.Square,
                                   bias=bk[:, c:c + 1]).then_inc(q.b_ksq, G // HP)
                for c in range(HP):
                    act.activation(kct[:, 0, c], ps[2 + c][:, :], ACT.Identity,
                                   bias=bk[:, c:c + 1]).then_inc(q.b_khi, G // HP)

            def b_exp(w, columns):
                act.wait_ge(q.b_sn, w + G)
                act.wait_ge(q.b_pv, w)
                for k in range(2):
                    half = slice(k * G // 2, (k + 1) * G // 2)
                    for i in range(half.start, half.stop):
                        act.activation(pr[:, i], pr[:, i], ACT.Exp, bias=maskb[:, ds(columns[i], 1)]).then_inc(q.b_p, 1)
                    act.wait_ge(q.b_p, w + half.stop)
                    act.activation(flat(prh[:, half]), flat(pr[:, half]), ACT.Copy).then_inc(q.b_ph, G // 2)

            b_tokens(G)
            b_keys(G)
            with act.Fori(0, count, 2 * G) as w:
                for h in range(2):
                    at = w + h * G
                    columns = [act.value_load(wl[0:1, 1, ds(at + i, 1)], min_val=0, max_val=NT) for i in range(G)]
                    b_high(at + 2 * G, 1 - h, 1, True)
                    b_tokens(at + 2 * G)
                    b_exp(at, columns)
                    act.wait_ge(q.b_ss, at + G)
                    act.wait_ge(q.b_s, at + G)
                    b_keys(at + 2 * G)
                    b_high(at + 3 * G, h, 0, True)
            b_high(count + 2 * G, 1, 1, True)

            act.wait_ge(q.b_acc, count)
            act.wait_ge(q.b_lo, count + 2 * G)
            act.wait_ge(q.b_lo2, count + 2 * G)
            act.wait_ge(q.b_t, count + G)

            def c_high(n, j, first=False):
                if not first:
                    act.wait_ge(q.c_ot, n - 1)
                for c in range(FC):
                    last = act.activation(c_uh[j][:, c], acc_heads(n, c), ACT.Copy)
                last.then_inc(q.c_uh, 1)

            def c_out_high(n, j):
                act.wait_ge(q.c_on, n + 1)
                act.activation(c_oth[j], c_ot[j], ACT.Copy).then_inc(q.c_oh, 1)

            def c_transposed(n, j):
                act.wait_ge(q.c_t, n + 1)
                act.activation(c_otT[j].rearrange("p l c n -> p (l c n)"), ps[2 + j][:, :].bitcast(BF16)[:, 0:4 * P],
                               ACT.Copy).then_inc(q.c_te, 1)

            c_high(0, 0, first=True)
            c_high(1, 1, first=True)
            c_out_high(0, 0)
            with act.Fori(1, RT - 2, 2) as n:
                for j in range(2):
                    c_high(n + (j + 1), j)
                    c_transposed(n + (j - 1), j)
                    c_out_high(n + j, 1 - j)
            c_transposed(RT - 2, 0)
            c_out_high(RT - 1, 1)
            c_transposed(RT - 1, 1)
            def row_store(n, bank, at):
                act.wait_ge(q.r_t, at)
                act.activation(rowT[:, :, :, ds(n * P, P)],
                               ps[bank][:, :].bitcast(BF16)[:, 0:4 * P].rearrange("p (l c n) -> p l c n", l=2, c=FC),
                               ACT.Copy).then_inc(q.r_e, 1)

            def d_qk(n, c):
                act.wait_ge(q.d_qk, 4 * n + (c + 1))
                act.activation(qkh[:, 4 * c:4 * c + 4].rearrange("p c n -> p (c n)"), ps[QK_BANKS[c]][:, :], ACT.Copy,
                               scale=SCALE if c < 2 else 1.0).then_inc(q.d_qhi, 1)

            def d_step(k, p):
                if runs(k, 0):
                    for l, done in enumerate((q.d_peh, q.d_pel)):
                        act.wait_ge(q.d_pt, 2 * k + (l + 1))
                        act.activation(pT[:, l].rearrange("p c n -> p (c n)"), ps[4 + l][:, :].bitcast(BF16),
                                       ACT.Copy).then_inc(done, 1)
                if norms(k):
                    act.wait_ge(q.r_n, k + (RT + 4))
                    act.wait_ge(q.r_t, k + (RT + 3))
                    act.activation(d_rh, d_rn[:, :], ACT.Copy).then_inc(q.r_hi, 1)
                if runs(k, 0):
                    act.wait_ge(q.f_ld, 16 * k + 16)
                    act.activation(wff[:, 0, ds(k * PIECE, PIECE)], wst, ACT.Copy).then_inc(q.f_hi, 1)
                if runs(k, -1):
                    for c in range(2):
                        act.wait_ge(q.d_v, 2 * k + (c + 3))
                        act.activation(vh[1 - p][:, c * 512:c * 512 + 512], ps[c][:, :], ACT.Copy).then_inc(q.d_vhi, 1)
                    act.wait_ge(q.d_sub, k + 2)
                    act.activation(flat(sc), flat(sc), ACT.Exp).then_inc(q.d_ex, 1)
                if runs(k, 0):
                    act.wait_ge(q.d_pv, k + 1)
                    for b in range(2):
                        act.activation(ath[:, :, b * S:b * S + S], ps[6 + b][:, :].rearrange("p (c n) -> p c n", c=AP_),
                                       ACT.Copy).then_inc(q.d_ahi, 1)
                if runs(k, -2):
                    d_qk(k + 2, 0)
                    d_qk(k + 2, 1)
                if runs(k, -1):
                    act.wait_ge(q.d_pn, k + 2)
                    act.activation(flat(sph), flat(sc), ACT.Copy).then_inc(q.d_phi, 1)
                if runs(k, -2):
                    d_qk(k + 2, 2)
                    d_qk(k + 2, 3)
                if norms(k):
                    row_store((k + 3) % RT if isinstance(k, int) else k + 3, 0, k + (RT + 4))

            for k in range(-3, D_RUN.start):
                d_step(k, k % 2)
            with act.Fori(D_RUN.start, D_RUN.stop - 1, 2) as k:
                for i in range(2):
                    d_step(k + i, 1 - i)
            for k in range(D_RUN.stop, RT + 1):
                d_step(k, k % 2)
            def e_block(n, ahead):
                for m in range(HC):
                    act.wait_ge(q.e_1, HC * n + (m + 1))
                    if m < 2:
                        act.wait_ge(q.e_hf, HC * n)
                    else:
                        act.wait_ge(q.e_hf, HC * n + (m - 1))
                    act.activation(sil[m % 2], ps[2 * (m % 2)][:, :], ACT.Silu,
                                   scale=hs[:, 0, m:m + 1]).then_inc(q.e_sil, 1)
                for layer, (ready, done) in enumerate(((q.e_h1, q.e_g1), (q.e_h2, q.e_g2))):
                    for m in range(HC):
                        tile = layer * HC + m - 1
                        if ahead and 0 < tile <= BR:
                            row_store(n * BR + (BR + tile - 1), (tile - 1) % 2, n * BR + (2 * RT + BR + tile))
                        if ahead and 0 <= tile < BR:
                            act.wait_ge(q.r_n, n * BR + (2 * RT + BR + tile + 1))
                            act.activation(d_rh, d_rn[:, :], ACT.Copy).then_inc(q.r_hi, 1)
                        act.wait_ge(ready, HC * n + (m + 1))
                        act.activation(hb[1 - layer][:, 0, m], ps[4 + m % 2][:, :], ACT.Gelu,
                                       scale=hs[:, 2 + layer, m:m + 1])
                        if m < 2 and layer == 0:
                            act.wait_ge(q.e_lo, HC * n + HC)
                        else:
                            act.wait_ge(q.e_glo, 2 * HC * n + (HC * layer + m - 1))
                        act.activation(hf[m % 2], ps[4 + m % 2][:, :], ACT.Gelu,
                                       scale=hs[:, 2 + layer, m:m + 1]).then_inc(done, 1)

            with act.Fori(0, NB - 1) as n:
                e_block(n, True)
            e_block(NB - 1, False)

        @block.vector
        def _(v):
            rows_moments, group_moments = (q.m_halves, q.m_terms), (q.n_halves, q.n_terms)

            def moments(st, to, var, sems, k, done, step=1):
                halves, terms = sems
                n = st.shape[1]
                dif, dev, spread = mt[:, 0, 0:n], mt[:, 1, 0:n], mt[:, 2, 0:n]
                v.tensor_tensor(to[:, :, 0], st[:, :, 1], st[:, :, 4], ALU.add).then_inc(halves, step)
                v.tensor_tensor(dif, st[:, :, 1], st[:, :, 4], ALU.subtract).then_inc(halves, step)
                v.tensor_tensor(dev, st[:, :, 2], st[:, :, 5], ALU.add).then_inc(halves, step)
                v.wait_ge(halves, 3 * k)
                v.tensor_scalar(to[:, :, 0], to[:, :, 0], 0.5, None, ALU.mult).then_inc(terms, step)
                v.scalar_tensor_tensor(spread, dif, 0.25, dif, ALU.mult, ALU.mult).then_inc(terms, step)
                v.tensor_scalar(dev, dev, 1.0 / D, LN_EPS, ALU.mult, ALU.add).then_inc(terms, step)
                v.wait_ge(terms, 3 * k)
                v.tensor_tensor(var, dev, spread, ALU.add).then_inc(done, step)

            v.wait_ge(q.work_in, 16 * 8)
            v.tensor_copy(maskbf, mask8).then_inc(q.maskbf, 1)
            v.wait_ge(q.maskbf, 1)
            v.tensor_scalar(maskb[:, :], maskbf, 1.0, -MASKED, ALU.subtract, ALU.mult).then_inc(q.consts_bf, 1)
            v.tensor_copy(tri, trif).then_inc(q.consts_bf, 1)
            v.tensor_copy(code, codef).then_inc(q.consts_bf, 1)
            v.tensor_copy(ident[:, :], identf).then_inc(q.consts_bf, 1)
            v.wait_ge(q.ps_set, 1)
            v.tensor_scalar(actf, ps[6][0:ER, 0:EC], 1.0, None, ALU.min).then_inc(q.act, 1)
            v.tensor_scalar(actb, ps[6][0:ER, 0:EC], 1.0, None, ALU.min).then_inc(q.act, 1)
            v.wait_ge(q.ps_set, 2)
            v.tensor_copy(pos, ps[6][0:ER, 8:8 + EC]).then_inc(q.pos_sb, 1)
            v.tensor_scalar(wn[:, :], ps[6][0:1, 16:17], 1.0, 2.0 * G - 1, ALU.max, ALU.add).then_inc(q.pos_sb, 1)
            v.wait_ge(q.pos_sb, 2)
            v.tensor_scalar(wn[:, :], wn[:, :], -2 * G, None, ALU.bitwise_and).then_inc(q.pos_sb, 1)
            for c in range(EC):
                v.tensor_scalar(hot[:, c], iota, pos[:, c:c + 1], actf[:, c:c + 1],
                                ALU.is_equal, ALU.mult).then_inc(q.hot, 1)
            v.wait_ge(q.const_set, 5)
            v.wait_ge(q.ps_set, 4)
            batch = ps[6][0:1, 0:NT]
            v.tensor_copy(wl[:, 0, 0:NT], batch).then_inc(q.list_sb, 1)
            v.tensor_copy(tile1, ps[7][0:1, 0:NT]).then_inc(q.list_sb, 1)
            v.tensor_scalar(row128, ps[7][0:1, 0:NT], float(P), None, ALU.mult).then_inc(q.list_sb, 1)
            v.wait_ge(q.list_sb, 3)
            v.scalar_tensor_tensor(wl[:, 1, 0:NT], batch, float(KT), tile1, ALU.mult, ALU.add).then_inc(q.list_sb, 1)
            v.scalar_tensor_tensor(wl[:, 2, 0:NT], batch, float(SC), row128, ALU.mult, ALU.add).then_inc(q.list_sb, 1)
            groups = wl[:, :, 0:NT].rearrange("o k (g i) -> o k g i", i=G)
            for i in range(G - 1, 0, -1):
                high = groups[:, 0, :, G - 1] if i == G - 1 else groups[:, 3, :, 0]
                v.scalar_tensor_tensor(groups[:, 3, :, 0], high, float(1 << BB), groups[:, 0, :, i - 1],
                                       ALU.mult, ALU.add).then_inc(q.list_sb, 1)
                v.wait_ge(q.list_sb, 5 + G - i)
            v.wait_ge(q.x_in, 16)

            def rows_stats(k, src):
                with v.Fori(0, RT - 3, 4) as n:
                    for j in range(4):
                        v.bn_stats(flat(stats[:, ds(n + j, 1), :]), flat(src[:, ds(n + j, 1), :])).then_inc(q.r_st, 1)
                v.wait_ge(q.r_st, (k + 2) * RT)
                moments(stats, mv, var_eps[:, :], rows_moments, k + 2, q.r_ve)

            rows_stats(-1, xres)
            v.wait_ge(q.small_in, 16 * 8)
            v.wait_ge(q.wstage_in, 16 * 2)
            for c in range(FC):
                v.tensor_scalar(wkg[:, c], st_qkv[:, c, D:3 * D], lnx[:, 0, c:c + 1], None, ALU.mult).then_inc(q.wkg, 1)
            for c in range(FC):
                v.tensor_scalar(lnx_b[:, c], onesb[:, :], lnx[:, 1, c:c + 1], None, ALU.mult).then_inc(q.wkg, 1)
            v.wait_ge(q.r_rs, 1)
            with v.Fori(0, RT - 3, 4) as n:
                for j in range(4):
                    v.tensor_scalar(flat(xn1[:, ds(n + j, 1), :]), flat(xres[:, ds(n + j, 1), :]), mv[:, ds(n + j, 1), 0],
                                    rstd[:, ds(n + j, 1)], ALU.subtract, ALU.mult).then_inc(q.x1_n, 1)
                v.wait_ge(q.x1_n, n + 4)
                for j in range(4):
                    v.bn_stats(flat(stats[:, ds(n + j, 1), :]), flat(xn1[:, ds(n + j, 1), :])).then_inc(q.r_st, 1)
            v.wait_ge(q.r_st, 2 * RT)
            moments(stats, mv, var_eps[:, :], rows_moments, 2, q.r_ve)
            for k, (full, parts) in enumerate(splits):
                v.wait_ge(q.split_hi, k + 1)
                v.tensor_tensor(parts[:, 1], full, parts[:, 0], ALU.subtract).then_inc(q.split_lo, 1)
            v.wait_ge(q.bo_hi, 1)
            v.tensor_tensor(bo[:, 1, :], bof[:, :], bo[:, 0, :], ALU.subtract).then_inc(q.bo_lo, 1)
            v.wait_ge(q.bk_ps, 1)
            v.tensor_copy(bk[:, :], ps[6][:, 0:HP]).then_inc(q.bk_sb, 1)
            v.tensor_copy(bv[:, :], ps[7][:, 0:D]).then_inc(q.bk_sb, 1)
            v.wait_ge(q.bias_ps, 1)
            for k in range(2):
                for h in range(2):
                    r = slice(h * S, h * S + S)
                    v.tensor_copy(bias[r, :, k * 32:k * 32 + 32],
                                  ps[k][r, :].rearrange("p (j c h) -> p c h j", c=AP_, h=2)[:, :, h, :]
                                  ).then_inc(q.bias_sb, 1)

            def a_step(k, p):
                loop = not isinstance(k, int)
                if runs(k, 4):
                    v.wait_ge(q.a_t, k - 3)
                    if loop or k > 5:
                        v.wait_ge(q.a_qst, 16 * k - 80)
                        v.wait_ge(q.a_s, k - 5)
                    for h in range(2):
                        r = slice(h * S, h * S + S)
                        v.tensor_copy(qpair[p][r, :, :, h * S:h * S + S],
                                      ps[4][r, :].rearrange("p (k b n) -> p b k n", k=4, b=2)).then_inc(q.a_qp, 1)
                if runs(k, -2):
                    n = k + 2
                    if loop or k >= 0:
                        v.wait_ge(q.r_lo, k + 1)
                    v.scalar_tensor_tensor(a_rn[:, p], flat(xn1[:, ds(n, 1), :]), mv[:, ds(n, 1), 0], lng,
                                           ALU.subtract, ALU.mult).then_inc(q.r_g, 1)
                    v.wait_ge(q.r_g, k + 3)
                    v.scalar_tensor_tensor(a_rn[:, p], a_rn[:, p], rstd[:, ds(n, 1)], lnb,
                                           ALU.mult, ALU.add).then_inc(q.r_n, 1)
                if runs(k, 2):
                    row = qkraw[p].rearrange("p (h d) -> p h d", d=DH)
                    v.wait_ge(q.a_rr, k - 1)
                    v.tensor_tensor(row, row, rr[:, ds(k * 8 - 16, 8)].rearrange("p (h o) -> p h o", o=1)
                                    .broadcast_to([P, 8, DH]), ALU.mult).then_inc(q.a_qkn, 1)
                if runs(k, 0):
                    v.wait_ge(q.w_hi, k + 1)
                    v.tensor_tensor(wat[:, 1, ds(k * ATP, ATP)], st_at[p], wat[:, 0, ds(k * ATP, ATP)],
                                    ALU.subtract).then_inc(q.w_lo, 1)
                if runs(k, 1):
                    j = 1 - p
                    v.wait_ge(q.a_sq, k)
                    if loop or k > 2:
                        v.wait_ge(q.a_lo, k - 2)
                    v.tensor_copy(qkraw[j], ps[2 * j][:, :]).then_inc(q.a_raw, 1)
                    v.tensor_reduce(ss[:, ds(k * 8 - 8, 8)], sq2[j].rearrange("p (h d) -> p h d", d=DH),
                                    AX.X, ALU.add).then_inc(q.a_ss, 1)
                    v.wait_ge(q.a_vhi, k)
                    v.tensor_tensor(vst[j][:, 1], ps[2 * j + 1][:, 0:D], vst[j][:, 0], ALU.subtract).then_inc(q.a_vlo, 1)
                    v.wait_ge(q.a_ss, k)
                    v.tensor_scalar(ss[:, ds(k * 8 - 8, 8)], ss[:, ds(k * 8 - 8, 8)], 1.0 / DH, RMS_FLOOR,
                                    ALU.mult, ALU.max).then_inc(q.a_ms, 1)

            v.wait_ge(q.r_rs, 2)
            for k in range(-2, RUN.start):
                a_step(k, k % 2)
            with v.Fori(RUN.start, RUN.stop - 1, 2) as k:
                for p in range(2):
                    a_step(k + p, p)

            def b_stats(w1, h):
                v.wait_ge(b_ld[h], 8 * w1 + (1 - h) * 8 * G)
                for i in range(G):
                    v.bn_stats(cst[:, i], xt[h][:, i]).then_inc(q.b_st, 1)

            def b_moments(w1):
                v.wait_ge(q.b_st, w1)
                moments(cst, cmv, cve, group_moments, w1, q.b_ve, G)

            def b_norm(w1, h, k):
                v.wait_ge(q.b_rs, w1)
                for i in range(k * G // 2, (k + 1) * G // 2):
                    v.tensor_scalar(xt[h][:, i], xt[h][:, i], cmv[:, i, 0:1], crs[:, i:i + 1],
                                    ALU.subtract, ALU.mult).then_inc(q.b_n, 1)

            for k in range(RUN.stop, LAST):
                a_step(k, k % 2)
                if k in (AHEAD + 1, AHEAD + 2):
                    for half in range(2):
                        b_norm((k - AHEAD) * G, k - AHEAD - 1, half)
                if k in (AHEAD, AHEAD + 1):
                    b_stats((k - AHEAD + 1) * G, k - AHEAD)
                    b_moments((k - AHEAD + 1) * G)

            count = v.value_load(wn[0:1, 0:1], min_val=1, max_val=NT)

            def b_tokens(w1):
                v.wait_ge(q.b_tl, w1)
                v.tensor_copy(xct[:, 1].rearrange("p c n -> p (c n)"), ps[1][:, :].bitcast(BF16)).then_inc(q.b_el, G)

            def b_keys(w1, c):
                v.wait_ge(q.b_khi, w1 - G // HP * (HP - 1 - c))
                v.scalar_tensor_tensor(kct[:, 1, c], ps[2 + c][:, :], bk[:, c:c + 1], kct[:, 0, c],
                                       ALU.add, ALU.subtract).then_inc(q.b_klo, G // HP)

            def b_mean_squares(w1):
                v.wait_ge(q.b_ss, w1)
                v.tensor_scalar(sm1[:, :], ps[6][:, 0:AH], 1.0 / DH, RMS_FLOOR, ALU.mult, ALU.max).then_inc(q.b_ms, G)

            def b_scores(w1):
                v.wait_ge(q.b_rr, w1)
                for k in range(2):
                    v.wait_ge(q.b_s, w1 - (1 - k) * G // 2)
                    v.tensor_tensor(pr[:, 2 * k:2 * k + 2].rearrange("p i (h n) -> p (i h) n", n=S),
                                    ps[5 + k][:, :].rearrange("p (k n) -> p k n", n=S),
                                    sm2[:, 8 * k:8 * k + 8].rearrange("p (k o) -> p k o", o=1).broadcast_to([P, 8, S]),
                                    ALU.mult).then_inc(q.b_sn, G // 2)

            def b_low_second(w1, h):
                half = slice(G // 2, G)
                v.wait_ge(q.b_hi, w1)
                v.tensor_tensor(flat(xcl[h][:, half]), flat(xt[h][:, half]), flat(xch[h][:, half]),
                                ALU.subtract).then_inc(q.b_lo2, G)

            def b_low(w, k):
                half = slice(k * G // 2, (k + 1) * G // 2)
                v.wait_ge(q.b_ph, w + half.stop)
                v.tensor_tensor(flat(prl[:, half]), flat(pr[:, half]), flat(prh[:, half]),
                                ALU.subtract).then_inc(q.b_pl, G // 2)

            def b_sum(w, i, batch):
                v.wait_ge(q.b_pv, w + (i + 1))
                v.wait_ge(q.b_acc, w + i)
                sums, ones = acc[:, ds(batch, 1), :], accs[:, ds(batch, 1), :]
                v.tensor_tensor(flat(sums), flat(sums), ps[0 if i % 2 == 0 else 7][:, :], ALU.add)
                v.tensor_tensor(flat(ones), flat(ones), ps[1 if i % 2 == 0 else 4][:, 0:HP], ALU.add).then_inc(q.b_acc, 1)

            v.wait_ge(q.acc_zero, 2)
            b_low_second(G, 0)
            b_tokens(G)
            for c in range(HP):
                b_keys(G, c)
            b_mean_squares(G)
            b_low_second(2 * G, 1)
            with v.Fori(0, count, 2 * G) as w:
                for h in range(2):
                    at = w + h * G
                    b_scores(at + G)
                    packed = v.value_load(wl[0:1, 3, ds(at, 1)], min_val=0, max_val=(1 << BB * G) - 1)
                    batches = [v.snap((packed >> BB * i) & (B - 1)) for i in range(G)]
                    b_tokens(at + 2 * G)
                    b_stats(at + 3 * G, h)
                    b_low(at, 0)
                    b_moments(at + 3 * G)
                    b_low(at, 1)
                    b_norm(at + 3 * G, h, 0)
                    b_sum(at, 0, batches[0])
                    b_norm(at + 3 * G, h, 1)
                    b_mean_squares(at + 2 * G)
                    b_sum(at, 1, batches[1])
                    for c in range(HP):
                        b_keys(at + 2 * G, c)
                    for i in range(2, G - 1):
                        b_sum(at, i, batches[i])
                    b_low_second(at + 3 * G, h)
                    b_sum(at, G - 1, batches[G - 1])
            v.wait_ge(q.b_acc, count)

            for j in range(2):
                for b in range(2):
                    v.memset(c_pb[j][b * S:b * S + S, :, :, 1 - b, :].rearrange("p l h n -> p (l h) n"), 0.0
                             ).then_inc(q.c_zero, 1)
            v.wait_ge(q.c_sums, 1)
            v.tensor_copy(csum.rearrange("p t (k h) -> p h t k", h=2),
                          ps[6][:, 0:RT * XH].rearrange("p (h t k) -> p h t k", h=2, t=RT)).then_inc(q.c_csum, 1)

            def row_stats(n):
                v.bn_stats(flat(stats[:, ds(n, 1), :]), flat(xres[:, ds(n, 1), :])).then_inc(q.r_st, 1)

            def c_normalise(n, j):
                v.wait_ge(q.c_ot, n + 1)
                v.tensor_tensor(sm1[:, 0:XH], ps[j][:, D:D + XH], flat(csum[:, ds(n, 1), :]), ALU.add).then_inc(q.c_step, 1)
                v.wait_ge(q.c_ub, n + 1)
                v.tensor_tensor(c_ot[j], ps[j][:, 0:D], c_ub[j], ALU.add).then_inc(q.c_step, 1)
                v.wait_ge(q.c_step, 3 * n + 2)
                v.reciprocal(sm2[:, 0:XH], sm1[:, 0:XH]).then_inc(q.c_step, 1)
                v.wait_ge(q.c_step, 3 * n + 3)
                heads_ = c_ot[j].rearrange("p (h d) -> p h d", h=XH)
                v.tensor_tensor(heads_, heads_, sm2[:, 0:XH].rearrange("p (h o) -> p h o", o=1)
                                .broadcast_to([P, XH, DH]), ALU.mult).then_inc(q.c_on, 1)

            def c_low(n, j):
                v.wait_ge(q.c_oh, n + 1)
                v.tensor_tensor(c_otl[j], c_ot[j], c_oth[j], ALU.subtract).then_inc(q.c_ol, 1)

            def c_residual(n, j):
                v.wait_ge(q.c_o, n + 1)
                v.tensor_tensor(flat(xres[:, ds(n, 1), :]), flat(xres[:, ds(n, 1), :]), ps[4 + j][:, 0:D],
                                ALU.add).then_inc(q.c_x, 1)
                v.wait_ge(q.c_x, n + 1)
                row_stats(n)

            for j in range(2):
                c_normalise(j, j)
                c_low(j, j)
            with v.Fori(2, RT - 1, 2) as n:
                for j in range(2):
                    c_normalise(n + j, j)
                    c_residual(n + (j - 2), j)
                    c_low(n + j, j)
            for j in range(2):
                c_residual(RT - 2 + j, j)

            v.wait_ge(q.r_st, 3 * RT)
            moments(stats, mv, var_eps[:, :], rows_moments, 3, q.r_ve)
            v.wait_ge(q.r_rs, 3)

            def d_qk(n, c):
                v.wait_ge(q.d_qhi, 4 * n + (c + 1))
                v.scalar_tensor_tensor(qkl[:, 4 * c:4 * c + 4].rearrange("p c n -> p (c n)"), ps[QK_BANKS[c]][:, :],
                                       SCALE if c < 2 else 1.0,
                                       qkh[:, 4 * c:4 * c + 4].rearrange("p c n -> p (c n)"),
                                       ALU.mult, ALU.subtract).then_inc(q.d_qlo, 1)

            def d_low_max(n):
                v.wait_ge(q.f_lo, n + 1)
                v.tensor_reduce(lowmax[:, ds(n, 1)], wff[:, 1, ds(n * PIECE, PIECE)], AX.X, ALU.max,
                                apply_absolute_value=True).then_inc(q.f_max, 1)

            def heads(values):
                return values[:, :].rearrange("p (k o) -> p k o", o=1).broadcast_to([P, AH, S])

            def d_out(n):
                v.wait_ge(q.d_o, n + 1)
                v.tensor_tensor(flat(xres[:, ds(n, 1), :]), flat(xres[:, ds(n, 1), :]), ps[5][:, 0:D],
                                ALU.add).then_inc(q.d_x, 1)
                v.wait_ge(q.d_x, n + 1)
                row_stats(n)

            def row_norm(n, before):
                v.wait_ge(q.r_lo, before)
                v.tensor_scalar(d_rn[:, :], flat(xres[:, ds(n, 1), :]), mv[:, ds(n, 1), 0],
                                rstd[:, ds(n, 1)], ALU.subtract, ALU.mult).then_inc(q.r_n, 1)

            def block_moments(count, at):
                v.wait_ge(q.r_st, 3 * RT + BR + at)
                tiles = ds(at, BR)
                moments(stats[:, tiles, :], mv[:, tiles, :], var_eps[:, tiles], rows_moments, count, q.r_ve)

            def d_step(k, p):
                if runs(k, 1):
                    d_out(k - 1)
                if isinstance(k, int) and k == RT - 3:
                    block_moments(4, 0)
                    v.wait_ge(q.r_rs, 4)
                if norms(k):
                    row_norm((k + 3) % RT if isinstance(k, int) else k + 3, k + (RT + 3))
                if runs(k, -1):
                    v.wait_ge(q.d_s, k + 2)
                    for c in range(2):
                        v.tensor_tensor(sc[:, 8 * c:8 * c + 8].rearrange("p (c b) n -> p c b n", b=2),
                                        ps[2 + c][:, :].rearrange("p (c b n) -> p c b n", c=4, b=2),
                                        bias[:, 4 * c:4 * c + 4, :].rearrange("p c (o n) -> p c o n", o=1)
                                        .broadcast_to([P, 4, 2, S]), ALU.add).then_inc(q.d_sb, 1)
                    v.wait_ge(q.d_sb, 2 * k + 4)
                    v.tensor_reduce(sm1[:, :], sc, AX.X, ALU.max).then_inc(q.d_stat, 1)
                    v.wait_ge(q.d_stat, 3 * k + 4)
                    v.tensor_tensor(sc, sc, heads(sm1), ALU.subtract).then_inc(q.d_sub, 1)
                    for c in range(2):
                        v.wait_ge(q.d_vhi, 2 * k + (c + 3))
                        v.tensor_tensor(vlo[1 - p][:, c * 512:c * 512 + 512], ps[c][:, :],
                                        vh[1 - p][:, c * 512:c * 512 + 512], ALU.subtract).then_inc(q.d_vlo, 1)
                    v.wait_ge(q.d_ex, k + 2)
                    v.tensor_reduce(sm2[:, :], sc, AX.X, ALU.add).then_inc(q.d_stat, 1)
                    v.wait_ge(q.d_stat, 3 * k + 5)
                    v.reciprocal(sm3[:, :], sm2[:, :]).then_inc(q.d_stat, 1)
                if runs(k, 0):
                    for b in range(2):
                        v.wait_ge(q.d_ahi, 2 * k + (b + 1))
                        v.tensor_tensor(atl[:, :, b * S:b * S + S], ps[6 + b][:, :].rearrange("p (c n) -> p c n", c=AP_),
                                        ath[:, :, b * S:b * S + S], ALU.subtract).then_inc(q.d_alo, 1)
                if runs(k, -1):
                    v.wait_ge(q.d_stat, 3 * k + 6)
                    v.tensor_tensor(sc, sc, heads(sm3), ALU.mult).then_inc(q.d_pn, 1)
                if runs(k, -2):
                    d_qk(k + 2, 0)
                    d_qk(k + 2, 1)
                if runs(k, -1):
                    v.wait_ge(q.d_phi, k + 2)
                    v.tensor_tensor(spl.rearrange("p c n -> p (c n)"), flat(sc), sph.rearrange("p c n -> p (c n)"),
                                    ALU.subtract).then_inc(q.d_plo, 1)
                if runs(k, -2):
                    d_qk(k + 2, 2)
                    d_qk(k + 2, 3)
                if runs(k, 0):
                    d_low_max(k)

            for k in range(-3, D_RUN.start):
                d_step(k, k % 2)
            with v.Fori(D_RUN.start, D_RUN.stop - 1, 2) as k:
                for i in range(2):
                    d_step(k + i, 1 - i)
            for k in range(D_RUN.stop, RT + 1):
                d_step(k, k % 2)

            v.wait_ge(q.f_max, RT)
            v.tensor_reduce(sm1[:, 0:1], lowmax[:, :], AX.X, ALU.max).then_inc(q.f_max, 1)
            v.wait_ge(q.f_max, RT + 1)
            v.tensor_scalar(lowany[:, :], sm1[:, 0:1], 0.0, None, ALU.is_gt).then_inc(q.f_any, 1)
            v.wait_ge(q.f_count, 1)
            v.tensor_copy(lown[:, :], ps[4][0:1, 0:1]).then_inc(q.f_known, 1)
            def e_block(n, ahead):
                for m in range(HC):
                    v.wait_ge(q.e_sil, HC * n + (m + 1))
                    if m < 2:
                        v.wait_ge(q.e_glo, 2 * HC * n)
                    else:
                        v.wait_ge(q.e_lo, HC * n + (m - 1))
                    v.scalar_tensor_tensor(hf[m % 2], ps[2 * (m % 2) + 1][:, :], hs[:, 1, m:m + 1], sil[m % 2],
                                           ALU.mult, ALU.mult).then_inc(q.e_hf, 1)
                    v.wait_ge(q.e_o, BR * n)
                    v.wait_ge(q.e_hf, HC * n + (m + 1))
                    v.tensor_copy(hb[0][:, 0, m], hf[m % 2]).then_inc(q.e_hi, 1)
                if ahead:
                    block_moments(n + 5, n * BR + BR)
                for layer, ready in enumerate((q.e_g1, q.e_g2)):
                    for m in range(HC):
                        v.wait_ge(ready, HC * n + (m + 1))
                        v.tensor_tensor(hb[1 - layer][:, 1, m], hf[m % 2], hb[1 - layer][:, 0, m],
                                        ALU.subtract).then_inc(q.e_glo, 1)
                        if ahead and layer == 0 and m < BR:
                            if m == 0:
                                v.wait_ge(q.r_rs, n + 5)
                            row_norm(n * BR + (BR + m), n * BR + (2 * RT + BR + m))
                for r in range(BR):
                    v.wait_ge(q.e_o, BR * n + (r + 1))
                    v.wait_ge(e_out[r % 2], 8 * BR * n + 8 * (r - r % 2))
                    v.tensor_tensor(fo[r % 2][:, :], ps[6 + r % 2][:, 0:D], w3s[:, :], ALU.mult).then_inc(q.e_os, 1)
                    v.wait_ge(q.e_os, BR * n + (r + 1))
                    v.tensor_tensor(fo[r % 2][:, :], fo[r % 2][:, :], flat(xres[:, ds(n * BR + r, 1), :]),
                                    ALU.add).then_inc(q.e_or, 1)

            with v.Fori(0, NB - 1) as n:
                e_block(n, True)
            e_block(NB - 1, False)

        @block.tensor
        def _(pe):
            def product(to, pairs, start=True, passes=PASSES):
                last, k = None, 0
                for left, right in pairs:
                    for l, r in passes:
                        last = pe.matmul(to, left(l), right(r), start=start and k == 0,
                                         stop=k == len(pairs) * len(passes) - 1)
                        k += 1
                return last

            pe.wait_ge(q.maskbf, 1)
            pe.wait_ge(q.const_set, 5)
            for c in range(EC):
                last = pe.matmul(ps[6][0:ER, c:c + 1], maskbf[:, 1 + c * ER:1 + (c + 1) * ER], onesb[:, 0:1],
                                 start=True, stop=True)
            last.then_inc(q.ps_set, 1)
            pe.wait_ge(q.act, 2)
            pe.wait_ge(q.consts_bf, 4)
            for c in range(EC):
                pe.matmul(ps[6][0:ER, 8 + c:9 + c], tri, actb[:, c:c + 1], start=True, stop=c == 0)
                for b in range(c):
                    pe.matmul(ps[6][0:ER, 8 + c:9 + c], onesb[0:ER, 0:ER], actb[:, b:b + 1], start=False, stop=b == c - 1)
            for c in range(EC):
                last = pe.matmul(ps[6][0:1, 16:17], onesb[0:ER, 0:1], actb[:, c:c + 1], start=c == 0, stop=c == EC - 1)
            last.then_inc(q.ps_set, 1)
            pe.wait_ge(q.hot, EC)
            pe.wait_ge(q.pos_sb, 2)
            for k in range(2):
                for c in range(EC):
                    last = pe.matmul(ps[6 + k][0:1, 0:NT], code[:, k * EC + c:k * EC + c + 1], hot[:, c],
                                     start=c == 0, stop=c == EC - 1)
                last.then_inc(q.ps_set, 1)
            pe.wait_ge(q.work_in, 16 * 8)
            for j in range(S):
                for h in range(2):
                    last = pe.matmul(ps[j // 32][h * S:h * S + S, (j % 32) * AH:(j % 32) * AH + AH],
                                     buck[:, S - 1 - j:2 * S - 1 - j], emb, start=True, stop=True)
            last.then_inc(q.bias_ps, 1)
            pe.wait_ge(q.small_in, 16 * 8)
            pe.wait_ge(q.wstage_in, 16 * 2)
            pe.wait_ge(q.list_sb, 4 + G)
            for h in range(HP):
                for c in range(FC):
                    pe.matmul(ps[6][:, h:h + 1], st_qkv[:, c, D + h * P:D + (h + 1) * P], lnx[:, 1, c:c + 1],
                              start=c == 0, stop=c == FC - 1)
            pe.wait_ge(q.wkg, 2 * FC)
            for c in range(FC):
                last = pe.matmul(ps[7][:, 0:D], lnx_b[:, c], st_qkv[:, c, 2 * D:3 * D], start=c == 0, stop=c == FC - 1)
            last.then_inc(q.bk_ps, 1)

            def a_step(k, p):
                loop = not isinstance(k, int)
                if runs(k, 0):
                    pe.wait_ge(q.r_lo, k + 1)
                    if loop or k > 0:
                        pe.wait_ge(q.r_e, k)
                    for l, part in enumerate((a_rh, a_rl)):
                        for c in range(FC):
                            at = (l * FC + c) * P
                            last = pe.transpose(ps[7][:, :].bitcast(BF16)[:, at:at + P], part[:, p, c * P:(c + 1) * P],
                                                ident[:, :])
                    last.then_inc(q.r_t, 1)
                if runs(k, 1):
                    j = 1 - p
                    pe.wait_ge(q.r_e, k)
                    if loop or k > 2:
                        pe.wait_ge(q.a_raw, k - 2)
                        pe.wait_ge(q.a_vlo, k - 2)
                    product(ps[2 * j][:, :], [(lambda l, c=c: aT[j][:, l, c, :], lambda r, c=c: wqkv[:, r, c, 0:2 * D])
                                              for c in range(FC)])
                    product(ps[2 * j + 1][:, 0:D], [(lambda l, c=c: aT[j][:, l, c, :],
                                                     lambda r, c=c: wqkv[:, r, c, 2 * D:3 * D])
                                                    for c in range(FC)]).then_inc(q.a_qkv, 1)
                if runs(k, 3):
                    j = 1 - p
                    pe.wait_ge(q.a_lo, k - 2)
                    if loop or k > 3:
                        pe.wait_ge(q.a_qp, 2 * k - 6)
                        pe.wait_ge(q.a_kt, k - 3)
                    for kind in range(2):
                        for l, part in enumerate((qkhi[j], qklo[j])):
                            for h in range(HP):
                                last = pe.matmul(ps[4 + 2 * kind][:, (2 * l + h) * P:(2 * l + h + 1) * P],
                                                 part[:, kind * D + h * P:kind * D + (h + 1) * P],
                                                 ident[:, :], start=True, stop=True)
                    last.then_inc(q.a_t, 1)
                if runs(k, 4):
                    pe.wait_ge(q.a_kt, k - 3)
                    pe.wait_ge(q.a_qp, 2 * k - 6)
                    if loop or k > 4:
                        pe.wait_ge(q.a_p, k - 4)
                    for b in range(2):
                        for h in range(HP):
                            last = product(ps[5][b * S:b * S + S, h * P:(h + 1) * P],
                                           [(lambda l: klt[p][:, 2 * l + h, b * S:b * S + S],
                                             lambda r: qpair[p][:, b, 2 * r + h, :])])
                    last.then_inc(q.a_s, 1)

            pe.wait_ge(q.bias_sb, 4)
            pe.wait_ge(q.bk_sb, 2)
            pe.wait_ge(q.split_lo, 1)
            for k in range(0, RUN.start):
                a_step(k, k % 2)
            with pe.Fori(RUN.start, RUN.stop - 1, 2) as k:
                for p in range(2):
                    a_step(k + p, p)
            for k in range(RUN.stop, LAST):
                a_step(k, k % 2)

            pe.wait_ge(q.pos_sb, 3)
            count = pe.value_load(wn[0:1, 0:1], min_val=1, max_val=NT)

            def b_transpose(w1, h):
                pe.wait_ge(q.b_lo, w1)
                pe.wait_ge(q.b_lo2, w1)
                for l, (part, done) in enumerate(((xch[h], q.b_t), (xcl[h], q.b_tl))):
                    for c in range(FC):
                        for i in range(G):
                            at = c * GT + i * P
                            last = pe.transpose(ps[l][:, :].bitcast(BF16)[:, at:at + P], part[:, i, c * P:(c + 1) * P],
                                                ident[:, :])
                    last.then_inc(done, G)

            def b_keys(w1):
                pe.wait_ge(q.b_eh, w1)
                for h in range(HP):
                    for k, (l, c) in enumerate(((0, 0), (0, 1), (1, 0), (1, 1))):
                        pe.matmul(ps[2 + h][:, :], wkx[:, l, c, h * P:(h + 1) * P], xct[:, 0, c, :],
                                  start=k == 0, stop=False)
                pe.wait_ge(q.b_el, w1)
                for h in range(HP):
                    for c in range(FC):
                        last = pe.matmul(ps[2 + h][:, :], wkx[:, 0, c, h * P:(h + 1) * P], xct[:, 1, c, :],
                                         start=False, stop=c == FC - 1)
                    last.then_inc(q.b_k, G // HP)

            def b_squares(w1):
                pe.wait_ge(q.b_ksq, w1)
                for i in range(G):
                    for h in range(HP):
                        last = pe.matmul(ps[6][:, XH * i:XH * i + XH], ksq[:, h, i * P:(i + 1) * P], headsum[:, h, :],
                                         start=h == 0, stop=h == HP - 1)
                last.then_inc(q.b_ss, G)

            def b_scores(w):
                pe.wait_ge(q.b_klo, w + G)
                pe.wait_ge(q.b_qld, 16 * w + 16 * G)
                for k in range(2):
                    if k == 1:
                        pe.wait_ge(q.b_ms, w + G)
                    for i in range(k * G // 2, (k + 1) * G // 2):
                        for h in range(HP):
                            at = (i % 2) * D + h * P
                            last = product(ps[5 + k][:, at:at + P],
                                           [(lambda l: kct[:, l, h, i * P:(i + 1) * P], lambda r: qc[:, i, 2 * r + h, :])])
                    last.then_inc(q.b_s, G // 2)

            def b_products(w, h):
                parts, probs = (xch[h], xcl[h]), (prh, prl)
                for i in range(G):
                    if i == G // 2:
                        b_squares(w + 2 * G)
                    if i % (G // 2) == 0:
                        pe.wait_ge(q.b_ph, w + (i + G // 2))
                        pe.wait_ge(q.b_pl, w + (i + G // 2))
                    if i >= 1:
                        pe.wait_ge(q.b_acc, w + (i - 1))
                    to, sums = (ps[0], ps[1]) if i % 2 == 0 else (ps[7], ps[4])
                    for h in range(HP):
                        for r in range(2):
                            pe.matmul(sums[:, h:h + 1], probs[r][:, i, h * P:(h + 1) * P], onesb[:, 0:1],
                                      start=r == 0, stop=r == 1)
                    for c in range(FC):
                        last = product(to[:, c * D:(c + 1) * D], [(lambda l: parts[l][:, i, c * P:(c + 1) * P],
                                                                   lambda r: probs[r][:, i])])
                    last.then_inc(q.b_pv, 1)

            pe.wait_ge(q.split_lo, len(splits))
            b_transpose(G, 0)
            b_keys(G)
            b_squares(G)
            with pe.Fori(0, count, 2 * G) as w:
                for h in range(2):
                    at = w + h * G
                    b_scores(at)
                    pe.wait_ge(q.b_acc, at - 1 if h == 1 else at)
                    b_transpose(at + 2 * G, 1 - h)
                    b_keys(at + 2 * G)
                    b_products(at, h)

            pe.wait_ge(q.c_sel, 16)
            pe.wait_ge(q.b_acc, count)
            for k in range(2):
                for b in range(2):
                    last = pe.matmul(ps[6][:, k * RT * HP:(k + 1) * RT * HP], sel[:, k, b, :],
                                     accs.rearrange("p (t b) k -> p b t k", b=2)[:, b], start=b == 0, stop=b == 1)
            last.then_inc(q.c_sums, 1)

            def c_heads(n, j, first=False):
                if not first:
                    pe.wait_ge(q.c_on, n - 1)
                pe.wait_ge(c_ld[j], 24 * n + (48 - 24 * j))
                pe.wait_ge(q.c_ul, 2 * n + 2)
                us = (c_uh[j], c_ul[j])
                for h in range(XH):
                    head = slice(h * DH, h * DH + DH)
                    latents = [c_pb[j][:, l, h].rearrange("p b n -> p (b n)") for l in range(2)]
                    product(ps[j][:, head],
                            [(lambda l, c=c: us[l][:, c, h].rearrange("p b n -> p (b n)"), lambda r, c=c: wvx[:, r, c, head])
                             for c in range(FC)] +
                            [(lambda l: latents[l], lambda r: c_vl[j][:, r, head])])
                    for l in range(2):
                        last = pe.matmul(ps[j][:, D + h:D + h + 1], latents[l], onesb[:, 0:1], start=l == 0, stop=l == 1)
                last.then_inc(q.c_ot, 1)

            def c_transpose(n, j):
                pe.wait_ge(q.c_ol, n + 1)
                for l, part in enumerate((c_oth[j], c_otl[j])):
                    for c in range(HP):
                        at = (l * HP + c) * P
                        last = pe.transpose(ps[2 + j][:, :].bitcast(BF16)[:, at:at + P], part[:, c * P:(c + 1) * P], ident[:, :])
                last.then_inc(q.c_t, 1)

            def c_out(n, j, first=False):
                pe.wait_ge(q.c_te, n + 1)
                if not first:
                    pe.wait_ge(q.c_x, n - 1)
                for r in range(2):
                    pe.matmul(ps[4 + j][:, 0:D], onesb[0:1, :], bo[0:1, r, :], start=r == 0, stop=False)
                product(ps[4 + j][:, 0:D], [(lambda l, c=c: c_otT[j][:, l, c, :], lambda r, c=c: wo[:, r, c, :])
                                            for c in range(HP)], start=False).then_inc(q.c_o, 1)

            pe.wait_ge(q.bo_lo, 1)
            c_heads(0, 0, first=True)
            c_heads(1, 1, first=True)
            c_transpose(0, 0)
            for j in range(2):
                c_heads(2 + j, j)
                c_transpose(1 + j, 1 - j)
                c_out(j, j, first=True)
            with pe.Fori(4, RT - 1, 2) as n:
                for j in range(2):
                    c_heads(n + j, j)
                    c_transpose(n + (j - 1), 1 - j)
                    c_out(n + (j - 2), j)
            c_transpose(RT - 1, 1)
            c_out(RT - 2, 0)
            c_out(RT - 1, 1)
            pe.wait_ge(q.c_x, RT)

            def rows_transpose(bank, parts):
                for l, part in enumerate(parts):
                    for c in range(FC):
                        at = (l * FC + c) * P
                        last = pe.transpose(ps[bank][:, :].bitcast(BF16)[:, at:at + P], part[:, c * P:(c + 1) * P],
                                            ident[:, :])
                last.then_inc(q.r_t, 1)

            def d_scores(n):
                parts = (qkh, qkl)
                for hp in range(AP_):
                    for b in range(2):
                        for l, r in PASSES:
                            for h2 in range(2):
                                c = (hp + 4 * h2) % AP_
                                rows_, cols = slice(h2 * DH, h2 * DH + DH), slice(b * S, b * S + S)
                                last = pe.matmul(ps[2 + c // 4][rows_, (c % 4) * P + b * S:(c % 4) * P + b * S + S],
                                                 parts[l][rows_, c, cols], parts[r][rows_, AP_ + c, cols],
                                                 start=(l, r) == PASSES[0], stop=(l, r) == PASSES[-1])
                last.then_inc(q.d_s, 1)

            def d_attend(j):
                values = (vh[j], vlo[j])
                for c in range(AP_):
                    for h2 in range(2):
                        head = (2 * c + h2) * DH
                        for l, r in PASSES:
                            for b in range(2):
                                rows_ = slice(b * S, b * S + S)
                                last = pe.matmul(ps[6 + b][h2 * DH:h2 * DH + DH, c * S:c * S + S],
                                                 values[l][rows_, head:head + DH], pT[rows_, r, c, h2 * S:h2 * S + S],
                                                 start=(l, r) == PASSES[0], stop=(l, r) == PASSES[-1])
                last.then_inc(q.d_pv, 1)

            def d_step(k, p):
                loop = not isinstance(k, int)
                if runs(k, 0):
                    pe.wait_ge(q.d_phi, k + 1)
                    pe.wait_ge(q.d_plo, k + 1)
                    for l, part in enumerate((sph, spl)):
                        if l == 1 and (loop or k > 0):
                            pe.wait_ge(q.d_x, k)
                        for c in range(AP_):
                            last = pe.transpose(ps[4 + l][:, :].bitcast(BF16)[:, c * P:(c + 1) * P], part[:, c, :],
                                                ident[:, :])
                        last.then_inc(q.d_pt, 1)
                if runs(k, -1):
                    pe.wait_ge(q.d_qlo, 4 * k + 8)
                    pe.sem_inc(q.gate, 1)
                    d_scores(k + 1)
                    pe.wait_ge(q.r_e, k + (RT + 3))
                    for c in range(2):
                        product(ps[c][:, :], [(lambda l, f=f: rowT[:, l, f, ds((k + 1) * P, P)],
                                               lambda r, f=f: wva[:, r, f, c * 512:c * 512 + 512])
                                              for f in range(FC)]).then_inc(q.d_v, 1)
                if runs(k, 0):
                    pe.wait_ge(q.d_peh, k + 1)
                    pe.wait_ge(q.d_pel, k + 1)
                    pe.wait_ge(q.d_vlo, 2 * k + 2)
                    pe.sem_inc(q.gate, 1)
                    d_attend(p)
                if runs(k, -2):
                    pe.wait_ge(q.r_e, k + (RT + 3))
                    if runs(k, -1):
                        pe.wait_ge(q.d_vlo, 2 * k + 4)
                    for b in range(4):
                        if b == 2 and runs(k, 0):
                            pe.wait_ge(q.d_alo, 2 * k + 2)
                        for c4 in range(4):
                            m = 4 * b + c4
                            last = product(ps[QK_BANKS[b]][:, c4 * P:(c4 + 1) * P],
                                           [(lambda l, c=c: wqk[:, l, c, m * P:(m + 1) * P],
                                             lambda r, c=c: rowT[:, r, c, ds((k + 2) * P, P)]) for c in range(FC)])
                        last.then_inc(q.d_qk, 1)
                if runs(k, 0):
                    pe.wait_ge(q.d_ahi, 2 * k + 2)
                    pe.wait_ge(q.d_alo, 2 * k + 2)
                    atts = (ath, atl)
                    product(ps[5][:, 0:D], [(lambda l, c=c: atts[l][:, c, :], lambda r, c=c: woa[:, r, c, :])
                                            for c in range(AP_)]).then_inc(q.d_o, 1)
                if norms(k):
                    pe.wait_ge(q.r_lo, k + (RT + 4))
                    if runs(k, -2):
                        pe.wait_ge(q.d_qlo, 4 * k + 9)
                    elif runs(k, -1):
                        pe.wait_ge(q.d_vlo, 2 * k + 4)
                    pe.wait_ge(q.r_e, k + (RT + 3))
                    rows_transpose(0, (d_rh, d_rl))

            for k in range(-3, D_RUN.start):
                d_step(k, k % 2)
            with pe.Fori(D_RUN.start, D_RUN.stop - 1, 2) as k:
                for i in range(2):
                    d_step(k + i, 1 - i)
            for k in range(D_RUN.stop, RT + 1):
                d_step(k, k % 2)
            pe.wait_ge(q.d_x, RT)

            pe.wait_ge(q.f_any, 1)
            pe.matmul(ps[4][0:1, 0:1], lowany[:, :], onesb[:, 0:1], start=True, stop=True).then_inc(q.f_count, 1)
            pe.wait_ge(q.f_known, 1)
            low_parts = pe.value_load(lown[0:1, 0:1], min_val=0, max_val=P)

            def feed_forward(passes):
                swapped = [(r, l) for l, r in passes]

                def e_block(n, ahead):
                    pe.wait_ge(q.r_e, n * BR + (2 * RT + BR))
                    for m in range(HC):
                        if m >= 2:
                            pe.wait_ge(q.e_hf, HC * n + (m - 1))
                        for k, w in enumerate((w1, w2)):
                            last = product(ps[2 * (m % 2) + k][:, :],
                                           [(lambda l, c=c: w[:, l, c, m * P:(m + 1) * P],
                                             lambda r, c=c: rowT[:, r, c, ds(n * BLK, BLK)]) for c in range(FC)],
                                           passes=passes)
                        last.then_inc(q.e_1, 1)
                    for layer, (w, ready, done) in enumerate(((h1, q.e_g1, q.e_h1), (h2, q.e_g2, q.e_h2))):
                        for m in range(HC):
                            if m < 2:
                                pe.wait_ge(q.e_g2 if layer == 0 else q.e_g1, HC * n + HC * layer)
                            else:
                                pe.wait_ge(ready, HC * n + (m - 1))
                            k = 0
                            for c in range(HC):
                                if m == 0:
                                    if layer == 0:
                                        pe.wait_ge(q.e_lo, HC * n + (c + 1))
                                    else:
                                        pe.wait_ge(q.e_glo, 2 * HC * n + (c + 1))
                                for l, r in passes:
                                    last = pe.matmul(ps[4 + m % 2][:, :], w[:, l, c, m * P:(m + 1) * P],
                                                     hb[layer][:, r, c], start=k == 0, stop=k == len(passes) * HC - 1)
                                    k += 1
                            last.then_inc(done, 1)
                            tile = layer * HC + m - 1
                            if ahead and 0 <= tile < BR:
                                pe.wait_ge(q.r_lo, n * BR + (2 * RT + BR + tile + 1))
                                rows_transpose(tile % 2, (d_rh, d_rl))
                    pe.wait_ge(q.e_glo, 2 * HC * n + 2 * HC)
                    for r_ in range(BR):
                        pe.wait_ge(q.e_os, BR * n + max(r_ - 1, 0))
                        product(ps[6 + r_ % 2][:, 0:D],
                                [(lambda l, c=c: hb[0][:, l, c, r_ * P:(r_ + 1) * P], lambda r, c=c: w3[:, r, c, :])
                                 for c in range(HC)], passes=swapped).then_inc(q.e_o, 1)

                with pe.Fori(0, NB - 1) as n:
                    e_block(n, True)
                e_block(NB - 1, False)

            with pe.If(low_parts < 1):
                feed_forward(PASSES[0:2])
            with pe.If(low_parts > 0):
                feed_forward(PASSES)


def rel_buckets():
    half, exact, far = NBUCK // 2, NBUCK // 4, 128
    table = np.zeros((NBUCK, P), np.float32)
    for m in range(2 * S - 1):
        rel = S - 1 - m
        dist = abs(rel)
        if dist >= exact:
            coeff = (half - exact) / np.log(far / exact)
            dist = min(half - 1, exact + int(np.log(np.float32(dist) / np.float32(exact)) * np.float32(coeff)))
        table[(half if rel > 0 else 0) + dist, m] = 1.0
    return table


def kernel(**inputs):
    import concourse.bacc as bacc
    from concourse.bass_utils import run_bass_kernel_spmd

    g = {k: np.asarray(v) for k, v in inputs.items()}
    x, mask = g["x"], g["mask_BxS2_bk0"]
    n = "L0_xattn_"
    f, a_ = "L0_ffn_", "L0_attn_"
    qkv = g[a_ + "qkv_w"]

    def chunks(w):
        return w.T.reshape(-1, P, w.shape[0]).transpose(1, 0, 2).reshape(P, -1)

    padded = np.zeros((B, KT * P), np.bool_)
    padded[:, FRONT:] = mask
    cols = padded.reshape(B * KT, P).T
    tiles = np.arange(NT).reshape(EC, ER).T
    arrays = {
        "x": x.reshape(ROWS, D),
        "ctx": np.concatenate([np.zeros((P + FRONT, D), np.float32), g["ctx_1024"].reshape(B * SC, D)]),
        "mask": np.concatenate([np.zeros((P, 1), np.bool_), cols], axis=1),
        "iota": np.broadcast_to(np.arange(NT, dtype=np.float32), (ER, NT)),
        "code": np.concatenate([tiles // KT, tiles % KT + 1], axis=1).astype(np.float32),
        "tri": np.triu(np.ones((ER, ER), np.float32), 1),
        "ident": np.eye(P, dtype=np.float32),
        "buck": rel_buckets(),
        "emb": g[a_ + "emb_weight"],
        "sel": (np.arange(P)[:, None, None, None] ==
                np.arange(2)[None, :, None, None] * S + np.arange(P) % S).astype(np.float32)
        * (np.arange(2)[:, None] == np.arange(P) // S),
        "headsum": (np.arange(HP * P).reshape(HP, P).T[:, :, None] // DH == np.arange(XH)).astype(np.float32),
        "ln_l_g": g[n + "ln_l_g"], "ln_l_b": g[n + "ln_l_b"],
        "q_gamma": g[n + "q_gamma"], "k_gamma": g[n + "k_gamma"],
        "lnx": np.stack([g[n + "ln_x_g"].reshape(FC, P).T, g[n + "ln_x_b"].reshape(FC, P).T], axis=1),
        "b_out": g[n + "b_out"].reshape(1, D),
        "w3_s": g[f + "w3_s"],
        "hs": np.stack([g[f + k].reshape(HC, P).T for k in ("w1_s", "w2_s", "h1_s", "h2_s")], axis=1),
        "wqkv": np.concatenate([g[n + "W_q"], g[n + "W_kv"]], axis=1),
        "wo": g[n + "W_out"],
        "wat": np.concatenate([chunks(qkv[0:2 * AH * DH]), chunks(qkv[2 * AH * DH:]), chunks(g[a_ + "o_w"])], axis=1)
        .reshape(P, RT, ATP).transpose(1, 0, 2),
        "wff": np.concatenate([chunks(g[f + k]) for k in ("w1_w", "w2_w", "h1_w", "h2_w", "w3_w")], axis=1)
        .reshape(P, RT, PIECE).transpose(1, 0, 2),
    }
    arrays = {k: np.ascontiguousarray(v) for k, v in arrays.items()}

    nc = bacc.Bacc("TRN2", target_bir_lowering=False, num_devices=1)
    t = {k: nc.dram_tensor("in_" + k, v.shape, mybir.dt.from_np(v.dtype), kind="ExternalInput").ap()
         for k, v in arrays.items()}
    out = nc.dram_tensor("out", [ROWS, D], F32, kind="ExternalOutput").ap()
    build(nc, t, out)
    result = run_bass_kernel_spmd(nc, [{"in_" + k: v for k, v in arrays.items()}], core_ids=[0])
    return result.results[0]["out"].reshape(B, S, D)
```
